# Optimizing a Trainium2 kernel written in Bass

```python
import numpy as np
import jax
import jax.numpy as jnp

def _softmax(x, axis=-1):
    return jax.nn.softmax(x, axis=axis)

def _gelu(x):
    return jax.nn.gelu(x, approximate=True)

def _silu(x):
    return jax.nn.silu(x)

def _sigmoid(x):
    return jax.nn.sigmoid(x)

def _layernorm(x, axis=-1, eps=1e-05):
    m = jnp.mean(x, axis=axis, keepdims=True)
    v = jnp.var(x, axis=axis, keepdims=True)
    return (x - m) / jnp.sqrt(v + eps)

def _scatter_add(tgt, idx, src, axis=0):
    return tgt.at[idx].add(src)

def _segment_sum(src, seg, n):
    return jax.ops.segment_sum(src, seg, n)
kernel_name = 'mk_adaln_ffn_d2_seqx_r8_1e5554'

def setup_inputs(seed: int=0):
    np.random.seed(seed)
    _w = jnp.asarray

    def _rec_inputs():
        import jax
        import jax.numpy as jnp
        _rk = jax.random.key(seed)
        x = -0.000125 + 0.9999 * jax.random.normal(jax.random.fold_in(_rk, 1), (32, 128, 128), jnp.float32)
        _lenS = 128 - jax.random.randint(jax.random.fold_in(_rk, 7), (32,), 0, max(1, 128 // 4) + 1, jnp.int32)
        _lenS2 = 128 - jax.random.randint(jax.random.fold_in(_rk, 8), (32,), 0, max(1, 128 // 4) + 1, jnp.int32)
        cond_1024 = 0.00782532 + 1.00527 * jax.random.normal(jax.random.fold_in(_rk, 11), (32, 128), jnp.float32)
        return (x, cond_1024)
    x, cond_1024 = _rec_inputs()

    def _L0_cond_setup():
        import jax, jax.numpy as jnp
        import numpy as np
        INV_SQRT2 = 0.7071067811865476
        key = jax.random.key(seed)
        k1, k2, k3, k4 = jax.random.split(key, 4)
        B, N, d = (8, 512, 128)
        scale = 1.0 / np.sqrt(d)
        return {'v': jax.random.normal(k1, (B, N, d), dtype=jnp.float32), 'q_pool': jax.random.normal(k2, (B, d), dtype=jnp.float32), 'W1': jax.random.normal(k3, (d, d), dtype=jnp.float32) * scale, 'b1': jnp.zeros((d,), dtype=jnp.float32), 'W2': jax.random.normal(k4, (d, d), dtype=jnp.float32) * scale, 'b2': jnp.zeros((d,), dtype=jnp.float32)}
    _L0_cond_all = _L0_cond_setup()
    _L0_cond_in = {k: v for k, v in _L0_cond_all.items() if k in ('W1', 'b1', 'W2', 'b2')}
    del _L0_cond_all

    def _L0_ffn_setup():
        import jax, jax.numpy as jnp
        import numpy as np
        DIM = 128
        INTER = 128
        E = 32
        K = 4
        G = 8
        LG = 4
        ROUTE_SCALE = 1.0
        CAP_FACTOR = 1.25
        B, S = (4, 256)

        def _gate(xf, wg):
            logits = xf @ wg.T
            scores = jax.nn.softmax(logits, axis=-1)
            sg = scores.reshape(-1, G, E // G)
            group_scores = sg.max(axis=-1)
            _, gtop = jax.lax.top_k(group_scores, LG)
            keep_g = jnp.sum(jax.nn.one_hot(gtop, G, dtype=jnp.float32), axis=1) > 0
            masked = jnp.where(keep_g[:, :, None], sg, -jnp.inf).reshape(-1, E)
            _, idx = jax.lax.top_k(masked, K)
            w = jnp.take_along_axis(scores, idx, axis=1)
            w = w / (w.sum(-1, keepdims=True) + 1e-09) * ROUTE_SCALE
            return (w.astype(xf.dtype), idx)

        def _forward(x, wg, w1, w2, w3, sw1, sw2, sw3):
            shape = x.shape
            xf = x.reshape(-1, DIM)
            N = xf.shape[0]
            cap = max(1, int(CAP_FACTOR * N * K / E))
            w, idx = _gate(xf, wg)
            fe = idx.reshape(-1)
            oh = jax.nn.one_hot(fe, E, dtype=jnp.int32)
            pos = (jnp.cumsum(oh, axis=0) * oh).sum(-1) - 1
            keep = pos < cap
            dest = jnp.where(keep, fe * cap + pos, E * cap)
            tok = jnp.arange(N * K, dtype=jnp.int32) // K
            buf_tok = jnp.full((E * cap + 1,), N, jnp.int32).at[dest].set(tok)[:-1]
            buf_w = jnp.zeros((E * cap + 1,), x.dtype).at[dest].set(w.reshape(-1))[:-1]
            xp = jnp.concatenate([xf, jnp.zeros((1, DIM), x.dtype)], axis=0)
            xe = xp[buf_tok].reshape(E, cap, DIM)
            h = jax.nn.silu(jnp.einsum('ecd,edh->ech', xe, w1)) * jnp.einsum('ecd,edh->ech', xe, w3)
            out = jnp.einsum('ech,ehd->ecd', h, w2) * buf_w.reshape(E, cap, 1)
            y = jnp.zeros((N + 1, DIM), x.dtype).at[buf_tok].add(out.reshape(E * cap, DIM))[:N]
            z = jax.nn.silu(xf @ sw1) * (xf @ sw3) @ sw2
            return (y + z).reshape(shape)
        key = jax.random.key(seed)
        ks = jax.random.split(key, 9)
        sd = DIM ** (-0.5)
        si = INTER ** (-0.5)
        x = jax.random.normal(ks[0], (B, S, DIM), jnp.float32)
        wg = jax.random.normal(ks[1], (E, DIM), jnp.float32) * sd
        w1 = jax.random.normal(ks[2], (E, DIM, INTER), jnp.float32) * sd
        w3 = jax.random.normal(ks[3], (E, DIM, INTER), jnp.float32) * sd
        w2 = jax.random.normal(ks[4], (E, INTER, DIM), jnp.float32) * si
        sw1 = jax.random.normal(ks[5], (DIM, INTER), jnp.float32) * sd
        sw3 = jax.random.normal(ks[6], (DIM, INTER), jnp.float32) * sd
        sw2 = jax.random.normal(ks[7], (INTER, DIM), jnp.float32) * si
        return dict(x=x, wg=wg, w1=w1, w2=w2, w3=w3, sw1=sw1, sw2=sw2, sw3=sw3)
    _L0_ffn_all = _L0_ffn_setup()
    _L0_ffn_in = {k: v for k, v in _L0_ffn_all.items() if k in ('wg', 'w1', 'w2', 'w3', 'sw1', 'sw2', 'sw3')}
    del _L0_ffn_all

    def _L1_cond_setup():
        import jax, jax.numpy as jnp
        import numpy as np
        N, T, D, H = (64, 64, 128, 128)
        key = jax.random.key(seed)
        k1, k2, k3, k4 = jax.random.split(key, 4)
        x = jax.random.normal(k1, (N, T, D), dtype=jnp.float32)
        h0 = jax.random.normal(k2, (N, H), dtype=jnp.float32)
        Wx = jax.random.normal(k3, (D, H), dtype=jnp.float32) / jnp.sqrt(jnp.float32(D))
        Wh = jax.random.normal(k4, (H, H), dtype=jnp.float32) / jnp.sqrt(jnp.float32(H))
        b = jnp.zeros((H,), dtype=jnp.float32)
        return {'x': x, 'h0': h0, 'Wx': Wx, 'Wh': Wh, 'b': b}
    _L1_cond_all = _L1_cond_setup()
    _L1_cond_in = {k: v for k, v in _L1_cond_all.items() if k in ('Wx', 'Wh', 'b')}
    del _L1_cond_all

    def _L1_ffn_setup():
        import jax, jax.numpy as jnp
        import numpy as np
        DIM = 128
        DEPTH = 2
        HEADS = 8
        DIM_HEAD = 64
        WINDOW = 64
        INNER = HEADS * DIM_HEAD
        HID = int(DIM * 4 * 2 / 3)
        B, N = (2, 1024)
        QK_SCALE = 8.0

        def shift_token(t):
            t1, t2 = jnp.split(t, 2, axis=-1)
            t2 = jnp.pad(t2, ((0, 0), (1, 0), (0, 0)))[:, :-1]
            return jnp.concatenate([t1, t2], axis=-1)

        def l2norm(t):
            return t / jnp.clip(jnp.linalg.norm(t, axis=-1, keepdims=True), 1e-12)

        def rotate_half(x):
            x1, x2 = jnp.split(x, 2, axis=-1)
            return jnp.concatenate([-x2, x1], axis=-1)

        def rotary_xpos(q, k):
            n = q.shape[-2]
            half_idx = jnp.arange(0, DIM_HEAD, 2, dtype=jnp.float32)
            inv_freq = 1.0 / 10000.0 ** (half_idx / DIM_HEAD)
            t = jnp.arange(n, dtype=jnp.float32)
            freqs = t[:, None] * inv_freq[None, :]
            freqs = jnp.concatenate([freqs, freqs], axis=-1)
            base = (half_idx + 0.4 * DIM_HEAD) / (1.4 * DIM_HEAD)
            power = (t - n // 2) / float(WINDOW // 2)
            scale = base[None, :] ** power[:, None]
            scale = jnp.concatenate([scale, scale], axis=-1)
            cos, sin = (jnp.cos(freqs), jnp.sin(freqs))
            q = q * cos * scale + rotate_half(q) * sin * scale
            k = k * cos / scale + rotate_half(k) * sin / scale
            return (q, k)

        def local_attention(q, k, v):
            b, h, n, d = q.shape
            w = n // WINDOW
            bq = q.reshape(b, h, w, WINDOW, d) * QK_SCALE
            bk = k.reshape(b, h, w, WINDOW, d)
            bv = v.reshape(b, h, w, WINDOW, d)

            def look_around(t):
                p = jnp.pad(t, ((0, 0), (0, 0), (1, 0), (0, 0), (0, 0)))
                return jnp.concatenate([p[:, :, :w], p[:, :, 1:]], axis=3)
            bk, bv = (look_around(bk), look_around(bv))
            bt = jnp.arange(n).reshape(w, WINDOW)
            btp = jnp.pad(bt, ((1, 0), (0, 0)), constant_values=-1)
            btk = jnp.concatenate([btp[:w], btp[1:]], axis=1)
            sim = jnp.einsum('bhwid,bhwjd->bhwij', bq, bk)
            i = bt[:, :, None]
            j = btk[:, None, :]
            mask = (i < j) | (i > j + WINDOW) | (j == -1)
            sim = jnp.where(mask, -jnp.finfo(sim.dtype).max, sim)
            attn = jax.nn.softmax(sim, axis=-1)
            out = jnp.einsum('bhwij,bhwjd->bhwid', attn, bv)
            return out.reshape(b, h, n, d)

        def _layer(x, wqkv, qs, ksc, wo, lg, lb, w1, b1, w2, b2):
            b, n, _ = x.shape
            h = shift_token(x)
            qkv = h @ wqkv
            q, k, v = jnp.split(qkv, 3, axis=-1)
            to_heads = lambda t: t.reshape(b, n, HEADS, DIM_HEAD).transpose(0, 2, 1, 3)
            q, k, v = (to_heads(q), to_heads(k), to_heads(v))
            q = l2norm(q) * qs
            k = l2norm(k) * ksc
            q, k = rotary_xpos(q, k)
            o = local_attention(q, k, v)
            o = o.transpose(0, 2, 1, 3).reshape(b, n, INNER)
            x = x + o @ wo
            h = shift_token(x)
            mu = h.mean(-1, keepdims=True)
            var = h.var(-1, keepdims=True)
            h = (h - mu) / jnp.sqrt(var + 1e-05) * lg + lb
            h = h @ w1 + b1
            a, g = jnp.split(h, 2, axis=-1)
            h = a * jax.nn.gelu(g, approximate=False)
            x = x + h @ w2 + b2
            return x
        key = jax.random.key(seed)
        ks = jax.random.split(key, 6)
        return {'x': jax.random.normal(ks[0], (B, N, DIM), jnp.float32), 'wqkv': jax.random.normal(ks[1], (DEPTH, DIM, 3 * INNER), jnp.float32) * 0.02, 'q_scale': jnp.ones((DEPTH, DIM_HEAD), jnp.float32), 'k_scale': jnp.ones((DEPTH, DIM_HEAD), jnp.float32), 'wo': jax.random.normal(ks[2], (DEPTH, INNER, DIM), jnp.float32) * 0.02, 'ln_g': jnp.ones((DEPTH, DIM), jnp.float32), 'ln_b': jnp.zeros((DEPTH, DIM), jnp.float32), 'w1': jax.random.normal(ks[3], (DEPTH, DIM, 2 * HID), jnp.float32) * 0.02, 'b1': jnp.zeros((DEPTH, 2 * HID), jnp.float32), 'w2': jax.random.normal(ks[4], (DEPTH, HID, DIM), jnp.float32) * 0.02, 'b2': jnp.zeros((DEPTH, DIM), jnp.float32)}
    _L1_ffn_all = _L1_ffn_setup()
    _L1_ffn_in = {k: v for k, v in _L1_ffn_all.items() if k in ('wqkv', 'q_scale', 'k_scale', 'wo', 'ln_g', 'ln_b', 'w1', 'b1', 'w2', 'b2')}
    del _L1_ffn_all
    return {'x': x, 'cond_1024': cond_1024, 'L0_cond_W1': _L0_cond_in['W1'], 'L0_cond_b1': _L0_cond_in['b1'], 'L0_cond_W2': _L0_cond_in['W2'], 'L0_cond_b2': _L0_cond_in['b2'], 'L0_ffn_wg': _L0_ffn_in['wg'], 'L0_ffn_w1': _L0_ffn_in['w1'], 'L0_ffn_w2': _L0_ffn_in['w2'], 'L0_ffn_w3': _L0_ffn_in['w3'], 'L0_ffn_sw1': _L0_ffn_in['sw1'], 'L0_ffn_sw2': _L0_ffn_in['sw2'], 'L0_ffn_sw3': _L0_ffn_in['sw3'], 'L1_cond_Wx': _L1_cond_in['Wx'], 'L1_cond_Wh': _L1_cond_in['Wh'], 'L1_cond_b': _L1_cond_in['b'], 'L1_ffn_wqkv': _L1_ffn_in['wqkv'], 'L1_ffn_q_scale': _L1_ffn_in['q_scale'], 'L1_ffn_k_scale': _L1_ffn_in['k_scale'], 'L1_ffn_wo': _L1_ffn_in['wo'], 'L1_ffn_ln_g': _L1_ffn_in['ln_g'], 'L1_ffn_ln_b': _L1_ffn_in['ln_b'], 'L1_ffn_w1': _L1_ffn_in['w1'], 'L1_ffn_b1': _L1_ffn_in['b1'], 'L1_ffn_w2': _L1_ffn_in['w2'], 'L1_ffn_b2': _L1_ffn_in['b2']}

def reference(x, cond_1024, L0_cond_W1, L0_cond_b1, L0_cond_W2, L0_cond_b2, L0_ffn_wg, L0_ffn_w1, L0_ffn_w2, L0_ffn_w3, L0_ffn_sw1, L0_ffn_sw2, L0_ffn_sw3, L1_cond_Wx, L1_cond_Wh, L1_cond_b, L1_ffn_wqkv, L1_ffn_q_scale, L1_ffn_k_scale, L1_ffn_wo, L1_ffn_ln_g, L1_ffn_ln_b, L1_ffn_w1, L1_ffn_b1, L1_ffn_w2, L1_ffn_b2):
    import jax
    import jax.numpy as jnp

    def _L0_cond_ref(v, q_pool, W1, b1, W2, b2):
        import jax, jax.numpy as jnp
        import numpy as np
        INV_SQRT2 = 0.7071067811865476
        B, N, d = v.shape
        h = jax.nn.silu(q_pool @ W1.T + b1)
        gate = jax.nn.sigmoid(h @ W2.T + b2)[:, None, :]
        levels = int(np.log2(N))
        a = v
        details = []
        for _ in range(levels):
            e, o = (a[:, 0::2], a[:, 1::2])
            details.append((e - o) * INV_SQRT2)
            a = (e + o) * INV_SQRT2
        a = a * gate
        for dc in reversed(details):
            dc = dc * gate
            e = (a + dc) * INV_SQRT2
            o = (a - dc) * INV_SQRT2
            n = e.shape[1]
            a = jnp.stack([e, o], axis=2).reshape(B, 2 * n, d)
        return v + a

    def _L0_ffn_ref(x, wg, w1, w2, w3, sw1, sw2, sw3):
        import jax, jax.numpy as jnp
        import numpy as np
        DIM = 128
        INTER = 128
        E = 32
        K = 4
        G = 8
        LG = 4
        ROUTE_SCALE = 1.0
        CAP_FACTOR = 1.25
        B, S = (4, 256)

        def _gate(xf, wg):
            logits = xf @ wg.T
            scores = jax.nn.softmax(logits, axis=-1)
            sg = scores.reshape(-1, G, E // G)
            group_scores = sg.max(axis=-1)
            _, gtop = jax.lax.top_k(group_scores, LG)
            keep_g = jnp.sum(jax.nn.one_hot(gtop, G, dtype=jnp.float32), axis=1) > 0
            masked = jnp.where(keep_g[:, :, None], sg, -jnp.inf).reshape(-1, E)
            _, idx = jax.lax.top_k(masked, K)
            w = jnp.take_along_axis(scores, idx, axis=1)
            w = w / (w.sum(-1, keepdims=True) + 1e-09) * ROUTE_SCALE
            return (w.astype(xf.dtype), idx)

        def _forward(x, wg, w1, w2, w3, sw1, sw2, sw3):
            shape = x.shape
            xf = x.reshape(-1, DIM)
            N = xf.shape[0]
            cap = max(1, int(CAP_FACTOR * N * K / E))
            w, idx = _gate(xf, wg)
            fe = idx.reshape(-1)
            oh = jax.nn.one_hot(fe, E, dtype=jnp.int32)
            pos = (jnp.cumsum(oh, axis=0) * oh).sum(-1) - 1
            keep = pos < cap
            dest = jnp.where(keep, fe * cap + pos, E * cap)
            tok = jnp.arange(N * K, dtype=jnp.int32) // K
            buf_tok = jnp.full((E * cap + 1,), N, jnp.int32).at[dest].set(tok)[:-1]
            buf_w = jnp.zeros((E * cap + 1,), x.dtype).at[dest].set(w.reshape(-1))[:-1]
            xp = jnp.concatenate([xf, jnp.zeros((1, DIM), x.dtype)], axis=0)
            xe = xp[buf_tok].reshape(E, cap, DIM)
            h = jax.nn.silu(jnp.einsum('ecd,edh->ech', xe, w1)) * jnp.einsum('ecd,edh->ech', xe, w3)
            out = jnp.einsum('ech,ehd->ecd', h, w2) * buf_w.reshape(E, cap, 1)
            y = jnp.zeros((N + 1, DIM), x.dtype).at[buf_tok].add(out.reshape(E * cap, DIM))[:N]
            z = jax.nn.silu(xf @ sw1) * (xf @ sw3) @ sw2
            return (y + z).reshape(shape)
        return _forward(x, wg, w1, w2, w3, sw1, sw2, sw3)

    def _L1_cond_ref(x, h0, Wx, Wh, b):
        import jax, jax.numpy as jnp
        import numpy as np
        N, T, D, H = (64, 64, 128, 128)
        xw = jnp.einsum('ntd,dh->nth', x, Wx) + b

        def step(prev_h, xw_t):
            next_h = jnp.tanh(xw_t + prev_h @ Wh)
            return (next_h, next_h)
        _, hs = jax.lax.scan(step, h0, jnp.swapaxes(xw, 0, 1))
        return jnp.swapaxes(hs, 0, 1)

    def _L1_ffn_ref(x, wqkv, q_scale, k_scale, wo, ln_g, ln_b, w1, b1, w2, b2):
        import jax, jax.numpy as jnp
        import numpy as np
        DIM = 128
        DEPTH = 2
        HEADS = 8
        DIM_HEAD = 64
        WINDOW = 64
        INNER = HEADS * DIM_HEAD
        HID = int(DIM * 4 * 2 / 3)
        B, N = (2, 1024)
        QK_SCALE = 8.0

        def shift_token(t):
            t1, t2 = jnp.split(t, 2, axis=-1)
            t2 = jnp.pad(t2, ((0, 0), (1, 0), (0, 0)))[:, :-1]
            return jnp.concatenate([t1, t2], axis=-1)

        def l2norm(t):
            return t / jnp.clip(jnp.linalg.norm(t, axis=-1, keepdims=True), 1e-12)

        def rotate_half(x):
            x1, x2 = jnp.split(x, 2, axis=-1)
            return jnp.concatenate([-x2, x1], axis=-1)

        def rotary_xpos(q, k):
            n = q.shape[-2]
            half_idx = jnp.arange(0, DIM_HEAD, 2, dtype=jnp.float32)
            inv_freq = 1.0 / 10000.0 ** (half_idx / DIM_HEAD)
            t = jnp.arange(n, dtype=jnp.float32)
            freqs = t[:, None] * inv_freq[None, :]
            freqs = jnp.concatenate([freqs, freqs], axis=-1)
            base = (half_idx + 0.4 * DIM_HEAD) / (1.4 * DIM_HEAD)
            power = (t - n // 2) / float(WINDOW // 2)
            scale = base[None, :] ** power[:, None]
            scale = jnp.concatenate([scale, scale], axis=-1)
            cos, sin = (jnp.cos(freqs), jnp.sin(freqs))
            q = q * cos * scale + rotate_half(q) * sin * scale
            k = k * cos / scale + rotate_half(k) * sin / scale
            return (q, k)

        def local_attention(q, k, v):
            b, h, n, d = q.shape
            w = n // WINDOW
            bq = q.reshape(b, h, w, WINDOW, d) * QK_SCALE
            bk = k.reshape(b, h, w, WINDOW, d)
            bv = v.reshape(b, h, w, WINDOW, d)

            def look_around(t):
                p = jnp.pad(t, ((0, 0), (0, 0), (1, 0), (0, 0), (0, 0)))
                return jnp.concatenate([p[:, :, :w], p[:, :, 1:]], axis=3)
            bk, bv = (look_around(bk), look_around(bv))
            bt = jnp.arange(n).reshape(w, WINDOW)
            btp = jnp.pad(bt, ((1, 0), (0, 0)), constant_values=-1)
            btk = jnp.concatenate([btp[:w], btp[1:]], axis=1)
            sim = jnp.einsum('bhwid,bhwjd->bhwij', bq, bk)
            i = bt[:, :, None]
            j = btk[:, None, :]
            mask = (i < j) | (i > j + WINDOW) | (j == -1)
            sim = jnp.where(mask, -jnp.finfo(sim.dtype).max, sim)
            attn = jax.nn.softmax(sim, axis=-1)
            out = jnp.einsum('bhwij,bhwjd->bhwid', attn, bv)
            return out.reshape(b, h, n, d)

        def _layer(x, wqkv, qs, ksc, wo, lg, lb, w1, b1, w2, b2):
            b, n, _ = x.shape
            h = shift_token(x)
            qkv = h @ wqkv
            q, k, v = jnp.split(qkv, 3, axis=-1)
            to_heads = lambda t: t.reshape(b, n, HEADS, DIM_HEAD).transpose(0, 2, 1, 3)
            q, k, v = (to_heads(q), to_heads(k), to_heads(v))
            q = l2norm(q) * qs
            k = l2norm(k) * ksc
            q, k = rotary_xpos(q, k)
            o = local_attention(q, k, v)
            o = o.transpose(0, 2, 1, 3).reshape(b, n, INNER)
            x = x + o @ wo
            h = shift_token(x)
            mu = h.mean(-1, keepdims=True)
            var = h.var(-1, keepdims=True)
            h = (h - mu) / jnp.sqrt(var + 1e-05) * lg + lb
            h = h @ w1 + b1
            a, g = jnp.split(h, 2, axis=-1)
            h = a * jax.nn.gelu(g, approximate=False)
            x = x + h @ w2 + b2
            return x
        for l in range(DEPTH):
            x = _layer(x, wqkv[l], q_scale[l], k_scale[l], wo[l], ln_g[l], ln_b[l], w1[l], b1[l], w2[l], b2[l])
        return x
    x = x + _L0_ffn_ref(_L0_cond_ref(x, cond_1024, L0_cond_W1, L0_cond_b1, L0_cond_W2, L0_cond_b2), L0_ffn_wg, L0_ffn_w1, L0_ffn_w2, L0_ffn_w3, L0_ffn_sw1, L0_ffn_sw2, L0_ffn_sw3)
    x = x + _L1_ffn_ref(_L1_cond_ref(x, cond_1024, L1_cond_Wx, L1_cond_Wh, L1_cond_b), L1_ffn_wqkv, L1_ffn_q_scale, L1_ffn_k_scale, L1_ffn_wo, L1_ffn_ln_g, L1_ffn_ln_b, L1_ffn_w1, L1_ffn_b1, L1_ffn_w2, L1_ffn_b2)
    return x

_drawn_inputs = setup_inputs


def setup_inputs(seed=0):
    import zlib

    import numpy as np

    out = dict(_drawn_inputs(seed))
    spreads = {'L0_cond_b1': (0.0, 0.1),
     'L0_cond_b2': (0.0, 0.1),
     'L1_cond_b': (0.0, 0.308),
     'L1_ffn_q_scale': (1.0, 0.6),
     'L1_ffn_k_scale': (1.0, 0.6),
     'L1_ffn_ln_g': (1.0, 0.6),
     'L1_ffn_ln_b': (0.0, 0.8),
     'L1_ffn_b1': (0.0, 0.8),
     'L1_ffn_b2': (0.0, 0.656)}
    factors = {'L1_ffn_wqkv': 3.55, 'L1_ffn_wo': 3.553, 'L1_ffn_w1': 6.887, 'L1_ffn_w2': 6.764}
    for name, (base, spread) in spreads.items():
        noise = np.random.default_rng([zlib.crc32(name.encode()), seed]).standard_normal(out[name].shape)
        drawn = base * np.exp(spread * noise) if base else spread * noise
        out[name] = jnp.asarray(drawn.astype(out[name].dtype))
    for name, factor in factors.items():
        out[name] = (out[name] * factor).astype(out[name].dtype)
    return out
```

```python
from contextlib import ExitStack

import numpy as np

import concourse.bass as bass
from concourse import mybir

F32, BF16, I32, U32 = mybir.dt.float32, mybir.dt.bfloat16, mybir.dt.int32, mybir.dt.uint32
ALU, ACT = mybir.AluOpType, mybir.ActivationFunctionType
X = mybir.AxisListType.X

B, N, D = 32, 128, 128
TOKENS = B * N
E, K, GROUPS = 32, 4, 8
PER_GROUP = E // GROUPS
KEPT_GROUPS = 4
CAP = int(1.25 * TOKENS * K / E)
SLOTS = E * CAP
HEADS, DH, WINDOW = 8, 64, 64
INNER = HEADS * DH
HID = int(D * 4 * 2 / 3)
DEPTH = 2
MASKED = -1e30
HALVES = ((slice(0, D // 2), 0), (slice(D // 2, D), 1))


def constants():
    f = np.float32
    p = np.arange(N)
    route = np.zeros((N, 3 * 128 + E + GROUPS * GROUPS + 1), f)
    route[:, 0:128] = np.eye(128)
    route[:, 128:256] = 1.0
    route[:, 256:384] = -(p[:, None] >= p[None, :]).astype(f)
    route[:, 384:384 + E] = np.arange(E)
    g = np.arange(GROUPS)
    route[:, 384 + E:384 + E + GROUPS * GROUPS] = (g[None, :] < g[:, None]).astype(f).reshape(-1)
    route[:, -1] = SLOTS + p
    half = np.arange(0, DH, 2, dtype=f)
    inv_freq = (1.0 / f(10000.0) ** (half / f(DH))).astype(f)
    t = np.arange(N, dtype=f)
    freqs = (t[:, None] * inv_freq[None, :]).astype(f).astype(np.float64)
    base = (half + 0.4 * DH) / (1.4 * DH)
    power = (t - N // 2) / float(WINDOW // 2)
    scale = base[None, :].astype(np.float64) ** power[:, None].astype(np.float64)
    cos, sin = np.cos(freqs), np.sin(freqs)
    rot = np.zeros((N, 2, 2, DH), f)
    for i, s in enumerate((scale, 1 / scale)):
        rot[:, 0, i] = np.concatenate([cos * s, cos * s], 1)
        rot[:, 1, i] = np.concatenate([-sin * s, sin * s], 1)
    mask = np.zeros((N, N), f)
    i, j = p[:, None], p[None, :]
    mask[(i < j) | (i > j + WINDOW)] = MASKED
    mean = np.full((D, D), 1.0 / D, f)
    center = np.eye(D, dtype=f) - mean
    return {"c_route": route, "c_rot": rot, "c_mask": np.tile(mask, (1, 4)),
            "c_mean": np.concatenate([center, mean], 1)}


class Chain:

    def __init__(self, eng, sem, before=0):
        self.eng, self.sem, self.before, self.n = eng, sem, before, 0

    def add(self, ins):
        ins.then_inc(self.sem, 1)
        self.n += 1
        return self.n

    def wait(self, n):
        self.eng.wait_ge(self.sem, self.before + n)

    def link(self, ins):
        self.wait(self.add(ins))


class Kit:

    def __init__(self, nc, ctx, tag):
        self.nc, self.ctx, self.tag, self.sems = nc, ctx, tag, []
        ctx.callback(self.close)

    def close(self):
        self.nc.clear_and_free_semaphores(self.sems)
        self.nc.all_engine_barrier()

    def sb(self, name, shape, dt=F32):
        return self.ctx.enter_context(self.nc.sbuf_tensor(f"{self.tag}_{name}", shape, dt))

    def ps(self, name, shape, dt=F32):
        return self.ctx.enter_context(self.nc.psum_tensor(f"{self.tag}_{name}", shape, dt))

    def sem(self, name):
        self.sems.append(self.nc.alloc_semaphore(name=f"{self.tag}_{name}"))
        return self.sems[-1]


NG = 4
GB = B // NG
J = 8


def dispatch_phase(nc, a, xbuf, idx_tm, w_tm, zT):
    with ExitStack() as ctx:
        kit = Kit(nc, ctx, "ds")
        xtok = kit.sb("xtok", [N, B, D])
        x1tok = kit.sb("x1tok", [N, B, D])
        x1T = kit.sb("x1T", [D, B, N])
        diag = kit.sb("diag", [D, B, D])
        zero = kit.sb("zero", [128, 4096])
        cst = kit.sb("cst", [128, 3 * 128 + E + GROUPS * GROUPS + 1])
        ident, ones = cst[:, 0:128], cst[:, 128:256]
        iota = cst[:, 384:384 + E]
        before_g = cst[:, 384 + E:384 + E + 64].rearrange("p (g h) -> p g h", g=GROUPS)
        dump = cst[:, 384 + E + 64:384 + E + 65]
        ones_h = kit.sb("ones_h", [128, 128], BF16)
        negtri_h = kit.sb("negtri_h", [128, 128], BF16)
        keep_run = kit.sb("keep_run", [128, E, GB])
        W1, W2 = kit.sb("W1", [D, D]), kit.sb("W2", [D, D])
        W1T, W2T = kit.sb("W1T", [D, D]), kit.sb("W2T", [D, D])
        cond, wg = kit.sb("cond", [B, D]), kit.sb("wg", [E, D])
        condT, wgT = kit.sb("condT", [D, B]), kit.sb("wgT", [D, E])
        b1, b2 = kit.sb("b1", [D, 1]), kit.sb("b2", [D, 1])
        hT, gateT, g1T = kit.sb("hT", [D, B]), kit.sb("gateT", [D, B]), kit.sb("g1T", [D, B])
        sw = kit.sb("sw", [D, 3, 128])
        zs, zh = kit.sb("zs", [128, 512]), kit.sb("zh", [128, 512])
        sc = kit.sb("sc", [N, GB, E])
        ms = kit.sb("ms", [N, GB, E])
        r1 = kit.sb("r1", [N, GB, 4])
        gmax, keepg, keepm = (kit.sb(n, [N, GB, GROUPS]) for n in ("gmax", "keepg", "keepm"))
        cmp1, cmp2 = (kit.sb(n, [N, GB, GROUPS, GROUPS]) for n in ("cmp1", "cmp2"))
        v8 = kit.sb("v8", [N, GB, 8])
        i8 = kit.sb("i8", [N, GB, 8], U32)
        idxf, posk, keepk, destf = (kit.sb(n, [N, GB, K]) for n in ("idxf", "posk", "keepk", "destf"))
        onehot, ohpos = kit.sb("onehot", [N, GB, K, E]), kit.sb("ohpos", [N, GB, K, E])
        maskM = kit.sb("maskM", [N, E, GB], BF16)
        tot, run, pos = (kit.sb(n, [N, E, GB]) for n in ("tot", "run", "pos"))
        carry = kit.sb("carry", [N, E])
        dest = kit.sb("dest", [N, B, K], I32)
        wk = kit.sb("wk", [N, B, K])

        p_b = kit.ps("p_b", [128, 2, 512])
        p_t = kit.ps("p_t", [128, 2, 512])
        p_l = kit.ps("p_l", [N, B, E])
        p_c = kit.ps("p_c", [128, 2, E, GB])
        p_s = kit.ps("p_s", [128, 512])

        s_x = [kit.sem(f"xload{q}") for q in range(4)]
        s_small, s_cst, s_sw = kit.sem("small"), kit.sem("cst"), kit.sem("sw")
        s_zero, s_fill = kit.sem("zero"), kit.sem("fill")
        s_smallT, s_smallc = kit.sem("smallT"), kit.sem("smallc")
        s_h, s_hs, s_g, s_gs = kit.sem("h"), kit.sem("hs"), kit.sem("g"), kit.sem("gs")
        s_diag, s_b, s_x1 = kit.sem("diag"), kit.sem("b"), kit.sem("x1")
        s_t, s_x1T, s_l = kit.sem("t"), kit.sem("x1T"), kit.sem("l")
        s_sub, s_exp = kit.sem("sub"), kit.sem("exp")
        s_M, s_c, s_cr = kit.sem("M"), kit.sem("c"), kit.sem("cr")
        s_zh, s_zs, s_zm, s_zo, s_zc = (kit.sem(n) for n in ("zh", "zs", "zm", "zo", "zc"))
        s_dest, s_sc, s_st = kit.sem("dest"), kit.sem("sc"), kit.sem("st")
        s_v = kit.sem("v")
        block = ctx.enter_context(nc.Block())

        @block.sync
        def _(sp):
            xv = a["x"].rearrange("b n d -> n b d")
            sp.dma_start(cond[:, :], a["cond_1024"]).then_inc(s_small, 16)
            sp.dma_start(W1[:, :], a["L0_cond_W1"]).then_inc(s_small, 16)
            sp.dma_start(W2[:, :], a["L0_cond_W2"]).then_inc(s_small, 16)
            sp.dma_start(wg[:, :], a["L0_ffn_wg"]).then_inc(s_small, 16)
            sp.dma_start(b1[:, :], a["L0_cond_b1"].rearrange("(d o) -> d o", o=1)).then_inc(s_small, 16)
            sp.dma_start(b2[:, :], a["L0_cond_b2"].rearrange("(d o) -> d o", o=1)).then_inc(s_small, 16)
            for q in range(4):
                sp.dma_start(xtok[:, 8 * q:8 * q + 8, :], xv[:, 8 * q:8 * q + 8, :]).then_inc(s_x[q], 16)
            for i, name in enumerate(("L0_ffn_sw1", "L0_ffn_sw3", "L0_ffn_sw2")):
                sp.dma_start(sw[:, i, :], a[name]).then_inc(s_sw, 16)
            for g in range(NG):
                bs = slice(g * GB, (g + 1) * GB)
                sp.wait_ge(s_dest, g + 1)
                sp.dma_start(idx_tm[:, bs, :], dest[:, bs, :]).then_inc(s_st, 16)
                sp.dma_start(w_tm[:, bs, :], wk[:, bs, :]).then_inc(s_st, 16)
            sp.wait_ge(s_st, 32 * NG)

        @block.gpsimd
        def _(pool):
            pool.memset(zero[:, :], 0.0).then_inc(s_zero, 1)
            pool.wait_ge(s_fill, 16 * 5)
            for g in range(NG):
                pool.wait_ge(s_dest, g + 1)
                for b in range(g * GB, (g + 1) * GB):
                    for k in range(K):
                        pool.indirect_dma_start(
                            xbuf, bass.IndirectOffsetOnAxis(ap=dest[:, b, k:k + 1], axis=0),
                            x1tok[:, b, :], None, bounds_check=SLOTS - 1, oob_is_err=False).then_inc(s_sc, 16)
            pool.wait_ge(s_sc, 16 * B * K)

        @block.scalar
        def _(act):
            act.dma_start(cst[:, :], a["c_route"]).then_inc(s_cst, 16)
            act.wait_ge(s_zero, 1)
            rows = SLOTS // 5
            for i in range(5):
                act.dma_start(xbuf[i * rows:(i + 1) * rows, :].rearrange("(p r) d -> p (r d)", p=128),
                              zero[:, :]).then_inc(s_fill, 16)
            act.wait_ge(s_small, 96)
            act.wait_ge(s_h, 1)
            act.activation(hT[:, :], p_s[:, 0:32], ACT.Silu, bias=b1[:, 0:1]).then_inc(s_hs, 1)
            act.wait_ge(s_g, 1)
            act.activation(gateT[:, :], p_s[:, 32:64], ACT.Sigmoid, bias=b2[:, 0:1]).then_inc(s_gs, 1)
            for j in range(J):
                act.wait_ge(s_t, j + 1)
                act.activation(x1T[:, 4 * j:4 * j + 4, :], p_t[:, j % 2, :].rearrange("p (b n) -> p b n", b=4),
                               ACT.Copy).then_inc(s_x1T, 1)
            for g in range(NG):
                act.wait_ge(s_sub, g + 1)
                act.activation(sc[:, :, :], sc[:, :, :], ACT.Exp).then_inc(s_exp, 1)
                for j in (2 * g, 2 * g + 1):
                    act.wait_ge(s_zh, j + 1)
                    if j >= 1:
                        act.wait_ge(s_zm, j)
                    act.activation(zs[:, :], p_b[:, 0, :], ACT.Silu).then_inc(s_zs, 1)
                    act.wait_ge(s_zo, j + 1)
                    act.activation(zT[:, :, 4 * j:4 * j + 4].rearrange("p n b -> p b n"),
                                   p_t[:, 0, :].rearrange("p (b n) -> p b n", b=4), ACT.Copy).then_inc(s_zc, 1)
            act.wait_ge(s_zc, J)

        @block.tensor
        def _(pe):
            pe.wait_ge(s_small, 96)
            pe.wait_ge(s_cst, 16)
            pe.transpose(p_s[:, 128:160], cond[:, :], ident[0:B, 0:B])
            pe.transpose(p_s[:, 160:192], wg[:, :], ident[0:E, 0:E])
            pe.transpose(p_s[:, 192:320], W1[:, :], ident)
            pe.transpose(p_s[:, 320:448], W2[:, :], ident).then_inc(s_smallT, 1)
            pe.wait_ge(s_smallc, 4)
            pe.matmul(p_s[:, 0:32], W1T[:, :], condT[:, :], start=True, stop=True).then_inc(s_h, 1)
            pe.wait_ge(s_hs, 1)
            pe.matmul(p_s[:, 32:64], W2T[:, :], hT[:, :], start=True, stop=True).then_inc(s_g, 1)
            for j in range(J):
                pe.wait_ge(s_diag, j // 2 + 1)
                if j >= 2:
                    pe.wait_ge(s_x1, j - 1)
                pe.matmul(p_b[:, j % 2, :], ones, diag[:, 4 * j:4 * j + 4, :].rearrange("p b d -> p (b d)"),
                          start=True, stop=True).then_inc(s_b, 1)
            for j in range(J):
                pe.wait_ge(s_x1, j + 1)
                if j >= 2:
                    pe.wait_ge(s_x1T, j - 1)
                for i in range(4):
                    t = pe.transpose(p_t[:, j % 2, 128 * i:128 * i + 128], x1tok[:, 4 * j + i, :], ident)
                t.then_inc(s_t, 1)
                pe.wait_ge(s_x1T, j + 1)
                for b in range(4 * j, 4 * j + 4):
                    m = pe.matmul(p_l[:, b, :], x1T[:, b, :], wgT[:, :], start=True, stop=True)
                m.then_inc(s_l, 1)
            pe.wait_ge(s_sw, 48)
            for g in range(NG):
                pe.wait_ge(s_M, g + 1)
                if g >= 1:
                    pe.wait_ge(s_cr, g)
                m = maskM[:, :, :].rearrange("p e b -> p (e b)")
                pe.matmul(p_c[:, 0, :, :].rearrange("p e b -> p (e b)"), ones_h[:, :], m, start=True, stop=True)
                pe.matmul(p_c[:, 1, :, :].rearrange("p e b -> p (e b)"), negtri_h[:, :], m,
                          start=True, stop=True).then_inc(s_c, 1)
                for j in (2 * g, 2 * g + 1):
                    tokens = x1T[:, 4 * j:4 * j + 4, :].rearrange("p b n -> p (b n)")
                    if j >= 1:
                        pe.wait_ge(s_zm, j)
                    pe.matmul(p_b[:, 0, :], sw[:, 0, :], tokens, start=True, stop=True)
                    pe.matmul(p_b[:, 1, :], sw[:, 1, :], tokens, start=True, stop=True).then_inc(s_zh, 1)
                    pe.wait_ge(s_zm, j + 1)
                    if j >= 1:
                        pe.wait_ge(s_zc, j)
                    pe.matmul(p_t[:, 0, :], sw[:, 2, :], zh[:, :], start=True, stop=True).then_inc(s_zo, 1)

        @block.vector
        def _(dve):
            v = Chain(dve, s_v)
            dve.wait_ge(s_cst, 16)
            dve.tensor_copy(ones_h[:, :], ones)
            dve.tensor_copy(negtri_h[:, :], cst[:, 256:384])
            dve.memset(carry[:, :], 0.0)
            v.link(dve.memset(keep_run[:, :, :], 1.0))
            dve.memset(keep_run[:, :, 0:1], 0.0)
            dve.wait_ge(s_smallT, 1)
            dve.tensor_copy(condT[:, :], p_s[:, 128:160]).then_inc(s_smallc, 1)
            dve.tensor_copy(wgT[:, :], p_s[:, 160:192]).then_inc(s_smallc, 1)
            dve.tensor_copy(W1T[:, :], p_s[:, 192:320]).then_inc(s_smallc, 1)
            dve.tensor_copy(W2T[:, :], p_s[:, 320:448]).then_inc(s_smallc, 1)
            dve.wait_ge(s_gs, 1)
            v.link(dve.tensor_scalar(g1T[:, :], gateT[:, :], 1.0, None, ALU.add))
            for q in range(4):
                bs = slice(8 * q, 8 * q + 8)
                dve.tensor_tensor(diag[:, bs, :], ident[:, None, :].to_broadcast([128, 8, 128]),
                                  g1T[:, bs][:, :, None].to_broadcast([128, 8, 128]), ALU.mult).then_inc(s_diag, 1)
            for j in range(J):
                bs = slice(4 * j, 4 * j + 4)
                dve.wait_ge(s_b, j + 1)
                dve.wait_ge(s_x[j // 2], 16)
                dve.tensor_tensor(x1tok[:, bs, :], xtok[:, bs, :],
                                  p_b[:, j % 2, :].rearrange("p (b d) -> p b d", b=4), ALU.mult).then_inc(s_x1, 1)

            def wide(col, n):
                return col[:, :, None].to_broadcast([N, GB, n])

            def shared_expert(j):
                dve.wait_ge(s_zs, j + 1)
                if j >= 1:
                    dve.wait_ge(s_zo, j)
                dve.tensor_tensor(zh[:, :], zs[:, :], p_b[:, 1, :], ALU.mult).then_inc(s_zm, 1)

            for g in range(NG):
                bs = slice(g * GB, (g + 1) * GB)
                dve.wait_ge(s_l, 4 * (g // 2 + 1))
                logits = p_l[:, bs, :]
                v.link(dve.tensor_reduce(r1[:, :, 0], logits, X, ALU.max))
                dve.tensor_tensor(sc[:, :, :], logits, wide(r1[:, :, 0], E), ALU.subtract).then_inc(s_sub, 1)
                dve.wait_ge(s_exp, g + 1)
                v.link(dve.tensor_reduce(r1[:, :, 1], sc[:, :, :], X, ALU.add))
                v.link(dve.reciprocal(r1[:, :, 2], r1[:, :, 1]))
                v.link(dve.tensor_tensor(sc[:, :, :], sc[:, :, :], wide(r1[:, :, 2], E), ALU.mult))
                v.link(dve.tensor_reduce(gmax[:, :, :], sc[:, :, :].rearrange("p b (g i) -> p b g i", g=GROUPS),
                                         X, ALU.max))
                other = gmax[:, :, None, :].to_broadcast([N, GB, GROUPS, GROUPS])
                own = gmax[:, :, :, None].to_broadcast([N, GB, GROUPS, GROUPS])
                dve.tensor_tensor(cmp2[:, :, :, :], other, own, ALU.is_gt)
                v.link(dve.tensor_tensor(cmp1[:, :, :, :], other, own, ALU.is_equal))
                v.link(dve.tensor_tensor(cmp1[:, :, :, :], cmp1[:, :, :, :],
                                         before_g[:, None, :, :].to_broadcast([N, GB, GROUPS, GROUPS]), ALU.mult))
                v.link(dve.tensor_tensor(cmp1[:, :, :, :], cmp1[:, :, :, :], cmp2[:, :, :, :], ALU.add))
                v.link(dve.tensor_reduce(keepm[:, :, :], cmp1[:, :, :, :], X, ALU.add))
                v.link(dve.tensor_scalar(keepg[:, :, :], keepm[:, :, :], float(KEPT_GROUPS), None, ALU.is_lt))
                v.link(dve.tensor_scalar(keepm[:, :, :], keepg[:, :, :], -1.0, None, ALU.add))
                msv = ms[:, :, :].rearrange("p b (g i) -> p b g i", g=GROUPS)
                v.link(dve.tensor_tensor(msv, sc[:, :, :].rearrange("p b (g i) -> p b g i", g=GROUPS),
                                         keepg[:, :, :, None].to_broadcast([N, GB, GROUPS, PER_GROUP]), ALU.mult))
                v.link(dve.tensor_tensor(msv, msv,
                                         keepm[:, :, :, None].to_broadcast([N, GB, GROUPS, PER_GROUP]), ALU.add))
                for b in range(GB):
                    n = v.add(dve.max(v8[:, b, :], ms[:, b, :]))
                v.wait(n)
                for b in range(GB):
                    n = v.add(dve.max_index(i8[:, b, :], v8[:, b, :], ms[:, b, :]))
                v.wait(n)
                v.link(dve.tensor_copy(idxf[:, :, :], i8[:, :, 0:K]))
                if g >= 1:
                    dve.wait_ge(s_c, g)
                v.link(dve.tensor_tensor(onehot[:, :, :, :], idxf[:, :, :, None].to_broadcast([N, GB, K, E]),
                                         iota[:, None, None, :].to_broadcast([N, GB, K, E]), ALU.is_equal))
                with nc.allow_low_precision(reason="zeros and ones"):
                    dve.tensor_reduce(maskM[:, :, :].rearrange("p e b -> p b e"),
                                      onehot[:, :, :, :].rearrange("p b k e -> p b e k"), X, ALU.add).then_inc(s_M, 1)
                v.link(dve.tensor_reduce(r1[:, :, 0], v8[:, :, 0:K], X, ALU.add))
                v.link(dve.tensor_scalar(r1[:, :, 1], r1[:, :, 0], 1e-9, None, ALU.add))
                v.link(dve.reciprocal(r1[:, :, 2], r1[:, :, 1]))
                v.link(dve.tensor_tensor(wk[:, bs, :], v8[:, :, 0:K], wide(r1[:, :, 2], K), ALU.mult))
                dve.wait_ge(s_c, g + 1)
                v.link(dve.tensor_copy(tot[:, :, :], p_c[:, 0, :, :]))
                v.link(dve.tensor_tensor(tot[:, :, 0], tot[:, :, 0], carry[:, :], ALU.add))
                flat = "p e b -> p (e b)"
                v.link(dve.tensor_tensor_scan(run[:, :, :].rearrange(flat), keep_run[:, :, :].rearrange(flat),
                                              tot[:, :, :].rearrange(flat), 0.0, ALU.mult, ALU.add))
                dve.tensor_copy(carry[:, :], run[:, :, GB - 1])
                v.link(dve.tensor_tensor(pos[:, :, :], p_c[:, 1, :, :], run[:, :, :], ALU.add))
                dve.engine_nop().then_inc(s_cr, 1)
                v.link(dve.tensor_tensor(ohpos[:, :, :, :], onehot[:, :, :, :],
                                         pos[:, :, :].rearrange("p e b -> p b e")[:, :, None, :]
                                         .to_broadcast([N, GB, K, E]), ALU.mult))
                v.link(dve.tensor_reduce(posk[:, :, :], ohpos[:, :, :, :], X, ALU.add))
                v.link(dve.tensor_scalar(keepk[:, :, :], posk[:, :, :], float(CAP), None, ALU.is_lt))
                v.link(dve.scalar_tensor_tensor(destf[:, :, :], idxf[:, :, :], float(CAP), posk[:, :, :],
                                                ALU.mult, ALU.add))
                v.link(dve.tensor_tensor(wk[:, bs, :], wk[:, bs, :], keepk[:, :, :], ALU.mult))
                v.link(dve.scalar_tensor_tensor(destf[:, :, :], destf[:, :, :], dump, keepk[:, :, :],
                                                ALU.subtract, ALU.mult))
                dve.tensor_scalar(dest[:, bs, :], destf[:, :, :], dump, None, ALU.add).then_inc(s_dest, 1)
                shared_expert(2 * g)
                shared_expert(2 * g + 1)


def turns(eng, count, body, last=1):
    body(0)
    with eng.Fori(1, count - last, 1) as i:
        body(i)
    for i in range(count - last, count):
        body(i)


def is_last(i, count):
    return isinstance(i, int) and i == count - 1


def wait(eng, sem, value):
    if not isinstance(value, int) or value > 0:
        eng.wait_ge(sem, value)


PARTS = CAP // 128
PA = 3
EU = 4


def expert_phase(nc, a, xbuf, obuf):
    with ExitStack() as ctx:
        kit = Kit(nc, ctx, "ex")
        ident = kit.sb("ident", [128, 128])
        zero = kit.sb("zero", [128, 128])
        xe = kit.sb("xe", [128, EU, PARTS, D])
        we = kit.sb("we", [128, EU, 3, 128])
        xeT = kit.sb("xeT", [D, 2, CAP])
        sa, hh = kit.sb("sa", [128, CAP]), kit.sb("hh", [128, CAP])
        oe = kit.sb("oe", [128, EU, PARTS, D])
        na = PA * 128
        shares = [(0, slice(0, na), range(0, PA)), (1, slice(na, CAP), range(PA, PARTS))]
        p_t = [kit.ps(f"p_t{h}", [128, 512]) for h in range(2)]
        p_1 = [kit.ps(f"p_1{h}", [128, 512]) for h in range(2)]
        p_3 = [kit.ps(f"p_3{h}", [128, 512]) for h in range(2)]
        p_o = [kit.ps(f"p_o{h}", [128, 512]) for h in range(2)]

        s_id, s_zero, s_zst = kit.sem("id"), kit.sem("zero"), kit.sem("zst")
        s_x = [kit.sem(f"x{u}") for u in range(EU)]
        s_w = [kit.sem(f"w{u}") for u in range(EU)]
        s_st = [kit.sem(f"st{u}") for u in range(EU)]
        s_t, s_xT, s_1, s_3, s_silu, s_hh, s_o, s_oe = (
            kit.sem(n) for n in ("t", "xT", "h1", "h3", "silu", "hh", "o", "oe"))
        T = E // EU
        xv = xbuf.rearrange("(e p j) d -> e p j d", p=128, j=PARTS)
        ov = obuf[0:SLOTS, :].rearrange("(e p j) d -> e p j d", p=128, j=PARTS)
        block = ctx.enter_context(nc.Block())

        @block.sync
        def _(sp):
            def load(e, u):
                sp.dma_start(xe[:, u, :, :], xv[bass.ds(e, 1)].rearrange("o p j d -> p (o j) d")).then_inc(s_x[u], 16)
                for i, name in enumerate(("L0_ffn_w1", "L0_ffn_w3", "L0_ffn_w2")):
                    sp.dma_start(we[:, u, i, :], a[name][bass.ds(e, 1)].rearrange("o p n -> p (o n)")).then_inc(s_w[u], 16)

            sp.dma_start(ident[:, :], a["c_route"][:, 0:128]).then_inc(s_id, 16)
            for u in range(EU):
                load(u, u)
            sp.wait_ge(s_zero, 1)
            sp.dma_start(obuf[SLOTS:SLOTS + 128, :], zero[:, :]).then_inc(s_zst, 16)

            def turn(i):
                for u in range(EU):
                    e = i * EU + u
                    wait(sp, s_oe, (e + 1) * 2)
                    sp.dma_start(ov[bass.ds(e, 1)].rearrange("o p j d -> p (o j) d"), oe[:, u, :, :]).then_inc(s_st[u], 16)
                    if not is_last(i, T):
                        load(e + EU, u)

            turns(sp, T, turn)
            for u in range(EU):
                sp.wait_ge(s_st[u], 16 * T)
            sp.wait_ge(s_zst, 16)

        @block.gpsimd
        def _(pool):
            pool.memset(zero[:, :], 0.0).then_inc(s_zero, 1)

        @block.tensor
        def _(pe):
            def transposes(e, u, i):
                wait(pe, s_x[u], 16 * (i + 1))
                for h, _, tiles in shares:
                    wait(pe, s_xT, 2 * e - 1 + h)
                    for j in tiles:
                        t = pe.transpose(p_t[h][:, 128 * (j - tiles[0]):128 * (j - tiles[0]) + 128],
                                         xe[:, u, j, :], ident[:, :])
                    t.then_inc(s_t, 1)

            def turn(i):
                for u in range(EU):
                    e = i * EU + u
                    wait(pe, s_w[u], 48 * (i + 1))
                    for h, cols, tiles in shares:
                        n = len(tiles) * 128
                        wait(pe, s_xT, 2 * e + 1 + h)
                        wait(pe, s_silu, 2 * e - 1 + h)
                        pe.matmul(p_1[h][:, 0:n], we[:, u, 0, :], xeT[:, u % 2, cols], start=True, stop=True).then_inc(s_1, 1)
                        wait(pe, s_hh, 2 * e - 1 + h)
                        pe.matmul(p_3[h][:, 0:n], we[:, u, 1, :], xeT[:, u % 2, cols], start=True, stop=True).then_inc(s_3, 1)
                    if not (is_last(i, T) and u == EU - 1):
                        transposes(e + 1, (u + 1) % EU, i + (u + 1) // EU)
                    for h, cols, tiles in shares:
                        wait(pe, s_hh, 2 * e + 1 + h)
                        wait(pe, s_oe, 2 * e - 1 + h)
                        for j in tiles:
                            q = 128 * (j - tiles[0])
                            m = pe.matmul(p_o[h][:, q:q + 128], hh[:, 128 * j:128 * j + 128], we[:, u, 2, :],
                                          start=True, stop=True)
                        m.then_inc(s_o, 1)

            pe.wait_ge(s_id, 16)
            transposes(0, 0, 0)
            turns(pe, T, turn)

        @block.scalar
        def _(act):
            def copy_xT(e, u):
                for h, cols, tiles in shares:
                    wait(act, s_t, 2 * e + 1 + h)
                    wait(act, s_3, 2 * e - 3 + h)
                    act.activation(xeT[:, u % 2, cols], p_t[h][:, 0:len(tiles) * 128], ACT.Copy).then_inc(s_xT, 1)

            def turn(i):
                for u in range(EU):
                    e = i * EU + u
                    for h, cols, tiles in shares:
                        wait(act, s_1, 2 * e + 1 + h)
                        wait(act, s_hh, 2 * e - 1 + h)
                        act.activation(sa[:, cols], p_1[h][:, 0:len(tiles) * 128], ACT.Silu).then_inc(s_silu, 1)
                    if not (is_last(i, T) and u == EU - 1):
                        copy_xT(e + 1, u + 1)

            copy_xT(0, 0)
            turns(act, T, turn)

        @block.vector
        def _(dve):
            def turn(i):
                for u in range(EU):
                    e = i * EU + u
                    for h, cols, tiles in shares:
                        wait(dve, s_silu, 2 * e + 1 + h)
                        wait(dve, s_3, 2 * e + 1 + h)
                        wait(dve, s_o, 2 * e - 1 + h)
                        dve.tensor_tensor(hh[:, cols], sa[:, cols], p_3[h][:, 0:len(tiles) * 128],
                                          ALU.mult).then_inc(s_hh, 1)
                    for h, cols, tiles in shares:
                        wait(dve, s_o, 2 * e + 1 + h)
                        if h == 0:
                            wait(dve, s_st[u], 16 * i)
                        dve.tensor_copy(oe[:, u, tiles[0]:tiles[-1] + 1, :],
                                        p_o[h][:, 0:len(tiles) * 128].rearrange("p (j d) -> p j d", d=D)
                                        ).then_inc(s_oe, 1)

            turns(dve, T, turn)


CT = 4
CHUNKS = N // CT
CU = 4


def recurrence_phase(nc, a, obuf, idx_tm, w_tm, zT, xl):
    with ExitStack() as ctx:
        kit = Kit(nc, ctx, "rc")
        ident, cond = kit.sb("ident", [128, 128]), kit.sb("cond", [B, D])
        Wx, Wh, bias = kit.sb("Wx", [D, D]), kit.sb("Wh", [D, D]), kit.sb("bias", [D, 1])
        h0T = kit.sb("h0T", [D, B])
        ix, wc = kit.sb("ix", [128, CU, K], I32), kit.sb("wc", [128, CU, K])
        xc = kit.sb("xc", [128, CU, D])
        rows = kit.sb("rows", [128, CU, K, D])
        acc = kit.sb("acc", [128, 2, D])
        hr = kit.sb("hr", [D, CU, CT, B])
        p_0 = kit.ps("p_0", [128, 512])
        p_t = [kit.ps(f"p_t{i}", [128, 512]) for i in range(2)]
        p_w = [kit.ps(f"p_w{i}", [128, 512]) for i in range(2)]
        s_k, s_h0, s_h0c = kit.sem("k"), kit.sem("h0"), kit.sem("h0c")
        s_in = [kit.sem(f"in{u}") for u in range(CU)]
        s_g = [kit.sem(f"g{u}") for u in range(CU)]
        s_acc, s_t, s_x2, s_mm, s_h, s_hc, s_v = (kit.sem(n) for n in ("acc", "t", "x2", "mm", "h", "hc", "v"))
        T = CHUNKS // CU
        ixv = idx_tm.rearrange("(c t) b k -> c (t b) k", t=CT)
        wv = w_tm.rearrange("(c t) b k -> c (t b) k", t=CT)
        xv = a["x"].rearrange("b (c t) d -> c t b d", t=CT)
        block = ctx.enter_context(nc.Block())

        @block.sync
        def _(sp):
            def load(c, u):
                sp.dma_start(ix[:, u, :], ixv[bass.ds(c, 1)].rearrange("o p k -> p (o k)")).then_inc(s_in[u], 16)
                sp.dma_start(wc[:, u, :], wv[bass.ds(c, 1)].rearrange("o p k -> p (o k)")).then_inc(s_in[u], 16)
                for t in range(CT):
                    sp.dma_start(xc[B * t:B * t + B, u, :],
                                 xv[bass.ds(c, 1), t].rearrange("o b d -> b (o d)")).then_inc(s_in[u], 16)

            load(0, 0)
            sp.dma_start(ident[:, :], a["c_route"][:, 0:128]).then_inc(s_k, 16)
            sp.dma_start(cond[:, :], a["cond_1024"]).then_inc(s_k, 16)
            sp.dma_start(Wx[:, :], a["L1_cond_Wx"]).then_inc(s_k, 16)
            sp.dma_start(Wh[:, :], a["L1_cond_Wh"]).then_inc(s_k, 16)
            sp.dma_start(bias[:, :], a["L1_cond_b"].rearrange("(d o) -> d o", o=1)).then_inc(s_k, 16)
            for u in range(1, CU):
                load(u, u)

            def turn(i):
                for u in range(CU):
                    if not is_last(i, T):
                        sp.wait_ge(s_acc, i * CU + u + 1)
                        load(i * CU + u + CU, u)

            turns(sp, T, turn)

        @block.gpsimd
        def _(pool):
            for c in range(CHUNKS):
                i, u = divmod(c, CU)
                pool.wait_ge(s_in[u], (i + 1) * 16 * (2 + CT))
                wait(pool, s_acc, c - CU + 1)
                for k in range(K):
                    pool.indirect_dma_start(
                        rows[:, u, k, :], None, obuf,
                        bass.IndirectOffsetOnAxis(ap=ix[:, u, k:k + 1], axis=0)).then_inc(s_g[u], 16)

        @block.vector
        def _(dve):
            dve.memset(xl[D // 2:D, :, 0:1], 0.0)
            dve.wait_ge(s_h0, 1)
            dve.tensor_copy(h0T[:, :], p_0[:, 0:B]).then_inc(s_h0c, 1)

            def keep_h(c, u):
                dve.wait_ge(s_h, (c + 1) * CT)
                for half, o in HALVES:
                    ins = dve.tensor_copy(xl[half, :, bass.ds(c * CT + o, CT)], hr[half, u, :, :].rearrange("p t b -> p b t"))
                ins.then_inc(s_hc, 1)

            def turn(i):
                v = Chain(dve, s_v, i * CU * (K - 1))
                for u in range(CU):
                    c = i * CU + u
                    dve.wait_ge(s_g[u], (i + 1) * 16 * K)
                    wait(dve, s_t, c - 1)
                    dve.wait_ge(s_in[u], (i + 1) * 16 * (2 + CT))
                    for k in range(K):
                        add_to = xc[:, u, :] if k == 0 else acc[:, u % 2, :]
                        ins = dve.scalar_tensor_tensor(out=acc[:, u % 2, :], in0=rows[:, u, k, :],
                                                       scalar=wc[:, u, k:k + 1], in1=add_to,
                                                       op0=ALU.mult, op1=ALU.add)
                        if k < K - 1:
                            v.link(ins)
                    ins.then_inc(s_acc, 1)
                    dve.wait_ge(s_t, c + 1)
                    zc = zT[:, bass.ds(c * CT, CT), :]
                    dve.tensor_tensor(zc, p_t[u % 2][:, 0:128].rearrange("p (t b) -> p t b", t=CT), zc,
                                      ALU.add).then_inc(s_x2, 1)
                    if u > 0:
                        keep_h(c - 1, u - 1)
                    elif not (isinstance(i, int) and i == 0):
                        keep_h(c - 1, CU - 1)

            turns(dve, T, turn)
            keep_h(CHUNKS - 1, CU - 1)

        @block.tensor
        def _(pe):
            pe.wait_ge(s_k, 80)
            pe.transpose(p_0[:, 0:B], cond[:, :], ident[0:B, 0:B]).then_inc(s_h0, 1)
            pe.wait_ge(s_h0c, 1)

            def turn(i):
                for u in range(CU):
                    c = i * CU + u
                    pe.wait_ge(s_acc, c + 1)
                    wait(pe, s_x2, c - 1)
                    pe.transpose(p_t[u % 2][:, 0:128], acc[:, u % 2, :], ident[:, :]).then_inc(s_t, 1)
                    pe.wait_ge(s_x2, c + 1)
                    pe.matmul(p_w[u % 2][:, 0:128], Wx[:, :], zT[:, bass.ds(c * CT, CT), :].rearrange("p t b -> p (t b)"),
                              start=True, stop=True, skip_group_check=True)
                    for t in range(CT):
                        if t > 0:
                            prev = hr[:, u, t - 1, :]
                        elif u > 0 or not (isinstance(i, int) and i == 0):
                            prev = hr[:, (u - 1) % CU, CT - 1, :]
                        else:
                            prev = h0T[:, :]
                        wait(pe, s_h, c * CT + t)
                        pe.matmul(p_w[u % 2][:, B * t:B * t + B], Wh[:, :], prev, start=False, stop=True,
                                  skip_group_check=True).then_inc(s_mm, 1)

            turns(pe, T, turn)

        @block.scalar
        def _(act):
            act.wait_ge(s_k, 80)

            def turn(i):
                for u in range(CU):
                    c = i * CU + u
                    wait(act, s_hc, c - CU + 1)
                    for t in range(CT):
                        act.wait_ge(s_mm, c * CT + t + 1)
                        act.activation(hr[:, u, t, :], p_w[u % 2][:, B * t:B * t + B], ACT.Tanh,
                                       bias=bias[:, 0:1]).then_inc(s_h, 1)

            turns(act, T, turn)


AU = 2
AHEAD = 2


def exists(b):
    return not isinstance(b, int) or b < B


def attention_phase(nc, a, layer, xl):
    with ExitStack() as ctx:
        kit = Kit(nc, ctx, f"at{layer}")
        ident, identh = kit.sb("ident", [128, 128]), kit.sb("identh", [128, 128], BF16)
        maskf, maskh = kit.sb("maskf", [128, 512]), kit.sb("maskh", [128, 512], BF16)
        wqkv, wo = kit.sb("wqkv", [D, 3 * INNER]), kit.sb("wo", [128, 4, D])
        rot, scales = kit.sb("rot", [N, 2, 2, DH]), kit.sb("scales", [N, 2, DH])
        tcos, tsin = kit.sb("tcos", [N, 2, DH]), kit.sb("tsin", [N, 2, DH])
        minus_half = kit.sb("minus_half", [N, 16])
        h = kit.sb("h", [D, 2, N])
        raw = kit.sb("raw", [N, 2, 2 * INNER])
        sq = kit.sb("sq", [N, 2 * INNER])
        ss, rn = kit.sb("ss", [N, 2, 16]), kit.sb("rn", [N, 2, 16])
        t1, t2 = kit.sb("t1", [N, 2, 2 * INNER]), kit.sb("t2", [N, 2, 2 * INNER])
        qn = kit.sb("qn", [N, 2, 2 * INNER])
        vaug = kit.sb("vaug", [N, 2, HEADS, DH + 1])
        qT, kT = kit.sb("qT", [128, 4, N]), kit.sb("kT", [128, 4, N])
        mx = kit.sb("mx", [N, 2, 4])
        sm = [kit.sb(f"sm{r}", [N, 4, N]) for r in range(2)]
        pr = [kit.sb(f"pr{r}", [N, 4, N]) for r in range(2)]
        prT = [kit.sb(f"prT{r}", [N, 4, N]) for r in range(2)]
        rinv = kit.sb("rinv", [N, 2, 4])
        on = kit.sb("on", [N, 4, 2, DH])
        oT = kit.sb("oT", [128, 4, N])
        p_qk = kit.ps("p_qk", [N, 2 * INNER])
        p_v = kit.ps("p_v", [N, INNER])
        p_t = [kit.ps(f"p_t{r}", [128, 512]) for r in range(2)]
        p_s = [kit.ps(f"p_s{r}", [128, 512]) for r in range(2)]
        p_o = kit.ps("p_o", [128, 512])
        p_d = p_t[0][:, 0:N]

        s_c, s_cc, s_tab, s_cv = kit.sem("c"), kit.sem("cc"), kit.sem("tab"), kit.sem("cv")
        (s_h, s_qk, s_vm, s_raw, s_sum, s_sq, s_ss, s_t12, s_qn, s_T, s_Tc, s_S, s_sub, s_P, s_PT, s_PTc, s_vc, s_O,
         s_on, s_oT, s_oTc, s_dl, s_xl, s_v, s_p) = (kit.sem(n) for n in (
             "h", "qk", "vm", "raw", "sum", "sq", "ss", "t12", "qn", "T", "Tc", "S", "sub", "P", "PT", "PTc", "vc", "O",
             "on", "oT", "oTc", "dl", "xl", "v", "pc"))
        TURNS = B // AU
        block = ctx.enter_context(nc.Block())

        @block.sync
        def _(sp):
            sp.dma_start(ident[:, :], a["c_route"][:, 0:128]).then_inc(s_c, 16)
            sp.dma_start(wqkv[:, :], a["L1_ffn_wqkv"][layer]).then_inc(s_c, 16)
            sp.dma_start(maskf[:, :], a["c_mask"]).then_inc(s_c, 16)
            sp.dma_start(rot[:, :, :, :], a["c_rot"]).then_inc(s_c, 16)
            for i, name in enumerate(("L1_ffn_q_scale", "L1_ffn_k_scale")):
                sp.dma_start(scales[:, i, :], a[name][layer:layer + 1, :].to_broadcast([N, DH])).then_inc(s_c, 16)
            sp.dma_start(wo[:, :, :], a["L1_ffn_wo"][layer].rearrange("(c p) d -> p c d", p=128)).then_inc(s_c, 16)

        @block.gpsimd
        def _(pool):
            def shifted(b, u):
                wait(pool, s_vm, b - 1)
                pool.tensor_copy(h[:, u, :].rearrange("p (o n) -> p o n", o=1), xl[:, bass.ds(b, 1), 0:N]).then_inc(s_h, 1)

            def normal(b, u, before):
                p = Chain(pool, s_p, before)
                pool.wait_ge(s_ss, b + 1)
                p.add(pool.tensor_tensor(rn[:, u, :], ss[:, u, :], minus_half[:, :], ALU.pow))
                pool.wait_ge(s_t12, b + 1)
                wait(pool, s_T, 2 * (b - 1))
                p.link(pool.tensor_tensor(qn[:, u, :], t1[:, u, :], t2[:, u, :], ALU.add))
                qv = qn[:, u, :].rearrange("p (g d) -> p g d", g=16)
                pool.tensor_tensor(qv, qv, rn[:, u, :, None].to_broadcast([N, 16, DH]), ALU.mult).then_inc(s_qn, 1)

            pool.memset(minus_half[:, :], -0.5).then_inc(s_p, 1)
            pool.memset(vaug[:, :, :, DH:DH + 1], 1.0).then_inc(s_cv, 1)
            pool.wait_ge(s_p, 1)
            shifted(0, 0)
            shifted(1, 1)
            normal(0, 0, 1)
            shifted(2, 0)
            normal(1, 1, 3)

            def turn(i):
                for u in range(AU):
                    b = i * AU + u
                    if exists(b + AHEAD + 1):
                        shifted(b + AHEAD + 1, (u + 1) % 2)
                    if exists(b + AHEAD):
                        normal(b + AHEAD, u, 1 + 2 * (b + AHEAD))

            turns(pool, TURNS, turn, 2)

        @block.tensor
        def _(pe):
            def project(b, u):
                wait(pe, s_h, b + 1)
                wait(pe, s_raw, b)
                pe.matmul(p_qk[:, 0:INNER], h[:, u, :], wqkv[:, 0:INNER], start=True, stop=True)
                pe.matmul(p_qk[:, INNER:2 * INNER], h[:, u, :], wqkv[:, INNER:2 * INNER], start=True, stop=True).then_inc(s_qk, 1)
                wait(pe, s_vc, b)
                pe.matmul(p_v[:, :], h[:, u, :], wqkv[:, 2 * INNER:], start=True, stop=True).then_inc(s_vm, 1)

            def attend(b, u):
                pe.wait_ge(s_qn, b + 1)
                wait(pe, s_xl, b)
                wait(pe, s_PTc, 2 * b)
                for r in range(2):
                    for c in range(4):
                        q = r * INNER + 128 * c
                        t = pe.transpose(p_t[r][:, 128 * c:128 * c + 128], qn[:, u, q:q + 128], ident[:, :])
                    t.then_inc(s_T, 1)
                wait(pe, s_Tc, 2 * b + 2)
                for r in range(2):
                    half = slice(64 * r, 64 * r + 64)
                    wait(pe, s_on, 2 * b - 1 + r)
                    pe.matmul(p_s[r][:, :], identh[:, :], maskh[:, :], start=True, stop=False, skip_group_check=True)
                    for c in range(4):
                        m = pe.matmul(p_s[r][:, 128 * c:128 * c + 128], qT[half, c, :], kT[half, c, :],
                                      start=False, stop=True, skip_group_check=True)
                    m.then_inc(s_S, 1)
                if exists(b + AHEAD):
                    project(b + AHEAD, u)
                for r in range(2):
                    wait(pe, s_P, 2 * b + 1 + r)
                    for c in range(4):
                        t = pe.transpose(p_t[r][:, 128 * c:128 * c + 128], pr[r][:, c, :], ident[:, :])
                    t.then_inc(s_PT, 1)
                wait(pe, s_vc, b + 1)
                for r in range(2):
                    wait(pe, s_PTc, 2 * b + 1 + r)
                    for c in range(4):
                        m = pe.matmul(p_s[r][:, (DH + 1) * c:(DH + 1) * (c + 1)], prT[r][:, c, :],
                                      vaug[:, u, 2 * c + r, :], start=True, stop=True)
                    m.then_inc(s_O, 1)
                wait(pe, s_on, 2 * b + 2)
                wait(pe, s_oTc, b)
                for c in range(4):
                    t = pe.transpose(p_o[:, 128 * c:128 * c + 128], on[:, c, :, :].rearrange("p r d -> p (r d)"), ident[:, :])
                t.then_inc(s_oT, 1)
                wait(pe, s_oTc, b + 1)
                for c in range(4):
                    m = pe.matmul(p_d, wo[:, c, :], oT[:, c, :], start=(c == 0), stop=(c == 3))
                m.then_inc(s_dl, 1)

            pe.wait_ge(s_c, 16 * 7)
            pe.wait_ge(s_cc, 2)
            project(0, 0)
            project(1, 1)

            def turn(i):
                for u in range(AU):
                    attend(i * AU + u, u)

            turns(pe, TURNS, turn, 2)

        @block.scalar
        def _(act):
            def squares(b, u):
                act.wait_ge(s_qk, b + 1)
                wait(act, s_t12, b - 1)
                act.activation(raw[:, u, :], p_qk[:, :], ACT.Copy).then_inc(s_raw, 1)
                act.wait_ge(s_raw, b + 1)
                wait(act, s_ss, b)
                act.activation(sq[:, :], raw[:, u, :], ACT.Square).then_inc(s_sq, 1)

            def copy_v(b, u):
                act.wait_ge(s_vm, b + 1)
                wait(act, s_O, 2 * (b - 1))
                act.activation(vaug[:, u, :, 0:DH], p_v[:, :].rearrange("p (h d) -> p h d", h=HEADS), ACT.Copy).then_inc(s_vc, 1)

            act.wait_ge(s_cv, 1)
            for b in range(AHEAD):
                squares(b, b)
                copy_v(b, b)

            def turn(i):
                for u in range(AU):
                    b = i * AU + u
                    wait(act, s_S, 2 * b)
                    for r, to in ((0, qT), (1, kT)):
                        wait(act, s_T, 2 * b + 1 + r)
                        act.activation(to[:, :, :].rearrange("p c n -> p (c n)"), p_t[r][:, :], ACT.Copy).then_inc(s_Tc, 1)
                    for r in range(2):
                        wait(act, s_sub, 2 * b + 1 + r)
                        wait(act, s_PT, 2 * b - 1 + r)
                        act.activation(pr[r][:, :, :], sm[r][:, :, :], ACT.Exp, scale=8.0).then_inc(s_P, 1)
                    if exists(b + AHEAD):
                        squares(b + AHEAD, u)
                    for r in range(2):
                        wait(act, s_PT, 2 * b + 1 + r)
                        wait(act, s_O, 2 * b - 1 + r)
                        act.activation(prT[r][:, :, :].rearrange("p c n -> p (c n)"), p_t[r][:, :], ACT.Copy).then_inc(s_PTc, 1)
                    wait(act, s_oT, b + 1)
                    wait(act, s_dl, b)
                    act.activation(oT[:, :, :].rearrange("p c n -> p (c n)"), p_o[:, :], ACT.Copy).then_inc(s_oTc, 1)
                    if exists(b + AHEAD):
                        copy_v(b + AHEAD, u)

            turns(act, TURNS, turn, 2)

        @block.vector
        def _(dve):
            dve.wait_ge(s_c, 16 * 7)
            dve.tensor_copy(identh[:, :], ident[:, :]).then_inc(s_cc, 1)
            dve.tensor_copy(maskh[:, :], maskf[:, :]).then_inc(s_cc, 1)
            dve.tensor_tensor(tcos[:, :, :], rot[:, 0, :, :], scales[:, :, :], ALU.mult).then_inc(s_tab, 1)
            for lo, hi in ((0, DH // 2), (DH // 2, 0)):
                dve.tensor_tensor(tsin[:, :, lo:lo + DH // 2], rot[:, 1, :, lo:lo + DH // 2],
                                  scales[:, :, hi:hi + DH // 2], ALU.mult).then_inc(s_tab, 1)
            dve.wait_ge(s_tab, 3)

            def rotate(b, u):
                dve.wait_ge(s_raw, b + 1)
                wait(dve, s_qn, b - 1)
                view = "p (w h d) -> p w h d"
                src = raw[:, u, :].rearrange(view, w=2, h=HEADS)
                dve.tensor_tensor(t1[:, u, :].rearrange(view, w=2, h=HEADS), src,
                                  tcos[:, :, None, :].to_broadcast([N, 2, HEADS, DH]), ALU.mult)
                to = t2[:, u, :].rearrange(view, w=2, h=HEADS)
                for lo, hi in ((0, DH // 2), (DH // 2, 0)):
                    ins = dve.tensor_tensor(to[:, :, :, lo:lo + DH // 2], src[:, :, :, hi:hi + DH // 2],
                                            tsin[:, :, None, lo:lo + DH // 2].to_broadcast([N, 2, HEADS, DH // 2]), ALU.mult)
                ins.then_inc(s_t12, 1)
                dve.wait_ge(s_sq, b + 1)
                dve.tensor_reduce(ss[:, u, :], sq[:, :].rearrange("p (g d) -> p g d", g=16), X, ALU.add).then_inc(s_sum, 1)
                dve.wait_ge(s_sum, b + 1)
                dve.tensor_scalar(ss[:, u, :], ss[:, u, :], 1e-24, None, ALU.max).then_inc(s_ss, 1)

            for b in range(AHEAD):
                rotate(b, b)

            def turn(i):
                v = Chain(dve, s_v, i * AU * 4)
                for u in range(AU):
                    b = i * AU + u
                    for r in range(2):
                        wait(dve, s_S, 2 * b + 1 + r)
                        wait(dve, s_P, 2 * b - 1 + r)
                        sv = p_s[r][:, :].rearrange("p (c n) -> p c n", c=4)
                        v.link(dve.tensor_reduce(mx[:, r, :], sv, X, ALU.max))
                        dve.tensor_tensor(sm[r][:, :, :], sv, mx[:, r, :, None].to_broadcast([N, 4, N]),
                                          ALU.subtract).then_inc(s_sub, 1)
                    if exists(b + AHEAD):
                        rotate(b + AHEAD, u)
                    wait(dve, s_oT, b)
                    for r in range(2):
                        wait(dve, s_O, 2 * b + 1 + r)
                        ov = p_s[r][:, 0:4 * (DH + 1)].rearrange("p (c d) -> p c d", c=4)
                        v.link(dve.reciprocal(rinv[:, r, :], ov[:, :, DH]))
                        dve.tensor_tensor(on[:, :, r, :], ov[:, :, 0:DH],
                                          rinv[:, r, :, None].to_broadcast([N, 4, DH]), ALU.mult).then_inc(s_on, 1)
                    wait(dve, s_dl, b + 1)
                    for half, o in HALVES:
                        xb = xl[half, bass.ds(b, 1), o:o + N]
                        ins = dve.tensor_tensor(xb, p_d[half, :].rearrange("p (o n) -> p o n", o=1), xb, ALU.add)
                    ins.then_inc(s_xl, 1)

            turns(dve, TURNS, turn, 2)


FCHUNKS = [(0, 128), (128, 256), (256, HID)]


def ffn_phase(nc, a, layer, xl, x2T, out):
    final = layer == DEPTH - 1
    with ExitStack() as ctx:
        kit = Kit(nc, ctx, f"ff{layer}")
        route, cm = kit.sb("route", [128, 256]), kit.sb("cm", [128, 256])
        ident, ones = route[:, 0:128], route[:, 128:256]
        w1, w1g = kit.sb("w1", [D, 2 * HID]), kit.sb("w1g", [D, 2 * HID])
        w2 = kit.sb("w2", [128, 3, D])
        lg, lb, b2 = kit.sb("lg", [D, 1]), kit.sb("lb", [D, 1]), kit.sb("b2", [D, 1])
        b1, b1l = kit.sb("b1", [128, 6]), kit.sb("b1l", [128, 6])
        minus_half = kit.sb("minus_half", [128, 4])
        sq, rstd = kit.sb("sq", [D, 512]), kit.sb("rstd", [D, 512])
        vs, rs = kit.sb("vs", [N, 4]), kit.sb("rs", [N, 4])
        diag = kit.sb("diag", [N, 4, N])
        hn = kit.sb("hn", [D, 2, 512])
        gg, hm = kit.sb("gg", [128, 3, 512]), kit.sb("hm", [128, 3, 512])
        res, ot = kit.sb("res", [D, 2, 512]), kit.sb("ot", [N, 2, 4, D])
        p_c, p_v = kit.ps("p_c", [128, 512]), kit.ps("p_v", [128, 512])
        p_a = [kit.ps(f"p_a{i}", [128, 512]) for i in range(2)]
        p_g = [kit.ps(f"p_g{i}", [128, 512]) for i in range(2)]
        p_d, p_r = kit.ps("p_d", [128, 512]), kit.ps("p_r", [128, 512])
        (s_c, s_mh, s_bm, s_b1, s_h, s_cen, s_sq, s_var, s_vs, s_rs, s_diag, s_bc, s_rstd, s_hn, s_w1, s_gelu, s_hm, s_d, s_x,
         s_res, s_r, s_ot, s_v) = (kit.sem(n) for n in (
             "c", "mh", "bm", "b1", "h", "cen", "sq", "var", "vs", "rs", "diag", "bc", "rstd", "hn", "w1", "gelu", "hm", "d", "x",
             "res", "r", "ot", "v"))
        s_out = [kit.sem(f"out{u}") for u in range(2)]
        TURNS = J // 2
        block = ctx.enter_context(nc.Block())

        def here(j):
            return not isinstance(j, int) or j < J

        @block.sync
        def _(sp):
            col = "(d o) -> d o"
            sp.dma_start(cm[:, :], a["c_mean"]).then_inc(s_c, 16)
            sp.dma_start(route[:, :], a["c_route"][:, 0:256]).then_inc(s_c, 16)
            sp.dma_start(w1[:, :], a["L1_ffn_w1"][layer]).then_inc(s_c, 16)
            for c, (lo, hi) in enumerate(FCHUNKS):
                sp.dma_start(w2[0:hi - lo, c, :], a["L1_ffn_w2"][layer, lo:hi, :]).then_inc(s_c, 16)
                for part in range(2):
                    o = part * HID
                    sp.dma_start(b1[0:hi - lo, 3 * part + c:3 * part + c + 1],
                                 a["L1_ffn_b1"][layer, o + lo:o + hi].rearrange(col, o=1)).then_inc(s_c, 16)
            for to, name in ((lg, "L1_ffn_ln_g"), (lb, "L1_ffn_ln_b"), (b2, "L1_ffn_b2")):
                sp.dma_start(to[:, :], a[name][layer].rearrange(col, o=1)).then_inc(s_c, 16)
            if final:
                ov = out.rearrange("(j b) n d -> j n b d", b=4)

                def turn(i):
                    for u in range(2):
                        j = 2 * i + u
                        sp.wait_ge(s_ot, j + 1)
                        sp.dma_start(ov[bass.ds(j, 1)].rearrange("o n b d -> n (o b) d"), ot[:, u, :, :]).then_inc(s_out[u], 16)

                turns(sp, TURNS, turn)
                for u in range(2):
                    sp.wait_ge(s_out[u], 16 * TURNS)

        @block.gpsimd
        def _(pool):
            pool.memset(minus_half[:, :], -0.5).then_inc(s_mh, 1)
            pool.wait_ge(s_mh, 1)

            def turn(i):
                for u in range(2):
                    j = 2 * i + u
                    pool.wait_ge(s_vs, j + 1)
                    wait(pool, s_diag, j)
                    pool.tensor_tensor(rs[:, :], vs[:, :], minus_half[:, :], ALU.pow).then_inc(s_rs, 1)

            turns(pool, TURNS, turn)

        @block.tensor
        def _(pe):
            pe.wait_ge(s_c, 16 * 15)
            for c, (lo, hi) in enumerate(FCHUNKS):
                for part in range(2):
                    o = part * HID
                    m = pe.matmul(p_r[0:hi - lo, 3 * part + c:3 * part + c + 1], w1[:, o + lo:o + hi], lb[:, 0:1],
                                  start=True, stop=True)
            m.then_inc(s_bm, 1)

            def center(j):
                wait(pe, s_hn, j)
                pe.matmul(p_c[:, :], cm[:, 0:128], xl[:, bass.ds(4 * j, 4), 0:N],
                          start=True, stop=True).then_inc(s_cen, 1)

            def variance(j):
                wait(pe, s_sq, j + 1)
                wait(pe, s_rstd, j)
                for q in range(4):
                    m = pe.matmul(p_v[:, q:q + 1], sq[:, 128 * q:128 * q + 128], cm[:, 128:129], start=True, stop=True)
                m.then_inc(s_var, 1)

            def broadcast(j):
                wait(pe, s_diag, j + 1)
                pe.matmul(p_v[:, :], ones, diag[:, :, :].rearrange("p b n -> p (b n)"), start=True, stop=True).then_inc(s_bc, 1)

            center(0)
            variance(0)
            broadcast(0)
            pe.wait_ge(s_b1, 2)

            def hidden(j, u, c):
                n, s = 3 * j + c, (3 * u + c) % 2
                lo, hi = FCHUNKS[c]
                wait(pe, s_hm, n - 1)
                wait(pe, s_gelu, n - 1)
                pe.matmul(p_g[s][0:hi - lo, :], w1g[:, HID + lo:HID + hi], hn[:, u, :], start=True, stop=True)
                pe.matmul(p_a[s][0:hi - lo, :], w1g[:, lo:hi], hn[:, u, :], start=True, stop=True).then_inc(s_w1, 1)

            def turn(i):
                for u in range(2):
                    j = 2 * i + u
                    wait(pe, s_hn, j + 1)
                    hidden(j, u, 0)
                    if here(j + 1):
                        center(j + 1)
                    hidden(j, u, 1)
                    if here(j + 1):
                        variance(j + 1)
                    hidden(j, u, 2)
                    if here(j + 1):
                        broadcast(j + 1)
                    wait(pe, s_x, j)
                    for c, (lo, hi) in enumerate(FCHUNKS):
                        wait(pe, s_hm, 3 * j + c + 1)
                        m = pe.matmul(p_d[:, :], w2[0:hi - lo, c, :], hm[0:hi - lo, c, :], start=(c == 0), stop=(c == 2))
                    m.then_inc(s_d, 1)
                    if final:
                        wait(pe, s_res, j + 1)
                        wait(pe, s_ot, j)
                        for b in range(4):
                            t = pe.transpose(p_r[:, 128 * b:128 * b + 128], res[:, u, 128 * b:128 * b + 128], ident)
                        t.then_inc(s_r, 1)

            turns(pe, TURNS, turn)

        @block.scalar
        def _(act):
            def squares(j):
                wait(act, s_cen, j + 1)
                wait(act, s_var, j)
                act.activation(sq[:, :], p_c[:, :], ACT.Square).then_inc(s_sq, 1)

            def copy_rstd(j):
                wait(act, s_bc, j + 1)
                wait(act, s_hn, j)
                act.activation(rstd[:, :], p_v[:, :], ACT.Copy).then_inc(s_rstd, 1)

            squares(0)
            copy_rstd(0)
            act.wait_ge(s_b1, 2)

            def gelu(j, u, c):
                n, s = 3 * j + c, (3 * u + c) % 2
                w = FCHUNKS[c][1] - FCHUNKS[c][0]
                wait(act, s_w1, n + 1)
                wait(act, s_hm, n - 2)
                act.activation(gg[0:w, c, :], p_g[s][0:w, :], ACT.Gelu, bias=b1l[0:w, 3 + c:4 + c]).then_inc(s_gelu, 1)

            def turn(i):
                for u in range(2):
                    j = 2 * i + u
                    gelu(j, u, 0)
                    if here(j + 1):
                        squares(j + 1)
                    gelu(j, u, 1)
                    gelu(j, u, 2)
                    if here(j + 1):
                        copy_rstd(j + 1)
                    if final:
                        wait(act, s_r, j + 1)
                        wait(act, s_out[u], 16 * i)
                        act.activation(ot[:, u, :, :].rearrange("p b d -> p (b d)"), p_r[:, :], ACT.Copy).then_inc(s_ot, 1)

            turns(act, TURNS, turn)

        @block.vector
        def _(dve):
            dve.wait_ge(s_c, 16 * 15)
            dve.tensor_scalar(w1g[:, :], w1[:, :], lg[:, 0:1], None, ALU.mult).then_inc(s_b1, 1)
            dve.wait_ge(s_bm, 1)
            for c, (lo, hi) in enumerate(FCHUNKS):
                w = hi - lo
                for q in (c, 3 + c):
                    m = dve.tensor_tensor(b1l[0:w, q:q + 1], p_r[0:w, q:q + 1], b1[0:w, q:q + 1], ALU.add)
            m.then_inc(s_b1, 1)

            def spread(j):
                wait(dve, s_var, j + 1)
                wait(dve, s_rs, j)
                dve.tensor_scalar(vs[:, :], p_v[:, 0:4], 1e-5, None, ALU.add).then_inc(s_vs, 1)
                wait(dve, s_rs, j + 1)
                wait(dve, s_bc, j)
                dve.tensor_tensor(diag[:, :, :], ident[:, None, :].to_broadcast([N, 4, N]),
                                  rs[:, :, None].to_broadcast([N, 4, N]), ALU.mult).then_inc(s_diag, 1)

            def normal(j, u):
                wait(dve, s_rstd, j + 1)
                wait(dve, s_w1, 3 * (j - 1))
                dve.tensor_tensor(hn[:, u, :], p_c[:, :], rstd[:, :], ALU.mult).then_inc(s_hn, 1)

            def gate(j, u, c):
                n, s = 3 * j + c, (3 * u + c) % 2
                w = FCHUNKS[c][1] - FCHUNKS[c][0]
                wait(dve, s_gelu, n + 1)
                wait(dve, s_d, j)
                dve.scalar_tensor_tensor(out=hm[0:w, c, :], in0=p_a[s][0:w, :], scalar=b1l[0:w, c:c + 1],
                                         in1=gg[0:w, c, :], op0=ALU.add, op1=ALU.mult).then_inc(s_hm, 1)

            spread(0)
            normal(0, 0)

            def turn(i):
                v = Chain(dve, s_v, 2 * i)
                for u in range(2):
                    j = 2 * i + u
                    gate(j, u, 0)
                    gate(j, u, 1)
                    if here(j + 1):
                        spread(j + 1)
                    gate(j, u, 2)
                    if here(j + 1):
                        normal(j + 1, (u + 1) % 2)
                    wait(dve, s_d, j + 1)
                    dv = p_d[:, :].rearrange("p (b n) -> p b n", b=4)
                    rv = res[:, u, :].rearrange("p (b n) -> p b n", b=4)
                    if final:
                        wait(dve, s_r, j - 1)
                    for half, o in HALVES:
                        xv = xl[half, bass.ds(4 * j, 4), o:o + N]
                        ins = dve.scalar_tensor_tensor(out=rv[half] if final else xv, in0=dv[half], scalar=b2[half, 0:1],
                                                       in1=xv, op0=ALU.add, op1=ALU.add)
                    ins.then_inc(s_x, 1)
                    if final:
                        dve.wait_ge(s_x, j + 1)
                        dve.tensor_tensor(rv, rv, x2T[:, :, bass.ds(4 * j, 4)].rearrange("p n b -> p b n"),
                                          ALU.add).then_inc(s_res, 1)

            turns(dve, TURNS, turn)


def program(nc, a, out):
    xbuf = nc.dram_tensor("xbuf", (SLOTS, D), F32, kind="Internal").ap()
    obuf = nc.dram_tensor("obuf", (SLOTS + 128, D), F32, kind="Internal").ap()
    idx_tm = nc.dram_tensor("idx_tm", (N, B, K), I32, kind="Internal").ap()
    w_tm = nc.dram_tensor("w_tm", (N, B, K), F32, kind="Internal").ap()
    with ExitStack() as ctx:
        x2T = ctx.enter_context(nc.sbuf_tensor("x2T", [D, N, B], F32))
        dispatch_phase(nc, a, xbuf, idx_tm, w_tm, x2T)
        expert_phase(nc, a, xbuf, obuf)
        xl = ctx.enter_context(nc.sbuf_tensor("xl", [D, B, N + 1], F32))
        recurrence_phase(nc, a, obuf, idx_tm, w_tm, x2T, xl)
        for layer in range(DEPTH):
            attention_phase(nc, a, layer, xl)
            ffn_phase(nc, a, layer, xl, x2T, out)


def kernel(**inputs):
    import concourse.bacc as bacc
    from concourse.bass_utils import run_bass_kernel_spmd

    nc = bacc.Bacc("TRN2", target_bir_lowering=False, num_devices=1)
    arrays = {k: np.ascontiguousarray(v) for k, v in inputs.items()}
    arrays.update(constants())
    args = {k: nc.dram_tensor(f"in_{k}", v.shape, mybir.dt.from_np(v.dtype), kind="ExternalInput").ap()
            for k, v in arrays.items()}
    out = nc.dram_tensor("out", (B, N, D), F32, kind="ExternalOutput").ap()
    program(nc, args, out)
    r = run_bass_kernel_spmd(nc, [{f"in_{k}": v for k, v in arrays.items()}], core_ids=[0])
    return r.results[0]["out"]
```

```python
from contextlib import ExitStack

import numpy as np

import concourse.bass as bass
from concourse import mybir

F32, BF16, I32, U32 = mybir.dt.float32, mybir.dt.bfloat16, mybir.dt.int32, mybir.dt.uint32
ALU, ACT = mybir.AluOpType, mybir.ActivationFunctionType
X = mybir.AxisListType.X

B, N, D = 32, 128, 128
TOKENS = B * N
E, K, GROUPS = 32, 4, 8
PER_GROUP = E // GROUPS
KEPT_GROUPS = 4
CAP = int(1.25 * TOKENS * K / E)
SLOTS = E * CAP
HEADS, DH, WINDOW = 8, 64, 64
INNER = HEADS * DH
HID = int(D * 4 * 2 / 3)
DEPTH = 2
MASKED = -1e30
HALVES = ((slice(0, D // 2), 0), (slice(D // 2, D), 1))


def constants():
    f = np.float32
    p = np.arange(N)
    route = np.zeros((N, 3 * 128 + E + GROUPS * GROUPS + 1), f)
    route[:, 0:128] = np.eye(128)
    route[:, 128:256] = 1.0
    route[:, 256:384] = -(p[:, None] >= p[None, :]).astype(f)
    route[:, 384:384 + E] = np.arange(E)
    g = np.arange(GROUPS)
    route[:, 384 + E:384 + E + GROUPS * GROUPS] = (g[None, :] < g[:, None]).astype(f).reshape(-1)
    route[:, -1] = SLOTS + p
    half = np.arange(0, DH, 2, dtype=f)
    inv_freq = (1.0 / f(10000.0) ** (half / f(DH))).astype(f)
    t = np.arange(N, dtype=f)
    freqs = (t[:, None] * inv_freq[None, :]).astype(f).astype(np.float64)
    base = (half + 0.4 * DH) / (1.4 * DH)
    power = (t - N // 2) / float(WINDOW // 2)
    scale = base[None, :].astype(np.float64) ** power[:, None].astype(np.float64)
    cos, sin = np.cos(freqs), np.sin(freqs)
    rot = np.zeros((N, 2, 2, DH), f)
    for i, s in enumerate((scale, 1 / scale)):
        rot[:, 0, i] = np.concatenate([cos * s, cos * s], 1)
        rot[:, 1, i] = np.concatenate([-sin * s, sin * s], 1)
    mask = np.zeros((N, N), f)
    i, j = p[:, None], p[None, :]
    mask[(i < j) | (i > j + WINDOW)] = MASKED
    mean = np.full((D, D), 1.0 / D, f)
    center = np.eye(D, dtype=f) - mean
    return {"c_route": route, "c_rot": rot, "c_mask": mask,
            "c_mean": np.concatenate([center, mean], 1)}


class Chain:

    def __init__(self, eng, sem, before=0):
        self.eng, self.sem, self.before, self.n = eng, sem, before, 0

    def add(self, ins):
        ins.then_inc(self.sem, 1)
        self.n += 1
        return self.n

    def wait(self, n):
        self.eng.wait_ge(self.sem, self.before + n)

    def link(self, ins):
        self.wait(self.add(ins))


class Kit:

    def __init__(self, nc, ctx, tag):
        self.nc, self.ctx, self.tag, self.sems = nc, ctx, tag, []
        ctx.callback(self.close)

    def close(self):
        self.nc.clear_and_free_semaphores(self.sems)
        self.nc.all_engine_barrier()

    def sb(self, name, shape, dt=F32):
        return self.ctx.enter_context(self.nc.sbuf_tensor(f"{self.tag}_{name}", shape, dt))

    def ps(self, name, shape, dt=F32):
        return self.ctx.enter_context(self.nc.psum_tensor(f"{self.tag}_{name}", shape, dt))

    def sem(self, name):
        self.sems.append(self.nc.alloc_semaphore(name=f"{self.tag}_{name}"))
        return self.sems[-1]


NG = 4
GB = B // NG
J = 8


def dispatch_phase(nc, a, xbuf, idx_tm, w_tm, zT):
    with ExitStack() as ctx:
        kit = Kit(nc, ctx, "ds")
        xtok = kit.sb("xtok", [N, B, D])
        x1tok = kit.sb("x1tok", [N, B, D])
        x1T = kit.sb("x1T", [D, B, N])
        diag = kit.sb("diag", [D, B, D])
        zero = kit.sb("zero", [128, 4096])
        cst = kit.sb("cst", [128, 3 * 128 + E + GROUPS * GROUPS + 1])
        ident, ones = cst[:, 0:128], cst[:, 128:256]
        iota = cst[:, 384:384 + E]
        before_g = cst[:, 384 + E:384 + E + 64].rearrange("p (g h) -> p g h", g=GROUPS)
        dump = cst[:, 384 + E + 64:384 + E + 65]
        ones_h = kit.sb("ones_h", [128, 128], BF16)
        negtri_h = kit.sb("negtri_h", [128, 128], BF16)
        keep_run = kit.sb("keep_run", [128, E, GB])
        W1, W2 = kit.sb("W1", [D, D]), kit.sb("W2", [D, D])
        W1T, W2T = kit.sb("W1T", [D, D]), kit.sb("W2T", [D, D])
        cond, wg = kit.sb("cond", [B, D]), kit.sb("wg", [E, D])
        condT, wgT = kit.sb("condT", [D, B]), kit.sb("wgT", [D, E])
        b1, b2 = kit.sb("b1", [D, 1]), kit.sb("b2", [D, 1])
        hT, gateT, g1T = kit.sb("hT", [D, B]), kit.sb("gateT", [D, B]), kit.sb("g1T", [D, B])
        sw = kit.sb("sw", [D, 3, 128])
        zs, zh = kit.sb("zs", [128, 512]), kit.sb("zh", [128, 512])
        sc = kit.sb("sc", [N, GB, E])
        ms = kit.sb("ms", [N, GB, E])
        r1 = kit.sb("r1", [N, GB, 4])
        gmax, keepg, keepm = (kit.sb(n, [N, GB, GROUPS]) for n in ("gmax", "keepg", "keepm"))
        cmp1, cmp2 = (kit.sb(n, [N, GB, GROUPS, GROUPS]) for n in ("cmp1", "cmp2"))
        v8 = kit.sb("v8", [N, GB, 8])
        i8 = kit.sb("i8", [N, GB, 8], U32)
        idxf, posk, keepk, destf = (kit.sb(n, [N, GB, K]) for n in ("idxf", "posk", "keepk", "destf"))
        onehot, ohpos = kit.sb("onehot", [N, GB, K, E]), kit.sb("ohpos", [N, GB, K, E])
        maskM = kit.sb("maskM", [N, E, GB], BF16)
        tot, run, pos = (kit.sb(n, [N, E, GB]) for n in ("tot", "run", "pos"))
        carry = kit.sb("carry", [N, E])
        dest = kit.sb("dest", [N, B, K], I32)
        wk = kit.sb("wk", [N, B, K])

        p_b = kit.ps("p_b", [128, 2, 512])
        p_t = kit.ps("p_t", [128, 2, 512])
        p_l = kit.ps("p_l", [N, B, E])
        p_c = kit.ps("p_c", [128, 2, E, GB])
        p_s = kit.ps("p_s", [128, 512])

        s_x = [kit.sem(f"xload{q}") for q in range(4)]
        s_small, s_cst, s_sw = kit.sem("small"), kit.sem("cst"), kit.sem("sw")
        s_zero, s_fill = kit.sem("zero"), kit.sem("fill")
        s_smallT, s_smallc = kit.sem("smallT"), kit.sem("smallc")
        s_h, s_hs, s_g, s_gs = kit.sem("h"), kit.sem("hs"), kit.sem("g"), kit.sem("gs")
        s_diag, s_b, s_x1 = kit.sem("diag"), kit.sem("b"), kit.sem("x1")
        s_t, s_x1T, s_l = kit.sem("t"), kit.sem("x1T"), kit.sem("l")
        s_sub, s_exp = kit.sem("sub"), kit.sem("exp")
        s_M, s_c, s_cr = kit.sem("M"), kit.sem("c"), kit.sem("cr")
        s_zh, s_zs, s_zm, s_zo, s_zc = (kit.sem(n) for n in ("zh", "zs", "zm", "zo", "zc"))
        s_dest, s_sc, s_st = kit.sem("dest"), kit.sem("sc"), kit.sem("st")
        s_v = kit.sem("v")
        block = ctx.enter_context(nc.Block())

        @block.sync
        def _(sp):
            xv = a["x"].rearrange("b n d -> n b d")
            sp.dma_start(cond[:, :], a["cond_1024"]).then_inc(s_small, 16)
            sp.dma_start(W1[:, :], a["L0_cond_W1"]).then_inc(s_small, 16)
            sp.dma_start(W2[:, :], a["L0_cond_W2"]).then_inc(s_small, 16)
            sp.dma_start(wg[:, :], a["L0_ffn_wg"]).then_inc(s_small, 16)
            sp.dma_start(b1[:, :], a["L0_cond_b1"].rearrange("(d o) -> d o", o=1)).then_inc(s_small, 16)
            sp.dma_start(b2[:, :], a["L0_cond_b2"].rearrange("(d o) -> d o", o=1)).then_inc(s_small, 16)
            for q in range(4):
                sp.dma_start(xtok[:, 8 * q:8 * q + 8, :], xv[:, 8 * q:8 * q + 8, :]).then_inc(s_x[q], 16)
            for i, name in enumerate(("L0_ffn_sw1", "L0_ffn_sw3", "L0_ffn_sw2")):
                sp.dma_start(sw[:, i, :], a[name]).then_inc(s_sw, 16)
            for g in range(NG):
                bs = slice(g * GB, (g + 1) * GB)
                sp.wait_ge(s_dest, g + 1)
                sp.dma_start(idx_tm[:, bs, :], dest[:, bs, :]).then_inc(s_st, 16)
                sp.dma_start(w_tm[:, bs, :], wk[:, bs, :]).then_inc(s_st, 16)
            sp.wait_ge(s_st, 32 * NG)

        @block.gpsimd
        def _(pool):
            pool.memset(zero[:, :], 0.0).then_inc(s_zero, 1)
            pool.wait_ge(s_fill, 16 * 5)
            for g in range(NG):
                pool.wait_ge(s_dest, g + 1)
                for b in range(g * GB, (g + 1) * GB):
                    for k in range(K):
                        pool.indirect_dma_start(
                            xbuf, bass.IndirectOffsetOnAxis(ap=dest[:, b, k:k + 1], axis=0),
                            x1tok[:, b, :], None, bounds_check=SLOTS - 1, oob_is_err=False).then_inc(s_sc, 16)
            pool.wait_ge(s_sc, 16 * B * K)

        @block.scalar
        def _(act):
            act.dma_start(cst[:, :], a["c_route"]).then_inc(s_cst, 16)
            act.wait_ge(s_zero, 1)
            rows = SLOTS // 5
            for i in range(5):
                act.dma_start(xbuf[i * rows:(i + 1) * rows, :].rearrange("(p r) d -> p (r d)", p=128),
                              zero[:, :]).then_inc(s_fill, 16)
            act.wait_ge(s_small, 96)
            act.wait_ge(s_h, 1)
            act.activation(hT[:, :], p_s[:, 0:32], ACT.Silu, bias=b1[:, 0:1]).then_inc(s_hs, 1)
            act.wait_ge(s_g, 1)
            act.activation(gateT[:, :], p_s[:, 32:64], ACT.Sigmoid, bias=b2[:, 0:1]).then_inc(s_gs, 1)
            for j in range(J):
                act.wait_ge(s_t, j + 1)
                act.activation(x1T[:, 4 * j:4 * j + 4, :], p_t[:, j % 2, :].rearrange("p (b n) -> p b n", b=4),
                               ACT.Copy).then_inc(s_x1T, 1)
            for g in range(NG):
                act.wait_ge(s_sub, g + 1)
                act.activation(sc[:, :, :], sc[:, :, :], ACT.Exp).then_inc(s_exp, 1)
                for j in (2 * g, 2 * g + 1):
                    act.wait_ge(s_zh, j + 1)
                    if j >= 1:
                        act.wait_ge(s_zm, j)
                    act.activation(zs[:, :], p_b[:, 0, :], ACT.Silu).then_inc(s_zs, 1)
                    act.wait_ge(s_zo, j + 1)
                    act.activation(zT[:, :, 4 * j:4 * j + 4].rearrange("p n b -> p b n"),
                                   p_t[:, 0, :].rearrange("p (b n) -> p b n", b=4), ACT.Copy).then_inc(s_zc, 1)
            act.wait_ge(s_zc, J)

        @block.tensor
        def _(pe):
            pe.wait_ge(s_small, 96)
            pe.wait_ge(s_cst, 16)
            pe.transpose(p_s[:, 128:160], cond[:, :], ident[0:B, 0:B])
            pe.transpose(p_s[:, 160:192], wg[:, :], ident[0:E, 0:E])
            pe.transpose(p_s[:, 192:320], W1[:, :], ident)
            pe.transpose(p_s[:, 320:448], W2[:, :], ident).then_inc(s_smallT, 1)
            pe.wait_ge(s_smallc, 4)
            pe.matmul(p_s[:, 0:32], W1T[:, :], condT[:, :], start=True, stop=True).then_inc(s_h, 1)
            pe.wait_ge(s_hs, 1)
            pe.matmul(p_s[:, 32:64], W2T[:, :], hT[:, :], start=True, stop=True).then_inc(s_g, 1)
            for j in range(J):
                pe.wait_ge(s_diag, j // 2 + 1)
                if j >= 2:
                    pe.wait_ge(s_x1, j - 1)
                pe.matmul(p_b[:, j % 2, :], ones, diag[:, 4 * j:4 * j + 4, :].rearrange("p b d -> p (b d)"),
                          start=True, stop=True).then_inc(s_b, 1)
            for j in range(J):
                pe.wait_ge(s_x1, j + 1)
                if j >= 2:
                    pe.wait_ge(s_x1T, j - 1)
                for i in range(4):
                    t = pe.transpose(p_t[:, j % 2, 128 * i:128 * i + 128], x1tok[:, 4 * j + i, :], ident)
                t.then_inc(s_t, 1)
                pe.wait_ge(s_x1T, j + 1)
                for b in range(4 * j, 4 * j + 4):
                    m = pe.matmul(p_l[:, b, :], x1T[:, b, :], wgT[:, :], start=True, stop=True)
                m.then_inc(s_l, 1)
            pe.wait_ge(s_sw, 48)
            for g in range(NG):
                pe.wait_ge(s_M, g + 1)
                if g >= 1:
                    pe.wait_ge(s_cr, g)
                m = maskM[:, :, :].rearrange("p e b -> p (e b)")
                pe.matmul(p_c[:, 0, :, :].rearrange("p e b -> p (e b)"), ones_h[:, :], m, start=True, stop=True)
                pe.matmul(p_c[:, 1, :, :].rearrange("p e b -> p (e b)"), negtri_h[:, :], m,
                          start=True, stop=True).then_inc(s_c, 1)
                for j in (2 * g, 2 * g + 1):
                    tokens = x1T[:, 4 * j:4 * j + 4, :].rearrange("p b n -> p (b n)")
                    if j >= 1:
                        pe.wait_ge(s_zm, j)
                    pe.matmul(p_b[:, 0, :], sw[:, 0, :], tokens, start=True, stop=True)
                    pe.matmul(p_b[:, 1, :], sw[:, 1, :], tokens, start=True, stop=True).then_inc(s_zh, 1)
                    pe.wait_ge(s_zm, j + 1)
                    if j >= 1:
                        pe.wait_ge(s_zc, j)
                    pe.matmul(p_t[:, 0, :], sw[:, 2, :], zh[:, :], start=True, stop=True).then_inc(s_zo, 1)

        @block.vector
        def _(dve):
            v = Chain(dve, s_v)
            dve.wait_ge(s_cst, 16)
            dve.tensor_copy(ones_h[:, :], ones)
            dve.tensor_copy(negtri_h[:, :], cst[:, 256:384])
            dve.memset(carry[:, :], 0.0)
            v.link(dve.memset(keep_run[:, :, :], 1.0))
            dve.memset(keep_run[:, :, 0:1], 0.0)
            dve.wait_ge(s_smallT, 1)
            dve.tensor_copy(condT[:, :], p_s[:, 128:160]).then_inc(s_smallc, 1)
            dve.tensor_copy(wgT[:, :], p_s[:, 160:192]).then_inc(s_smallc, 1)
            dve.tensor_copy(W1T[:, :], p_s[:, 192:320]).then_inc(s_smallc, 1)
            dve.tensor_copy(W2T[:, :], p_s[:, 320:448]).then_inc(s_smallc, 1)
            dve.wait_ge(s_gs, 1)
            v.link(dve.tensor_scalar(g1T[:, :], gateT[:, :], 1.0, None, ALU.add))
            for q in range(4):
                bs = slice(8 * q, 8 * q + 8)
                dve.tensor_tensor(diag[:, bs, :], ident[:, None, :].to_broadcast([128, 8, 128]),
                                  g1T[:, bs][:, :, None].to_broadcast([128, 8, 128]), ALU.mult).then_inc(s_diag, 1)
            for j in range(J):
                bs = slice(4 * j, 4 * j + 4)
                dve.wait_ge(s_b, j + 1)
                dve.wait_ge(s_x[j // 2], 16)
                dve.tensor_tensor(x1tok[:, bs, :], xtok[:, bs, :],
                                  p_b[:, j % 2, :].rearrange("p (b d) -> p b d", b=4), ALU.mult).then_inc(s_x1, 1)

            def wide(col, n):
                return col[:, :, None].to_broadcast([N, GB, n])

            def shared_expert(j):
                dve.wait_ge(s_zs, j + 1)
                if j >= 1:
                    dve.wait_ge(s_zo, j)
                dve.tensor_tensor(zh[:, :], zs[:, :], p_b[:, 1, :], ALU.mult).then_inc(s_zm, 1)

            for g in range(NG):
                bs = slice(g * GB, (g + 1) * GB)
                dve.wait_ge(s_l, 4 * (g // 2 + 1))
                logits = p_l[:, bs, :]
                v.link(dve.tensor_reduce(r1[:, :, 0], logits, X, ALU.max))
                dve.tensor_tensor(sc[:, :, :], logits, wide(r1[:, :, 0], E), ALU.subtract).then_inc(s_sub, 1)
                dve.wait_ge(s_exp, g + 1)
                v.link(dve.tensor_reduce(r1[:, :, 1], sc[:, :, :], X, ALU.add))
                v.link(dve.reciprocal(r1[:, :, 2], r1[:, :, 1]))
                v.link(dve.tensor_tensor(sc[:, :, :], sc[:, :, :], wide(r1[:, :, 2], E), ALU.mult))
                v.link(dve.tensor_reduce(gmax[:, :, :], sc[:, :, :].rearrange("p b (g i) -> p b g i", g=GROUPS),
                                         X, ALU.max))
                other = gmax[:, :, None, :].to_broadcast([N, GB, GROUPS, GROUPS])
                own = gmax[:, :, :, None].to_broadcast([N, GB, GROUPS, GROUPS])
                dve.tensor_tensor(cmp2[:, :, :, :], other, own, ALU.is_gt)
                v.link(dve.tensor_tensor(cmp1[:, :, :, :], other, own, ALU.is_equal))
                v.link(dve.tensor_tensor(cmp1[:, :, :, :], cmp1[:, :, :, :],
                                         before_g[:, None, :, :].to_broadcast([N, GB, GROUPS, GROUPS]), ALU.mult))
                v.link(dve.tensor_tensor(cmp1[:, :, :, :], cmp1[:, :, :, :], cmp2[:, :, :, :], ALU.add))
                v.link(dve.tensor_reduce(keepm[:, :, :], cmp1[:, :, :, :], X, ALU.add))
                v.link(dve.tensor_scalar(keepg[:, :, :], keepm[:, :, :], float(KEPT_GROUPS), None, ALU.is_lt))
                v.link(dve.tensor_scalar(keepm[:, :, :], keepg[:, :, :], -1.0, None, ALU.add))
                msv = ms[:, :, :].rearrange("p b (g i) -> p b g i", g=GROUPS)
                v.link(dve.tensor_tensor(msv, sc[:, :, :].rearrange("p b (g i) -> p b g i", g=GROUPS),
                                         keepg[:, :, :, None].to_broadcast([N, GB, GROUPS, PER_GROUP]), ALU.mult))
                v.link(dve.tensor_tensor(msv, msv,
                                         keepm[:, :, :, None].to_broadcast([N, GB, GROUPS, PER_GROUP]), ALU.add))
                for b in range(GB):
                    n = v.add(dve.max(v8[:, b, :], ms[:, b, :]))
                v.wait(n)
                for b in range(GB):
                    n = v.add(dve.max_index(i8[:, b, :], v8[:, b, :], ms[:, b, :]))
                v.wait(n)
                v.link(dve.tensor_copy(idxf[:, :, :], i8[:, :, 0:K]))
                if g >= 1:
                    dve.wait_ge(s_c, g)
                v.link(dve.tensor_tensor(onehot[:, :, :, :], idxf[:, :, :, None].to_broadcast([N, GB, K, E]),
                                         iota[:, None, None, :].to_broadcast([N, GB, K, E]), ALU.is_equal))
                with nc.allow_low_precision(reason="zeros and ones"):
                    dve.tensor_reduce(maskM[:, :, :].rearrange("p e b -> p b e"),
                                      onehot[:, :, :, :].rearrange("p b k e -> p b e k"), X, ALU.add).then_inc(s_M, 1)
                v.link(dve.tensor_reduce(r1[:, :, 0], v8[:, :, 0:K], X, ALU.add))
                v.link(dve.tensor_scalar(r1[:, :, 1], r1[:, :, 0], 1e-9, None, ALU.add))
                v.link(dve.reciprocal(r1[:, :, 2], r1[:, :, 1]))
                v.link(dve.tensor_tensor(wk[:, bs, :], v8[:, :, 0:K], wide(r1[:, :, 2], K), ALU.mult))
                dve.wait_ge(s_c, g + 1)
                v.link(dve.tensor_copy(tot[:, :, :], p_c[:, 0, :, :]))
                v.link(dve.tensor_tensor(tot[:, :, 0], tot[:, :, 0], carry[:, :], ALU.add))
                flat = "p e b -> p (e b)"
                v.link(dve.tensor_tensor_scan(run[:, :, :].rearrange(flat), keep_run[:, :, :].rearrange(flat),
                                              tot[:, :, :].rearrange(flat), 0.0, ALU.mult, ALU.add))
                dve.tensor_copy(carry[:, :], run[:, :, GB - 1])
                v.link(dve.tensor_tensor(pos[:, :, :], p_c[:, 1, :, :], run[:, :, :], ALU.add))
                dve.engine_nop().then_inc(s_cr, 1)
                v.link(dve.tensor_tensor(ohpos[:, :, :, :], onehot[:, :, :, :],
                                         pos[:, :, :].rearrange("p e b -> p b e")[:, :, None, :]
                                         .to_broadcast([N, GB, K, E]), ALU.mult))
                v.link(dve.tensor_reduce(posk[:, :, :], ohpos[:, :, :, :], X, ALU.add))
                v.link(dve.tensor_scalar(keepk[:, :, :], posk[:, :, :], float(CAP), None, ALU.is_lt))
                v.link(dve.scalar_tensor_tensor(destf[:, :, :], idxf[:, :, :], float(CAP), posk[:, :, :],
                                                ALU.mult, ALU.add))
                v.link(dve.tensor_tensor(wk[:, bs, :], wk[:, bs, :], keepk[:, :, :], ALU.mult))
                v.link(dve.scalar_tensor_tensor(destf[:, :, :], destf[:, :, :], dump, keepk[:, :, :],
                                                ALU.subtract, ALU.mult))
                dve.tensor_scalar(dest[:, bs, :], destf[:, :, :], dump, None, ALU.add).then_inc(s_dest, 1)
                shared_expert(2 * g)
                shared_expert(2 * g + 1)


def turns(eng, count, body, last=1):
    body(0)
    with eng.Fori(1, count - last, 1) as i:
        body(i)
    for i in range(count - last, count):
        body(i)


def is_last(i, count):
    return isinstance(i, int) and i == count - 1


def wait(eng, sem, value):
    if not isinstance(value, int) or value > 0:
        eng.wait_ge(sem, value)


PARTS = CAP // 128
PA = 3
EU = 4


def expert_phase(nc, a, xbuf, obuf):
    with ExitStack() as ctx:
        kit = Kit(nc, ctx, "ex")
        ident = kit.sb("ident", [128, 128])
        zero = kit.sb("zero", [128, 128])
        xe = kit.sb("xe", [128, EU, PARTS, D])
        we = kit.sb("we", [128, EU, 3, 128])
        xeT = kit.sb("xeT", [D, 2, CAP])
        sa, hh = kit.sb("sa", [128, CAP]), kit.sb("hh", [128, CAP])
        oe = kit.sb("oe", [128, EU, PARTS, D])
        na = PA * 128
        shares = [(0, slice(0, na), range(0, PA)), (1, slice(na, CAP), range(PA, PARTS))]
        p_t = [kit.ps(f"p_t{h}", [128, 512]) for h in range(2)]
        p_1 = [kit.ps(f"p_1{h}", [128, 512]) for h in range(2)]
        p_3 = [kit.ps(f"p_3{h}", [128, 512]) for h in range(2)]
        p_o = [kit.ps(f"p_o{h}", [128, 512]) for h in range(2)]

        s_id, s_zero, s_zst = kit.sem("id"), kit.sem("zero"), kit.sem("zst")
        s_x = [kit.sem(f"x{u}") for u in range(EU)]
        s_w = [kit.sem(f"w{u}") for u in range(EU)]
        s_st = [kit.sem(f"st{u}") for u in range(EU)]
        s_t, s_xT, s_1, s_3, s_silu, s_hh, s_o, s_oe = (
            kit.sem(n) for n in ("t", "xT", "h1", "h3", "silu", "hh", "o", "oe"))
        T = E // EU
        xv = xbuf.rearrange("(e p j) d -> e p j d", p=128, j=PARTS)
        ov = obuf[0:SLOTS, :].rearrange("(e p j) d -> e p j d", p=128, j=PARTS)
        block = ctx.enter_context(nc.Block())

        @block.sync
        def _(sp):
            def load(e, u):
                sp.dma_start(xe[:, u, :, :], xv[bass.ds(e, 1)].rearrange("o p j d -> p (o j) d")).then_inc(s_x[u], 16)
                for i, name in enumerate(("L0_ffn_w1", "L0_ffn_w3", "L0_ffn_w2")):
                    sp.dma_start(we[:, u, i, :], a[name][bass.ds(e, 1)].rearrange("o p n -> p (o n)")).then_inc(s_w[u], 16)

            sp.dma_start(ident[:, :], a["c_route"][:, 0:128]).then_inc(s_id, 16)
            for u in range(EU):
                load(u, u)
            sp.wait_ge(s_zero, 1)
            sp.dma_start(obuf[SLOTS:SLOTS + 128, :], zero[:, :]).then_inc(s_zst, 16)

            def turn(i):
                for u in range(EU):
                    e = i * EU + u
                    wait(sp, s_oe, (e + 1) * 2)
                    sp.dma_start(ov[bass.ds(e, 1)].rearrange("o p j d -> p (o j) d"), oe[:, u, :, :]).then_inc(s_st[u], 16)
                    if not is_last(i, T):
                        load(e + EU, u)

            turns(sp, T, turn)
            for u in range(EU):
                sp.wait_ge(s_st[u], 16 * T)
            sp.wait_ge(s_zst, 16)

        @block.gpsimd
        def _(pool):
            pool.memset(zero[:, :], 0.0).then_inc(s_zero, 1)

        @block.tensor
        def _(pe):
            def transposes(e, u, i):
                wait(pe, s_x[u], 16 * (i + 1))
                for h, _, tiles in shares:
                    wait(pe, s_xT, 2 * e - 1 + h)
                    for j in tiles:
                        t = pe.transpose(p_t[h][:, 128 * (j - tiles[0]):128 * (j - tiles[0]) + 128],
                                         xe[:, u, j, :], ident[:, :])
                    t.then_inc(s_t, 1)

            def turn(i):
                for u in range(EU):
                    e = i * EU + u
                    wait(pe, s_w[u], 48 * (i + 1))
                    for h, cols, tiles in shares:
                        n = len(tiles) * 128
                        wait(pe, s_xT, 2 * e + 1 + h)
                        wait(pe, s_silu, 2 * e - 1 + h)
                        pe.matmul(p_1[h][:, 0:n], we[:, u, 0, :], xeT[:, u % 2, cols], start=True, stop=True).then_inc(s_1, 1)
                        wait(pe, s_hh, 2 * e - 1 + h)
                        pe.matmul(p_3[h][:, 0:n], we[:, u, 1, :], xeT[:, u % 2, cols], start=True, stop=True).then_inc(s_3, 1)
                    if not (is_last(i, T) and u == EU - 1):
                        transposes(e + 1, (u + 1) % EU, i + (u + 1) // EU)
                    for h, cols, tiles in shares:
                        wait(pe, s_hh, 2 * e + 1 + h)
                        wait(pe, s_oe, 2 * e - 1 + h)
                        for j in tiles:
                            q = 128 * (j - tiles[0])
                            m = pe.matmul(p_o[h][:, q:q + 128], hh[:, 128 * j:128 * j + 128], we[:, u, 2, :],
                                          start=True, stop=True)
                        m.then_inc(s_o, 1)

            pe.wait_ge(s_id, 16)
            transposes(0, 0, 0)
            turns(pe, T, turn)

        @block.scalar
        def _(act):
            def copy_xT(e, u):
                for h, cols, tiles in shares:
                    wait(act, s_t, 2 * e + 1 + h)
                    wait(act, s_3, 2 * e - 3 + h)
                    act.activation(xeT[:, u % 2, cols], p_t[h][:, 0:len(tiles) * 128], ACT.Copy).then_inc(s_xT, 1)

            def turn(i):
                for u in range(EU):
                    e = i * EU + u
                    for h, cols, tiles in shares:
                        wait(act, s_1, 2 * e + 1 + h)
                        wait(act, s_hh, 2 * e - 1 + h)
                        act.activation(sa[:, cols], p_1[h][:, 0:len(tiles) * 128], ACT.Silu).then_inc(s_silu, 1)
                    if not (is_last(i, T) and u == EU - 1):
                        copy_xT(e + 1, u + 1)

            copy_xT(0, 0)
            turns(act, T, turn)

        @block.vector
        def _(dve):
            def turn(i):
                for u in range(EU):
                    e = i * EU + u
                    for h, cols, tiles in shares:
                        wait(dve, s_silu, 2 * e + 1 + h)
                        wait(dve, s_3, 2 * e + 1 + h)
                        wait(dve, s_o, 2 * e - 1 + h)
                        dve.tensor_tensor(hh[:, cols], sa[:, cols], p_3[h][:, 0:len(tiles) * 128],
                                          ALU.mult).then_inc(s_hh, 1)
                    for h, cols, tiles in shares:
                        wait(dve, s_o, 2 * e + 1 + h)
                        if h == 0:
                            wait(dve, s_st[u], 16 * i)
                        dve.tensor_copy(oe[:, u, tiles[0]:tiles[-1] + 1, :],
                                        p_o[h][:, 0:len(tiles) * 128].rearrange("p (j d) -> p j d", d=D)
                                        ).then_inc(s_oe, 1)

            turns(dve, T, turn)


CT = 4
CHUNKS = N // CT
CU = 4


def recurrence_phase(nc, a, obuf, idx_tm, w_tm, zT, xl):
    with ExitStack() as ctx:
        kit = Kit(nc, ctx, "rc")
        ident, cond = kit.sb("ident", [128, 128]), kit.sb("cond", [B, D])
        Wx, Wh, bias = kit.sb("Wx", [D, D]), kit.sb("Wh", [D, D]), kit.sb("bias", [D, 1])
        h0T = kit.sb("h0T", [D, B])
        ix, wc = kit.sb("ix", [128, CU, K], I32), kit.sb("wc", [128, CU, K])
        xc = kit.sb("xc", [128, CU, D])
        rows = kit.sb("rows", [128, CU, K, D])
        acc = kit.sb("acc", [128, 2, D])
        hr = kit.sb("hr", [D, CU, CT, B])
        p_0 = kit.ps("p_0", [128, 512])
        p_t = [kit.ps(f"p_t{i}", [128, 512]) for i in range(2)]
        p_w = [kit.ps(f"p_w{i}", [128, 512]) for i in range(2)]
        s_k, s_h0, s_h0c = kit.sem("k"), kit.sem("h0"), kit.sem("h0c")
        s_in = [kit.sem(f"in{u}") for u in range(CU)]
        s_g = [kit.sem(f"g{u}") for u in range(CU)]
        s_acc, s_t, s_x2, s_mm, s_h, s_hc, s_v = (kit.sem(n) for n in ("acc", "t", "x2", "mm", "h", "hc", "v"))
        T = CHUNKS // CU
        ixv = idx_tm.rearrange("(c t) b k -> c (t b) k", t=CT)
        wv = w_tm.rearrange("(c t) b k -> c (t b) k", t=CT)
        xv = a["x"].rearrange("b (c t) d -> c t b d", t=CT)
        block = ctx.enter_context(nc.Block())

        @block.sync
        def _(sp):
            def load(c, u):
                sp.dma_start(ix[:, u, :], ixv[bass.ds(c, 1)].rearrange("o p k -> p (o k)")).then_inc(s_in[u], 16)
                sp.dma_start(wc[:, u, :], wv[bass.ds(c, 1)].rearrange("o p k -> p (o k)")).then_inc(s_in[u], 16)
                for t in range(CT):
                    sp.dma_start(xc[B * t:B * t + B, u, :],
                                 xv[bass.ds(c, 1), t].rearrange("o b d -> b (o d)")).then_inc(s_in[u], 16)

            load(0, 0)
            sp.dma_start(ident[:, :], a["c_route"][:, 0:128]).then_inc(s_k, 16)
            sp.dma_start(cond[:, :], a["cond_1024"]).then_inc(s_k, 16)
            sp.dma_start(Wx[:, :], a["L1_cond_Wx"]).then_inc(s_k, 16)
            sp.dma_start(Wh[:, :], a["L1_cond_Wh"]).then_inc(s_k, 16)
            sp.dma_start(bias[:, :], a["L1_cond_b"].rearrange("(d o) -> d o", o=1)).then_inc(s_k, 16)
            for u in range(1, CU):
                load(u, u)

            def turn(i):
                for u in range(CU):
                    if not is_last(i, T):
                        sp.wait_ge(s_acc, i * CU + u + 1)
                        load(i * CU + u + CU, u)

            turns(sp, T, turn)

        @block.gpsimd
        def _(pool):
            for c in range(CHUNKS):
                i, u = divmod(c, CU)
                pool.wait_ge(s_in[u], (i + 1) * 16 * (2 + CT))
                wait(pool, s_acc, c - CU + 1)
                for k in range(K):
                    pool.indirect_dma_start(
                        rows[:, u, k, :], None, obuf,
                        bass.IndirectOffsetOnAxis(ap=ix[:, u, k:k + 1], axis=0)).then_inc(s_g[u], 16)

        @block.vector
        def _(dve):
            dve.memset(xl[D // 2:D, :, 0:1], 0.0)
            dve.wait_ge(s_h0, 1)
            dve.tensor_copy(h0T[:, :], p_0[:, 0:B]).then_inc(s_h0c, 1)

            def keep_h(c, u):
                dve.wait_ge(s_h, (c + 1) * CT)
                for half, o in HALVES:
                    ins = dve.tensor_copy(xl[half, :, bass.ds(c * CT + o, CT)], hr[half, u, :, :].rearrange("p t b -> p b t"))
                ins.then_inc(s_hc, 1)

            def turn(i):
                v = Chain(dve, s_v, i * CU * (K - 1))
                for u in range(CU):
                    c = i * CU + u
                    dve.wait_ge(s_g[u], (i + 1) * 16 * K)
                    wait(dve, s_t, c - 1)
                    dve.wait_ge(s_in[u], (i + 1) * 16 * (2 + CT))
                    for k in range(K):
                        add_to = xc[:, u, :] if k == 0 else acc[:, u % 2, :]
                        ins = dve.scalar_tensor_tensor(out=acc[:, u % 2, :], in0=rows[:, u, k, :],
                                                       scalar=wc[:, u, k:k + 1], in1=add_to,
                                                       op0=ALU.mult, op1=ALU.add)
                        if k < K - 1:
                            v.link(ins)
                    ins.then_inc(s_acc, 1)
                    dve.wait_ge(s_t, c + 1)
                    zc = zT[:, bass.ds(c * CT, CT), :]
                    dve.tensor_tensor(zc, p_t[u % 2][:, 0:128].rearrange("p (t b) -> p t b", t=CT), zc,
                                      ALU.add).then_inc(s_x2, 1)
                    if u > 0:
                        keep_h(c - 1, u - 1)
                    elif not (isinstance(i, int) and i == 0):
                        keep_h(c - 1, CU - 1)

            turns(dve, T, turn)
            keep_h(CHUNKS - 1, CU - 1)

        @block.tensor
        def _(pe):
            pe.wait_ge(s_k, 80)
            pe.transpose(p_0[:, 0:B], cond[:, :], ident[0:B, 0:B]).then_inc(s_h0, 1)
            pe.wait_ge(s_h0c, 1)

            def turn(i):
                for u in range(CU):
                    c = i * CU + u
                    pe.wait_ge(s_acc, c + 1)
                    wait(pe, s_x2, c - 1)
                    pe.transpose(p_t[u % 2][:, 0:128], acc[:, u % 2, :], ident[:, :]).then_inc(s_t, 1)
                    pe.wait_ge(s_x2, c + 1)
                    pe.matmul(p_w[u % 2][:, 0:128], Wx[:, :], zT[:, bass.ds(c * CT, CT), :].rearrange("p t b -> p (t b)"),
                              start=True, stop=True, skip_group_check=True)
                    for t in range(CT):
                        if t > 0:
                            prev = hr[:, u, t - 1, :]
                        elif u > 0 or not (isinstance(i, int) and i == 0):
                            prev = hr[:, (u - 1) % CU, CT - 1, :]
                        else:
                            prev = h0T[:, :]
                        wait(pe, s_h, c * CT + t)
                        pe.matmul(p_w[u % 2][:, B * t:B * t + B], Wh[:, :], prev, start=False, stop=True,
                                  skip_group_check=True).then_inc(s_mm, 1)

            turns(pe, T, turn)

        @block.scalar
        def _(act):
            act.wait_ge(s_k, 80)

            def turn(i):
                for u in range(CU):
                    c = i * CU + u
                    wait(act, s_hc, c - CU + 1)
                    for t in range(CT):
                        act.wait_ge(s_mm, c * CT + t + 1)
                        act.activation(hr[:, u, t, :], p_w[u % 2][:, B * t:B * t + B], ACT.Tanh,
                                       bias=bias[:, 0:1]).then_inc(s_h, 1)

            turns(act, T, turn)




def exists(b):
    return not isinstance(b, int) or 0 <= b < B


AU = 4
LO, HI = 0, 1


def attention_phase(nc, a, layer, xl):
    with ExitStack() as ctx:
        kit = Kit(nc, ctx, f"at{layer}")
        ident, mask = kit.sb("ident", [128, 128]), kit.sb("mask", [N, N])
        wqkv, wo = kit.sb("wqkv", [D, 3 * INNER]), kit.sb("wo", [128, 4, D])
        rot, scales = kit.sb("rot", [N, 2, 2, DH]), kit.sb("scales", [N, 2, DH])
        tcos, tsin = kit.sb("tcos", [N, 2, DH]), kit.sb("tsin", [N, 2, DH])
        minus_half = kit.sb("minus_half", [N, 16])
        h = kit.sb("h", [D, 2, N])
        raw = kit.sb("raw", [N, 2, 2 * INNER])
        sq = kit.sb("sq", [N, 2 * INNER])
        ss, rn = kit.sb("ss", [N, 2, 16]), kit.sb("rn", [N, 2, 16])
        t1, t2 = kit.sb("t1", [N, 2, 2 * INNER]), kit.sb("t2", [N, 2, 2 * INNER])
        qn = kit.sb("qn", [N, 2, 2 * INNER])
        vaug = kit.sb("vaug", [N, AU, HEADS, DH + 1])
        qT = kit.sb("qT", [128, 4, N])
        kT = kit.sb("kT", [128, 4, 2, N])
        mx, gate = kit.sb("mx", [N, 2, 4]), kit.sb("gate", [N, 2])
        sm, pr, prT = ([kit.sb(f"{n}{r}", [N, 4, N]) for r in range(2)] for n in ("sm", "pr", "prT"))
        rinv = kit.sb("rinv", [N, 2, 4])
        on = kit.sb("on", [N, HEADS, DH])
        oT = kit.sb("oT", [128, 4, AU, N])
        p_qk = kit.ps("p_qk", [N, 2 * INNER])
        p_v = kit.ps("p_v", [128, 512])
        p_t = [kit.ps(f"p_t{r}", [128, 512]) for r in range(2)]
        p_s = [kit.ps(f"p_s{r}", [128, 512]) for r in range(2)]
        p_o = kit.ps("p_o", [128, 512])

        s_c, s_tab, s_zero, s_one = kit.sem("c"), kit.sem("tab"), kit.sem("zero"), kit.sem("one")
        (s_h, s_qk, s_v, s_raw, s_vc, s_sq, s_sum, s_ss, s_t1, s_t2, s_rn, s_add, s_qn, s_Tq, s_Tk, s_Tqc, s_Tkc, s_oT,
         s_oTc, s_wo, s_xl) = (kit.sem(n) for n in (
             "h", "qk", "v", "raw", "vc", "sq", "sum", "ss", "t1", "t2", "rn", "add", "qn", "Tq", "Tk", "Tqc", "Tkc", "oT",
             "oTc", "wo", "xl"))
        s_S, s_mx, s_sub, s_P, s_PT, s_PTc, s_O, s_rinv, s_on = (
            [kit.sem(f"{n}{r}") for r in range(2)] for n in ("S", "mx", "sub", "P", "PT", "PTc", "O", "rinv", "on"))
        TURNS = B // AU
        block = ctx.enter_context(nc.Block())

        @block.sync
        def _(sp):
            sp.dma_start(wqkv[:, :], a["L1_ffn_wqkv"][layer]).then_inc(s_c, 16)
            sp.dma_start(rot[:, :, :, :], a["c_rot"]).then_inc(s_c, 16)
            for i, name in enumerate(("L1_ffn_q_scale", "L1_ffn_k_scale")):
                sp.dma_start(scales[:, i, :], a[name][layer:layer + 1, :].to_broadcast([N, DH])).then_inc(s_c, 16)
            sp.dma_start(ident[:, :], a["c_route"][:, 0:128]).then_inc(s_c, 16)
            sp.dma_start(mask[:, :], a["c_mask"]).then_inc(s_c, 16)
            sp.dma_start(wo[:, :, :], a["L1_ffn_wo"][layer].rearrange("(c p) d -> p c d", p=128)).then_inc(s_c, 16)

        @block.gpsimd
        def _(pool):
            def shifted(b, u):
                wait(pool, s_v, b - 1)
                pool.tensor_copy(h[:, u % 2, :].rearrange("p (o n) -> p o n", o=1), xl[:, bass.ds(b, 1), 0:N]).then_inc(s_h, 1)

            def normal(b, u):
                u = u % 2
                wait(pool, s_ss, b + 1)
                wait(pool, s_qn, b - 1)
                pool.tensor_tensor(rn[:, u, :], ss[:, u, :], minus_half[:, :], ALU.pow).then_inc(s_rn, 1)
                wait(pool, s_t1, b + 1)
                wait(pool, s_t2, b + 1)
                wait(pool, s_Tk, b - 1)
                pool.tensor_tensor(qn[:, u, :], t1[:, u, :], t2[:, u, :], ALU.add).then_inc(s_add, 1)
                wait(pool, s_rn, b + 1)
                wait(pool, s_add, b + 1)
                qv = qn[:, u, :].rearrange("p (g d) -> p g d", g=16)
                pool.tensor_tensor(qv, qv, rn[:, u, :, None].to_broadcast([N, 16, DH]), ALU.mult).then_inc(s_qn, 1)

            shifted(0, 0)
            shifted(1, 1)
            pool.memset(minus_half[:, :], -0.5).then_inc(s_one, 1)
            pool.memset(vaug[:, :, :, DH:DH + 1], 1.0).then_inc(s_one, 1)
            pool.memset(kT[:, :, :, :], 0.0).then_inc(s_zero, 1)
            pool.wait_ge(s_one, 1)
            shifted(2, 2)
            normal(0, 0)
            shifted(3, 3)
            normal(1, 1)

            def turn(i):
                for u in range(AU):
                    b = i * AU + u
                    if exists(b + 4):
                        shifted(b + 4, u)
                    if exists(b + 2):
                        normal(b + 2, u)

            turns(pool, TURNS, turn)

        @block.tensor
        def _(pe):
            def project(b, u, group):
                wait(pe, s_h, b + 1)
                wait(pe, s_raw, b)
                for w in range(2):
                    m = pe.matmul(p_qk[:, w * INNER:(w + 1) * INNER], h[:, u % 2, :], wqkv[:, w * INNER:(w + 1) * INNER],
                                  start=True, stop=True)
                m.then_inc(s_qk, 1)
                wait(pe, s_vc, b)
                wait(pe, s_oTc, b - 4)
                wait(pe, s_xl, group)
                pe.matmul(p_v[:, :], h[:, u % 2, :], wqkv[:, 2 * INNER:], start=True, stop=True).then_inc(s_v, 1)

            def transpose_qk(b, u):
                wait(pe, s_qn, b + 1)
                for w, sem in ((0, s_Tq), (1, s_Tk)):
                    wait(pe, s_PTc[w], b - w)
                    for c in range(4):
                        q = w * INNER + 128 * c
                        t = pe.transpose(p_t[w][:, 128 * c:128 * c + 128], qn[:, u % 2, q:q + 128], ident[:, :])
                    t.then_inc(sem, 1)

            def scores(b, r):
                wait(pe, s_Tqc, b + 1)
                wait(pe, s_Tkc, 2 * b + 2)
                wait(pe, s_mx[r], b)
                for c in range(2):
                    m = pe.matmul(p_s[r][:, 256 * c:256 * c + 256], qT[:, 2 * r + c, :],
                                  kT[:, 2 * r + c, :, :].rearrange("p j n -> p (j n)"), start=True, stop=True)
                m.then_inc(s_S[r], 1)

            def transpose_p(b, r):
                wait(pe, s_P[r], b + 1)
                if r == HI:
                    wait(pe, s_Tkc, 2 * b + (4 if exists(b + 1) else 2))
                for j in range(4):
                    t = pe.transpose(p_t[r][:, 128 * j:128 * j + 128], pr[r][:, j, :], ident[:, :])
                t.then_inc(s_PT[r], 1)

            def output(b, u, r):
                wait(pe, s_PTc[r], b + 1)
                wait(pe, s_vc, b + 1)
                wait(pe, s_on[1 - r], b + r)
                for j in range(4):
                    m = pe.matmul(p_o[:, (DH + 1) * j:(DH + 1) * (j + 1)], prT[r][:, j, :], vaug[:, u, 4 * r + j, :],
                                  start=True, stop=True)
                m.then_inc(s_O[r], 1)

            def transpose_o(b):
                wait(pe, s_on[HI], b + 1)
                wait(pe, s_on[LO], b + 1)
                wait(pe, s_vc, b + 5 if exists(b + 4) else B)
                if not exists(b + 4):
                    wait(pe, s_oTc, b)
                for c in range(4):
                    t = pe.transpose(p_v[:, 128 * c:128 * c + 128], on[:, 2 * c:2 * c + 2, :].rearrange("p r d -> p (r d)"),
                                     ident[:, :])
                t.then_inc(s_oT, 1)

            def out_project(g):
                wait(pe, s_oTc, AU * g + AU)
                wait(pe, s_vc, AU * g + 8 if exists(AU * g + 8) else B)
                for c in range(4):
                    m = pe.matmul(p_v[:, :], wo[:, c, :], oT[:, c, :, :].rearrange("p b n -> p (b n)"),
                                  start=(c == 0), stop=(c == 3))
                m.then_inc(s_wo, 1)

            pe.wait_ge(s_c, 16 * 7)
            for b in range(3):
                project(b, b, 0)
            transpose_qk(0, 0)

            def turn(i):
                for u in range(AU):
                    b = i * AU + u
                    scores(b, LO)
                    if exists(b - 1):
                        transpose_p(b - 1, HI)
                    if u == 1 and exists(b - AU):
                        out_project(i - 1)
                    if exists(b + 3):
                        project(b + 3, u + 3, i if u == 1 else 0)
                    if exists(b - 1):
                        output(b - 1, (u - 1) % AU, HI)
                    transpose_p(b, LO)
                    scores(b, HI)
                    if exists(b + 1):
                        transpose_qk(b + 1, u + 1)
                    if exists(b - 1):
                        transpose_o(b - 1)
                    output(b, u, LO)

            turns(pe, TURNS, turn)
            transpose_p(B - 1, HI)
            output(B - 1, AU - 1, HI)
            transpose_o(B - 1)
            out_project(TURNS - 1)

        @block.scalar
        def _(act):
            def copy_qk(b, u):
                wait(act, s_qk, b + 1)
                wait(act, s_t1, b - 1)
                wait(act, s_t2, b - 1)
                wait(act, s_sq, b - 1)
                act.activation(raw[:, u % 2, :], p_qk[:, :], ACT.Copy).then_inc(s_raw, 1)

            def copy_v(b, u):
                wait(act, s_v, b + 1)
                wait(act, s_O[HI], b - 3)
                wait(act, s_O[LO], b - 3)
                act.activation(vaug[:, u % AU, :, 0:DH], p_v[:, :].rearrange("p (h d) -> p h d", h=HEADS), ACT.Copy).then_inc(s_vc, 1)

            def square(b, u):
                wait(act, s_raw, b + 1)
                wait(act, s_sum, b)
                act.activation(sq[:, :], raw[:, u % 2, :], ACT.Square).then_inc(s_sq, 1)

            def copy_qkT(b):
                wait(act, s_Tq, b + 1)
                wait(act, s_S[HI], b)
                act.activation(qT[:, :, :].rearrange("p c n -> p (c n)"), p_t[0][:, :], ACT.Copy).then_inc(s_Tqc, 1)
                wait(act, s_Tk, b + 1)
                for j in range(2):
                    half = slice(64 * j, 64 * j + 64)
                    act.activation(kT[half, :, j, :], p_t[1][half, :].rearrange("p (c n) -> p c n", c=4),
                                   ACT.Copy).then_inc(s_Tkc, 1)

            def exp(b, r):
                wait(act, s_sub[r], b + 1)
                wait(act, s_PT[r], b)
                act.activation(pr[r][:, :, :], sm[r][:, :, :], ACT.Exp, scale=8.0).then_inc(s_P[r], 1)

            def copy_pT(b, r):
                wait(act, s_PT[r], b + 1)
                wait(act, s_O[r], b)
                act.activation(prT[r][:, :, :].rearrange("p c n -> p (c n)"), p_t[r][:, :], ACT.Copy).then_inc(s_PTc[r], 1)

            def copy_oT(b, u, group):
                wait(act, s_oT, b + 1)
                wait(act, s_wo, group)
                act.activation(oT[:, :, u, :], p_v[:, :].rearrange("p (c n) -> p c n", c=4), ACT.Copy).then_inc(s_oTc, 1)

            act.wait_ge(s_one, 2)
            act.wait_ge(s_zero, 1)
            for b in range(3):
                copy_qk(b, b)
                copy_v(b, b)
                square(b, b)
            copy_qkT(0)

            def turn(i):
                for u in range(AU):
                    b = i * AU + u
                    if exists(b - 1):
                        copy_pT(b - 1, HI)
                    exp(b, LO)
                    if exists(b + 3):
                        copy_qk(b + 3, u + 3)
                        copy_v(b + 3, u + 3)
                    copy_pT(b, LO)
                    if exists(b + 3):
                        square(b + 3, u + 3)
                    if exists(b + 1):
                        copy_qkT(b + 1)
                    if exists(b - 1):
                        copy_oT(b - 1, (u - 1) % AU, i if u == 1 else 0)
                    exp(b, HI)

            turns(act, TURNS, turn)
            copy_pT(B - 1, HI)
            copy_oT(B - 1, AU - 1, TURNS - 1)

        @block.vector
        def _(dve):
            dve.wait_ge(s_c, 16 * 7)
            dve.tensor_tensor(tcos[:, :, :], rot[:, 0, :, :], scales[:, :, :], ALU.mult).then_inc(s_tab, 1)
            for lo, hi in ((0, DH // 2), (DH // 2, 0)):
                dve.tensor_tensor(tsin[:, :, lo:lo + DH // 2], rot[:, 1, :, lo:lo + DH // 2],
                                  scales[:, :, hi:hi + DH // 2], ALU.mult).then_inc(s_tab, 1)
            dve.wait_ge(s_tab, 3)
            view = "p (w h d) -> p w h d"

            def norms(b, u):
                wait(dve, s_sq, b + 1)
                wait(dve, s_rn, b - 1)
                dve.tensor_reduce(ss[:, u % 2, :], sq[:, :].rearrange("p (g d) -> p g d", g=16), X, ALU.add).then_inc(s_sum, 1)
                wait(dve, s_sum, b + 1)
                dve.tensor_scalar(ss[:, u % 2, :], ss[:, u % 2, :], 1e-24, None, ALU.max).then_inc(s_ss, 1)

            def rotate_cos(b, u):
                wait(dve, s_raw, b + 1)
                wait(dve, s_add, b - 1)
                dve.tensor_tensor(t1[:, u % 2, :].rearrange(view, w=2, h=HEADS), raw[:, u % 2, :].rearrange(view, w=2, h=HEADS),
                                  tcos[:, :, None, :].to_broadcast([N, 2, HEADS, DH]), ALU.mult).then_inc(s_t1, 1)

            def rotate_sin(b, u):
                src = raw[:, u % 2, :].rearrange(view, w=2, h=HEADS)
                to = t2[:, u % 2, :].rearrange(view, w=2, h=HEADS)
                for lo, hi in ((0, DH // 2), (DH // 2, 0)):
                    ins = dve.tensor_tensor(to[:, :, :, lo:lo + DH // 2], src[:, :, :, hi:hi + DH // 2],
                                            tsin[:, :, None, lo:lo + DH // 2].to_broadcast([N, 2, HEADS, DH // 2]), ALU.mult)
                ins.then_inc(s_t2, 1)

            def masked(b, r):
                wait(dve, s_S[r], b + 1)
                wait(dve, s_P[r], b)
                wait(dve, s_sub[r], b)
                dve.memset(gate[:, r:r + 1], 0.0)
                for j in range(4):
                    m = dve.tensor_tensor_reduce(out=sm[r][:, j, :], in0=p_s[r][:, 128 * j:128 * j + 128], in1=mask[:, :],
                                                 scale=1.0, scalar=3 * MASKED, op0=ALU.add, op1=ALU.max,
                                                 accum_out=mx[:, r, j:j + 1])
                m.then_inc(s_mx[r], 1)
                wait(dve, s_mx[r], b + 1)
                dve.tensor_tensor(sm[r][:, :, :], sm[r][:, :, :], mx[:, r, :, None].to_broadcast([N, 4, N]),
                                  ALU.subtract).then_inc(s_sub[r], 1)

            def divide(b, r):
                wait(dve, s_O[r], b + 1)
                wait(dve, s_on[r], b)
                ov = p_o[:, 0:4 * (DH + 1)].rearrange("p (c d) -> p c d", c=4)
                dve.reciprocal(rinv[:, r, :], ov[:, :, DH]).then_inc(s_rinv[r], 1)
                wait(dve, s_rinv[r], b + 1)
                wait(dve, s_oT, b)
                dve.tensor_tensor(on[:, 4 * r:4 * r + 4, :], ov[:, :, 0:DH], rinv[:, r, :, None].to_broadcast([N, 4, DH]),
                                  ALU.mult).then_inc(s_on[r], 1)

            def add_group(g):
                wait(dve, s_wo, g + 1)
                wait(dve, s_h, AU * g + AU)
                for half, o in HALVES:
                    xb = xl[half, bass.ds(AU * g, AU), o:o + N]
                    ins = dve.tensor_tensor(xb, p_v[half, :].rearrange("p (b n) -> p b n", b=AU), xb, ALU.add)
                ins.then_inc(s_xl, 1)

            for b in range(2):
                norms(b, b)
                rotate_cos(b, b)
                rotate_sin(b, b)

            def turn(i):
                for u in range(AU):
                    b = i * AU + u
                    masked(b, LO)
                    if exists(b + 2):
                        norms(b + 2, u)
                        rotate_cos(b + 2, u)
                    if u == 1 and exists(b - AU):
                        add_group(i - 1)
                    if exists(b - 1):
                        divide(b - 1, HI)
                    if exists(b + 2):
                        rotate_sin(b + 2, u)
                    masked(b, HI)
                    divide(b, LO)

            turns(dve, TURNS, turn)
            divide(B - 1, HI)
            add_group(TURNS - 1)


FCHUNKS = [(0, 128), (128, 256), (256, HID)]


def ffn_phase(nc, a, layer, xl, x2T, out):
    final = layer == DEPTH - 1
    with ExitStack() as ctx:
        kit = Kit(nc, ctx, f"ff{layer}")
        route, cm = kit.sb("route", [128, 256]), kit.sb("cm", [128, 256])
        ident, ones = route[:, 0:128], route[:, 128:256]
        w1, w1g = kit.sb("w1", [D, 2 * HID]), kit.sb("w1g", [D, 2 * HID])
        w2 = kit.sb("w2", [128, 3, D])
        lg, lb, b2 = kit.sb("lg", [D, 1]), kit.sb("lb", [D, 1]), kit.sb("b2", [D, 1])
        b1, b1l = kit.sb("b1", [128, 6]), kit.sb("b1l", [128, 6])
        minus_half = kit.sb("minus_half", [128, 4])
        sq, rstd = kit.sb("sq", [D, 512]), kit.sb("rstd", [D, 512])
        vs, rs = kit.sb("vs", [N, 4]), kit.sb("rs", [N, 4])
        diag = kit.sb("diag", [N, 4, N])
        hn = kit.sb("hn", [D, 2, 512])
        gg, hm = kit.sb("gg", [128, 3, 512]), kit.sb("hm", [128, 3, 512])
        res, ot = kit.sb("res", [D, 2, 512]), kit.sb("ot", [N, 2, 4, D])
        p_c, p_v = kit.ps("p_c", [128, 512]), kit.ps("p_v", [128, 512])
        p_a = [kit.ps(f"p_a{i}", [128, 512]) for i in range(2)]
        p_g = [kit.ps(f"p_g{i}", [128, 512]) for i in range(2)]
        p_d, p_r = kit.ps("p_d", [128, 512]), kit.ps("p_r", [128, 512])
        (s_c, s_mh, s_bm, s_b1, s_h, s_cen, s_sq, s_var, s_vs, s_rs, s_diag, s_bc, s_rstd, s_hn, s_w1, s_gelu, s_hm, s_d, s_x,
         s_res, s_r, s_ot, s_v) = (kit.sem(n) for n in (
             "c", "mh", "bm", "b1", "h", "cen", "sq", "var", "vs", "rs", "diag", "bc", "rstd", "hn", "w1", "gelu", "hm", "d", "x",
             "res", "r", "ot", "v"))
        s_out = [kit.sem(f"out{u}") for u in range(2)]
        TURNS = J // 2
        block = ctx.enter_context(nc.Block())

        def here(j):
            return not isinstance(j, int) or j < J

        @block.sync
        def _(sp):
            col = "(d o) -> d o"
            sp.dma_start(cm[:, :], a["c_mean"]).then_inc(s_c, 16)
            sp.dma_start(route[:, :], a["c_route"][:, 0:256]).then_inc(s_c, 16)
            sp.dma_start(w1[:, :], a["L1_ffn_w1"][layer]).then_inc(s_c, 16)
            for c, (lo, hi) in enumerate(FCHUNKS):
                sp.dma_start(w2[0:hi - lo, c, :], a["L1_ffn_w2"][layer, lo:hi, :]).then_inc(s_c, 16)
                for part in range(2):
                    o = part * HID
                    sp.dma_start(b1[0:hi - lo, 3 * part + c:3 * part + c + 1],
                                 a["L1_ffn_b1"][layer, o + lo:o + hi].rearrange(col, o=1)).then_inc(s_c, 16)
            for to, name in ((lg, "L1_ffn_ln_g"), (lb, "L1_ffn_ln_b"), (b2, "L1_ffn_b2")):
                sp.dma_start(to[:, :], a[name][layer].rearrange(col, o=1)).then_inc(s_c, 16)
            if final:
                ov = out.rearrange("(j b) n d -> j n b d", b=4)

                def turn(i):
                    for u in range(2):
                        j = 2 * i + u
                        sp.wait_ge(s_ot, j + 1)
                        sp.dma_start(ov[bass.ds(j, 1)].rearrange("o n b d -> n (o b) d"), ot[:, u, :, :]).then_inc(s_out[u], 16)

                turns(sp, TURNS, turn)
                for u in range(2):
                    sp.wait_ge(s_out[u], 16 * TURNS)

        @block.gpsimd
        def _(pool):
            pool.memset(minus_half[:, :], -0.5).then_inc(s_mh, 1)
            pool.wait_ge(s_mh, 1)

            def turn(i):
                for u in range(2):
                    j = 2 * i + u
                    pool.wait_ge(s_vs, j + 1)
                    wait(pool, s_diag, j)
                    pool.tensor_tensor(rs[:, :], vs[:, :], minus_half[:, :], ALU.pow).then_inc(s_rs, 1)

            turns(pool, TURNS, turn)

        @block.tensor
        def _(pe):
            pe.wait_ge(s_c, 16 * 15)
            for c, (lo, hi) in enumerate(FCHUNKS):
                for part in range(2):
                    o = part * HID
                    m = pe.matmul(p_r[0:hi - lo, 3 * part + c:3 * part + c + 1], w1[:, o + lo:o + hi], lb[:, 0:1],
                                  start=True, stop=True)
            m.then_inc(s_bm, 1)

            def center(j):
                wait(pe, s_hn, j)
                pe.matmul(p_c[:, :], cm[:, 0:128], xl[:, bass.ds(4 * j, 4), 0:N],
                          start=True, stop=True).then_inc(s_cen, 1)

            def variance(j):
                wait(pe, s_sq, j + 1)
                wait(pe, s_rstd, j)
                for q in range(4):
                    m = pe.matmul(p_v[:, q:q + 1], sq[:, 128 * q:128 * q + 128], cm[:, 128:129], start=True, stop=True)
                m.then_inc(s_var, 1)

            def broadcast(j):
                wait(pe, s_diag, j + 1)
                pe.matmul(p_v[:, :], ones, diag[:, :, :].rearrange("p b n -> p (b n)"), start=True, stop=True).then_inc(s_bc, 1)

            center(0)
            variance(0)
            broadcast(0)
            pe.wait_ge(s_b1, 2)

            def hidden(j, u, c):
                n, s = 3 * j + c, (3 * u + c) % 2
                lo, hi = FCHUNKS[c]
                wait(pe, s_hm, n - 1)
                wait(pe, s_gelu, n - 1)
                pe.matmul(p_g[s][0:hi - lo, :], w1g[:, HID + lo:HID + hi], hn[:, u, :], start=True, stop=True)
                pe.matmul(p_a[s][0:hi - lo, :], w1g[:, lo:hi], hn[:, u, :], start=True, stop=True).then_inc(s_w1, 1)

            def turn(i):
                for u in range(2):
                    j = 2 * i + u
                    wait(pe, s_hn, j + 1)
                    hidden(j, u, 0)
                    if here(j + 1):
                        center(j + 1)
                    hidden(j, u, 1)
                    if here(j + 1):
                        variance(j + 1)
                    hidden(j, u, 2)
                    if here(j + 1):
                        broadcast(j + 1)
                    wait(pe, s_x, j)
                    for c, (lo, hi) in enumerate(FCHUNKS):
                        wait(pe, s_hm, 3 * j + c + 1)
                        m = pe.matmul(p_d[:, :], w2[0:hi - lo, c, :], hm[0:hi - lo, c, :], start=(c == 0), stop=(c == 2))
                    m.then_inc(s_d, 1)
                    if final:
                        wait(pe, s_res, j + 1)
                        wait(pe, s_ot, j)
                        for b in range(4):
                            t = pe.transpose(p_r[:, 128 * b:128 * b + 128], res[:, u, 128 * b:128 * b + 128], ident)
                        t.then_inc(s_r, 1)

            turns(pe, TURNS, turn)

        @block.scalar
        def _(act):
            def squares(j):
                wait(act, s_cen, j + 1)
                wait(act, s_var, j)
                act.activation(sq[:, :], p_c[:, :], ACT.Square).then_inc(s_sq, 1)

            def copy_rstd(j):
                wait(act, s_bc, j + 1)
                wait(act, s_hn, j)
                act.activation(rstd[:, :], p_v[:, :], ACT.Copy).then_inc(s_rstd, 1)

            squares(0)
            copy_rstd(0)
            act.wait_ge(s_b1, 2)

            def gelu(j, u, c):
                n, s = 3 * j + c, (3 * u + c) % 2
                w = FCHUNKS[c][1] - FCHUNKS[c][0]
                wait(act, s_w1, n + 1)
                wait(act, s_hm, n - 2)
                act.activation(gg[0:w, c, :], p_g[s][0:w, :], ACT.Gelu, bias=b1l[0:w, 3 + c:4 + c]).then_inc(s_gelu, 1)

            def turn(i):
                for u in range(2):
                    j = 2 * i + u
                    gelu(j, u, 0)
                    if here(j + 1):
                        squares(j + 1)
                    gelu(j, u, 1)
                    gelu(j, u, 2)
                    if here(j + 1):
                        copy_rstd(j + 1)
                    if final:
                        wait(act, s_r, j + 1)
                        wait(act, s_out[u], 16 * i)
                        act.activation(ot[:, u, :, :].rearrange("p b d -> p (b d)"), p_r[:, :], ACT.Copy).then_inc(s_ot, 1)

            turns(act, TURNS, turn)

        @block.vector
        def _(dve):
            dve.wait_ge(s_c, 16 * 15)
            dve.tensor_scalar(w1g[:, :], w1[:, :], lg[:, 0:1], None, ALU.mult).then_inc(s_b1, 1)
            dve.wait_ge(s_bm, 1)
            for c, (lo, hi) in enumerate(FCHUNKS):
                w = hi - lo
                for q in (c, 3 + c):
                    m = dve.tensor_tensor(b1l[0:w, q:q + 1], p_r[0:w, q:q + 1], b1[0:w, q:q + 1], ALU.add)
            m.then_inc(s_b1, 1)

            def spread(j):
                wait(dve, s_var, j + 1)
                wait(dve, s_rs, j)
                dve.tensor_scalar(vs[:, :], p_v[:, 0:4], 1e-5, None, ALU.add).then_inc(s_vs, 1)
                wait(dve, s_rs, j + 1)
                wait(dve, s_bc, j)
                dve.tensor_tensor(diag[:, :, :], ident[:, None, :].to_broadcast([N, 4, N]),
                                  rs[:, :, None].to_broadcast([N, 4, N]), ALU.mult).then_inc(s_diag, 1)

            def normal(j, u):
                wait(dve, s_rstd, j + 1)
                wait(dve, s_w1, 3 * (j - 1))
                dve.tensor_tensor(hn[:, u, :], p_c[:, :], rstd[:, :], ALU.mult).then_inc(s_hn, 1)

            def gate(j, u, c):
                n, s = 3 * j + c, (3 * u + c) % 2
                w = FCHUNKS[c][1] - FCHUNKS[c][0]
                wait(dve, s_gelu, n + 1)
                wait(dve, s_d, j)
                dve.scalar_tensor_tensor(out=hm[0:w, c, :], in0=p_a[s][0:w, :], scalar=b1l[0:w, c:c + 1],
                                         in1=gg[0:w, c, :], op0=ALU.add, op1=ALU.mult).then_inc(s_hm, 1)

            spread(0)
            normal(0, 0)

            def turn(i):
                v = Chain(dve, s_v, 2 * i)
                for u in range(2):
                    j = 2 * i + u
                    gate(j, u, 0)
                    gate(j, u, 1)
                    if here(j + 1):
                        spread(j + 1)
                    gate(j, u, 2)
                    if here(j + 1):
                        normal(j + 1, (u + 1) % 2)
                    wait(dve, s_d, j + 1)
                    dv = p_d[:, :].rearrange("p (b n) -> p b n", b=4)
                    rv = res[:, u, :].rearrange("p (b n) -> p b n", b=4)
                    if final:
                        wait(dve, s_r, j - 1)
                    for half, o in HALVES:
                        xv = xl[half, bass.ds(4 * j, 4), o:o + N]
                        ins = dve.scalar_tensor_tensor(out=rv[half] if final else xv, in0=dv[half], scalar=b2[half, 0:1],
                                                       in1=xv, op0=ALU.add, op1=ALU.add)
                    ins.then_inc(s_x, 1)
                    if final:
                        dve.wait_ge(s_x, j + 1)
                        dve.tensor_tensor(rv, rv, x2T[:, :, bass.ds(4 * j, 4)].rearrange("p n b -> p b n"),
                                          ALU.add).then_inc(s_res, 1)

            turns(dve, TURNS, turn)


def program(nc, a, out):
    xbuf = nc.dram_tensor("xbuf", (SLOTS, D), F32, kind="Internal").ap()
    obuf = nc.dram_tensor("obuf", (SLOTS + 128, D), F32, kind="Internal").ap()
    idx_tm = nc.dram_tensor("idx_tm", (N, B, K), I32, kind="Internal").ap()
    w_tm = nc.dram_tensor("w_tm", (N, B, K), F32, kind="Internal").ap()
    with ExitStack() as ctx:
        x2T = ctx.enter_context(nc.sbuf_tensor("x2T", [D, N, B], F32))
        dispatch_phase(nc, a, xbuf, idx_tm, w_tm, x2T)
        expert_phase(nc, a, xbuf, obuf)
        xl = ctx.enter_context(nc.sbuf_tensor("xl", [D, B, N + 1], F32))
        recurrence_phase(nc, a, obuf, idx_tm, w_tm, x2T, xl)
        for layer in range(DEPTH):
            attention_phase(nc, a, layer, xl)
            ffn_phase(nc, a, layer, xl, x2T, out)


def kernel(**inputs):
    import concourse.bacc as bacc
    from concourse.bass_utils import run_bass_kernel_spmd

    nc = bacc.Bacc("TRN2", target_bir_lowering=False, num_devices=1)
    arrays = {k: np.ascontiguousarray(v) for k, v in inputs.items()}
    arrays.update(constants())
    args = {k: nc.dram_tensor(f"in_{k}", v.shape, mybir.dt.from_np(v.dtype), kind="ExternalInput").ap()
            for k, v in arrays.items()}
    out = nc.dram_tensor("out", (B, N, D), F32, kind="ExternalOutput").ap()
    program(nc, args, out)
    r = run_bass_kernel_spmd(nc, [{f"in_{k}": v for k, v in arrays.items()}], core_ids=[0])
    return r.results[0]["out"]
```

```python
from contextlib import ExitStack

import numpy as np

import concourse.bass as bass
from concourse import mybir

F32, BF16, I32, U32 = mybir.dt.float32, mybir.dt.bfloat16, mybir.dt.int32, mybir.dt.uint32
F32R = mybir.dt.float32r
ALU, ACT = mybir.AluOpType, mybir.ActivationFunctionType
X = mybir.AxisListType.X

B, N, D = 32, 128, 128
TOKENS = B * N
E, K, GROUPS = 32, 4, 8
PER_GROUP = E // GROUPS
KEPT_GROUPS = 4
CAP = int(1.25 * TOKENS * K / E)
SLOTS = E * CAP
HEADS, DH, WINDOW = 8, 64, 64
INNER = HEADS * DH
HID = int(D * 4 * 2 / 3)
DEPTH = 2
MASKED = -1e20
FCHUNKS = [(0, 128), (128, 256), (256, HID)]
CT = 4
CHUNKS = N // CT
HALVES = ((slice(0, D // 2), 0), (slice(D // 2, D), 1))


def constants():
    f = np.float32
    p = np.arange(N)
    route = np.zeros((N, 3 * 128 + E + GROUPS * GROUPS + 1), f)
    route[:, 0:128] = np.eye(128)
    route[:, 128:256] = 1.0
    route[:, 256:384] = -(p[:, None] >= p[None, :]).astype(f)
    route[:, 384:384 + E] = np.arange(E)
    g = np.arange(GROUPS)
    route[:, 384 + E:384 + E + GROUPS * GROUPS] = (g[None, :] < g[:, None]).astype(f).reshape(-1)
    route[:, -1] = SLOTS + p
    half = np.arange(0, DH, 2, dtype=f)
    inv_freq = (1.0 / f(10000.0) ** (half / f(DH))).astype(f)
    t = np.arange(N, dtype=f)
    freqs = (t[:, None] * inv_freq[None, :]).astype(f).astype(np.float64)
    base = (half + 0.4 * DH) / (1.4 * DH)
    power = (t - N // 2) / float(WINDOW // 2)
    scale = base[None, :].astype(np.float64) ** power[:, None].astype(np.float64)
    cos, sin = np.cos(freqs), np.sin(freqs)
    rot = np.zeros((N, 2, 2, DH), f)
    for i, s in enumerate((scale, 1 / scale)):
        rot[:, 0, i] = np.concatenate([cos * s, cos * s], 1)
        rot[:, 1, i] = np.concatenate([-sin * s, sin * s], 1)
    mask = np.zeros((N, N), f)
    i, j = p[:, None], p[None, :]
    mask[(i < j) | (i > j + WINDOW)] = MASKED
    mean = np.full((D, D), 1.0 / D, f)
    center = np.eye(D, dtype=f) - mean
    return {"c_route": route, "c_rot": rot, "c_mask": mask,
            "c_mean": np.concatenate([center, mean], 1)}


class Chain:

    def __init__(self, eng, sem, before=0):
        self.eng, self.sem, self.before, self.n = eng, sem, before, 0

    def add(self, ins):
        ins.then_inc(self.sem, 1)
        self.n += 1
        return self.n

    def wait(self, n):
        self.eng.wait_ge(self.sem, self.before + n)

    def link(self, ins):
        self.wait(self.add(ins))


class Kit:

    def __init__(self, nc, ctx, tag):
        self.nc, self.ctx, self.tag, self.sems = nc, ctx, tag, []
        ctx.callback(self.close)

    def close(self):
        self.nc.clear_and_free_semaphores(self.sems)
        self.nc.all_engine_barrier()

    def sb(self, name, shape, dt=F32):
        return self.ctx.enter_context(self.nc.sbuf_tensor(f"{self.tag}_{name}", shape, dt))

    def ps(self, name, shape, dt=F32):
        return self.ctx.enter_context(self.nc.psum_tensor(f"{self.tag}_{name}", shape, dt))

    def sem(self, name):
        self.sems.append(self.nc.alloc_semaphore(name=f"{self.tag}_{name}"))
        return self.sems[-1]




class Resident:

    def __init__(self, nc, ctx):
        def sb(name, shape, dt=F32):
            return ctx.enter_context(nc.sbuf_tensor(f"r_{name}", shape, dt))

        self.cst = sb("cst", [128, 3 * 128 + E + GROUPS * GROUPS + 1])
        self.ident, self.ones = self.cst[:, 0:128], self.cst[:, 128:256]
        self.xc = sb("xc", [128, CHUNKS, D])
        self.ix, self.wc = sb("ix", [128, CHUNKS, K], I32), sb("wc", [128, CHUNKS, K])
        self.cond, self.bias = sb("cond", [B, D]), sb("bias", [D, 1])
        self.Wx, self.Wh = sb("Wx", [D, D]), sb("Wh", [D, D])
        self.mask = sb("mask", [N, N])
        self.rot, self.scales = sb("rot", [N, 2, 2, DH]), sb("scales", [N, DEPTH, 2, DH])
        self.tcos, self.tsin = sb("tcos", [N, DEPTH, 2, DH]), sb("tsin", [N, DEPTH, 2, DH])
        self.wqkv, self.wo = sb("wqkv", [D, DEPTH, 3 * INNER]), sb("wo", [128, DEPTH, 4, D])
        self.cm = sb("cm", [128, 256])
        self.w1, self.w1g = sb("w1", [D, DEPTH, 2 * HID]), sb("w1g", [D, DEPTH, 2 * HID])
        self.w2 = sb("w2", [128, DEPTH, 3, D])
        self.lg, self.lb, self.b2 = sb("lg", [D, DEPTH]), sb("lb", [D, DEPTH]), sb("b2", [D, DEPTH])
        self.b1, self.b1l = sb("b1", [128, DEPTH, 6]), sb("b1l", [128, DEPTH, 6])

    def parts(self, nc, ctx):
        def sb(name, shape):
            return ctx.enter_context(nc.sbuf_tensor(f"r_{name}", shape, F32R))

        self.wqkv_high, self.wqkv_low = sb("wqkv_high", [D, DEPTH, 3 * INNER]), sb("wqkv_low", [D, DEPTH, 3 * INNER])
        self.w1g_high, self.w1g_low = sb("w1g_high", [D, DEPTH, 2 * HID]), sb("w1g_low", [D, DEPTH, 2 * HID])

    def load(self, q, a, sem):
        col = "(d o) -> d o"
        xv = a["x"].rearrange("b (c t) d -> t b c d", t=CT)
        pairs = [(self.xc[B * t:B * t + B, :, :], xv[t]) for t in range(CT)]
        pairs += [(self.Wx[:, :], a["L1_cond_Wx"]), (self.Wh[:, :], a["L1_cond_Wh"]),
                  (self.bias[:, :], a["L1_cond_b"].rearrange(col, o=1)),
                  (self.mask[:, :], a["c_mask"]), (self.rot[:, :, :, :], a["c_rot"]), (self.cm[:, :], a["c_mean"])]
        for layer in range(DEPTH):
            pairs += [(self.wqkv[:, layer, :], a["L1_ffn_wqkv"][layer]),
                      (self.wo[:, layer, :, :], a["L1_ffn_wo"][layer].rearrange("(c p) d -> p c d", p=128)),
                      (self.w1[:, layer, :], a["L1_ffn_w1"][layer])]
            for i, name in enumerate(("L1_ffn_q_scale", "L1_ffn_k_scale")):
                pairs.append((self.scales[:, layer, i, :], a[name][layer:layer + 1, :].to_broadcast([N, DH])))
            for c, (lo, hi) in enumerate(FCHUNKS):
                pairs.append((self.w2[0:hi - lo, layer, c, :], a["L1_ffn_w2"][layer, lo:hi, :]))
                for part in range(2):
                    o = part * HID
                    pairs.append((self.b1[0:hi - lo, layer, 3 * part + c:3 * part + c + 1],
                                  a["L1_ffn_b1"][layer, o + lo:o + hi].rearrange(col, o=1)))
            for to, name in ((self.lg, "L1_ffn_ln_g"), (self.lb, "L1_ffn_ln_b"), (self.b2, "L1_ffn_b2")):
                pairs.append((to[:, layer:layer + 1], a[name][layer].rearrange(col, o=1)))
        for to, src in pairs:
            q.dma_start(to, src).then_inc(sem, 16)
        return 16 * len(pairs)


NG = 8
GB = B // NG
J = NG


def dispatch_phase(nc, a, r, xbuf, idx_tm, w_tm, zT):
    with ExitStack() as ctx:
        kit = Kit(nc, ctx, "ds")
        xtok = kit.sb("xtok", [N, B, D])
        x1tok = kit.sb("x1tok", [N, B, D])
        x1T = kit.sb("x1T", [D, B, N])
        diag = kit.sb("diag", [D, B, D])
        zero = kit.sb("zero", [128, 4096])
        cst, ident, ones, cond = r.cst, r.ident, r.ones, r.cond
        iota = cst[:, 384:384 + E]
        before_g = cst[:, 384 + E:384 + E + 64].rearrange("p (g h) -> p g h", g=GROUPS)
        dump = cst[:, 384 + E + 64:384 + E + 65]
        ones_h = kit.sb("ones_h", [128, 128], BF16)
        negtri_h = kit.sb("negtri_h", [128, 128], BF16)
        keep_run = kit.sb("keep_run", [128, E, GB])
        W1, W2 = kit.sb("W1", [D, D]), kit.sb("W2", [D, D])
        W1T, W2T = kit.sb("W1T", [D, D]), kit.sb("W2T", [D, D])
        wg = kit.sb("wg", [E, D])
        condT, wgT = kit.sb("condT", [D, B]), kit.sb("wgT", [D, E])
        b1, b2 = kit.sb("b1", [D, 1]), kit.sb("b2", [D, 1])
        hT, gateT, g1T = kit.sb("hT", [D, B]), kit.sb("gateT", [D, B]), kit.sb("g1T", [D, B])
        sig, warm = kit.sb("sig", [D, B]), kit.sb("warm", [D, 3])
        sw = kit.sb("sw", [D, 3, 128])
        zs, zh = kit.sb("zs", [128, 512]), kit.sb("zh", [128, 512])
        sc = kit.sb("sc", [N, GB, E])
        ms = kit.sb("ms", [N, GB, E])
        r1 = kit.sb("r1", [N, GB, 4])
        gmax, keepg, keepm = (kit.sb(n, [N, GB, GROUPS]) for n in ("gmax", "keepg", "keepm"))
        cmp1, cmp2 = (kit.sb(n, [N, GB, GROUPS, GROUPS]) for n in ("cmp1", "cmp2"))
        v8 = kit.sb("v8", [N, GB, 8])
        i8 = kit.sb("i8", [N, GB, 8], U32)
        idxf, posk, keepk, destf = (kit.sb(n, [N, GB, K]) for n in ("idxf", "posk", "keepk", "destf"))
        onehot, ohpos = kit.sb("onehot", [N, GB, K, E]), kit.sb("ohpos", [N, GB, K, E])
        maskM = kit.sb("maskM", [N, E, GB], BF16)
        tot, run, pos = (kit.sb(n, [N, E, GB]) for n in ("tot", "run", "pos"))
        carry = kit.sb("carry", [N, E])
        dest = kit.sb("dest", [N, B, K], I32)
        wk = kit.sb("wk", [N, B, K])

        p_b = kit.ps("p_b", [128, 2, 512])
        p_t = kit.ps("p_t", [128, 2, 512])
        p_l = kit.ps("p_l", [N, B, E])
        p_c = kit.ps("p_c", [128, 2, E, GB])
        p_s = kit.ps("p_s", [128, 512])

        s_x = [kit.sem(f"xload{q}") for q in range(4)]
        s_small, s_cst, s_sw = kit.sem("small"), kit.sem("cst"), kit.sem("sw")
        s_zero, s_fill = kit.sem("zero"), [kit.sem(f"fill{i}") for i in range(CAP // N)]
        s_smallT, s_smallc = kit.sem("smallT"), kit.sem("smallc")
        s_h, s_hs, s_g, s_gs = kit.sem("h"), kit.sem("hs"), kit.sem("g"), kit.sem("gs")
        s_diag, s_b, s_x1 = kit.sem("diag"), kit.sem("b"), kit.sem("x1")
        s_t, s_x1T, s_l = kit.sem("t"), kit.sem("x1T"), kit.sem("l")
        s_sub, s_exp = kit.sem("sub"), kit.sem("exp")
        s_M, s_c, s_cr = kit.sem("M"), kit.sem("c"), kit.sem("cr")
        s_zh, s_zs, s_zm, s_zo, s_zc = (kit.sem(n) for n in ("zh", "zs", "zm", "zo", "zc"))
        s_dest, s_sc, s_st = kit.sem("dest"), kit.sem("sc"), kit.sem("st")
        s_v, s_res, s_warm, s_sig = kit.sem("v"), kit.sem("res"), kit.sem("warm"), kit.sem("sig")
        block = ctx.enter_context(nc.Block())

        @block.sync
        def _(sp):
            xv = a["x"].rearrange("b n d -> n b d")
            sp.dma_start(cond[:, :], a["cond_1024"]).then_inc(s_small, 16)
            sp.dma_start(W1[:, :], a["L0_cond_W1"]).then_inc(s_small, 16)
            sp.dma_start(W2[:, :], a["L0_cond_W2"]).then_inc(s_small, 16)
            sp.dma_start(wg[:, :], a["L0_ffn_wg"]).then_inc(s_small, 16)
            sp.dma_start(b1[:, :], a["L0_cond_b1"].rearrange("(d o) -> d o", o=1)).then_inc(s_small, 16)
            sp.dma_start(b2[:, :], a["L0_cond_b2"].rearrange("(d o) -> d o", o=1)).then_inc(s_small, 16)
            for q in range(4):
                sp.dma_start(xtok[:, 8 * q:8 * q + 8, :], xv[:, 8 * q:8 * q + 8, :]).then_inc(s_x[q], 16)
            for i, name in enumerate(("L0_ffn_sw1", "L0_ffn_sw3", "L0_ffn_sw2")):
                sp.dma_start(sw[:, i, :], a[name]).then_inc(s_sw, 16)
            sp.wait_ge(s_zero, 1)
            for i in range(CAP // N):
                sp.dma_start(xbuf.rearrange("(e i n) d -> i n e d", e=E, n=N)[i],
                             zero[:, :].rearrange("p (e d) -> p e d", d=D)).then_inc(s_fill[i], 16)
            loaded = r.load(sp, a, s_res)
            for g in range(NG):
                bs = slice(g * GB, (g + 1) * GB)
                sp.wait_ge(s_dest, g + 1)
                sp.dma_start(idx_tm[:, bs, :], dest[:, bs, :]).then_inc(s_st, 16)
                sp.dma_start(w_tm[:, bs, :], wk[:, bs, :]).then_inc(s_st, 16)
            sp.wait_ge(s_st, 32 * NG)
            sp.wait_ge(s_res, loaded)

        @block.gpsimd
        def _(pool):
            pool.memset(zero[:, :], 0.0).then_inc(s_zero, 1)
            for g in range(NG):
                pool.wait_ge(s_dest, g + 1)
                for b in range(g * GB, (g + 1) * GB):
                    if b < CAP // N:
                        pool.wait_ge(s_fill[b], 16)
                    for k in range(K):
                        pool.indirect_dma_start(
                            xbuf, bass.IndirectOffsetOnAxis(ap=dest[:, b, k:k + 1], axis=0),
                            x1tok[:, b, :], None, bounds_check=SLOTS - 1, oob_is_err=False).then_inc(s_sc, 16)
            pool.wait_ge(s_sc, 16 * B * K)

        @block.scalar
        def _(act):
            act.dma_start(cst[:, :], a["c_route"]).then_inc(s_cst, 16)
            act.wait_ge(s_warm, 1)
            act.activation(warm[:, 1:2], warm[:, 0:1], ACT.Sigmoid)
            act.wait_ge(s_small, 96)
            act.wait_ge(s_h, 1)
            act.activation(sig[:, :], p_s[:, 0:32], ACT.Sigmoid, bias=b1[:, 0:1]).then_inc(s_sig, 1)
            act.wait_ge(s_g, 1)
            act.activation(gateT[:, :], p_s[:, 32:64], ACT.Sigmoid, bias=b2[:, 0:1]).then_inc(s_gs, 1)
            act.activation(warm[:, 2:3], warm[:, 0:1], ACT.Exp)
            def exp(g):
                act.wait_ge(s_sub, g + 1)
                act.activation(sc[:, :, :], sc[:, :, :], ACT.Exp).then_inc(s_exp, 1)

            for j in range(J):
                act.wait_ge(s_t, j + 1)
                act.activation(x1T[:, 4 * j:4 * j + 4, :], p_t[:, j % 2, :].rearrange("p (b n) -> p b n", b=4),
                               ACT.Copy).then_inc(s_x1T, 1)
                if j == 2:
                    exp(0)
            for g in range(NG):
                if g >= 1:
                    exp(g)
                act.wait_ge(s_zh, g + 1)
                if g >= 1:
                    act.wait_ge(s_zm, g)
                act.activation(zs[:, :], p_b[:, 0, :], ACT.Silu).then_inc(s_zs, 1)
                act.wait_ge(s_zo, g + 1)
                act.activation(zT[:, :, 4 * g:4 * g + 4].rearrange("p n b -> p b n"),
                               p_t[:, 0, :].rearrange("p (b n) -> p b n", b=4), ACT.Copy).then_inc(s_zc, 1)
            act.wait_ge(s_zc, J)

        @block.tensor
        def _(pe):
            pe.wait_ge(s_small, 96)
            pe.wait_ge(s_cst, 16)
            pe.transpose(p_s[:, 128:160], cond[:, :], ident[0:B, 0:B])
            pe.transpose(p_s[:, 160:192], wg[:, :], ident[0:E, 0:E])
            pe.transpose(p_s[:, 192:320], W1[:, :], ident)
            pe.transpose(p_s[:, 320:448], W2[:, :], ident).then_inc(s_smallT, 1)
            pe.wait_ge(s_smallc, 4)
            pe.matmul(p_s[:, 0:32], W1T[:, :], condT[:, :], start=True, stop=True).then_inc(s_h, 1)
            pe.wait_ge(s_hs, 1)
            pe.matmul(p_s[:, 32:64], W2T[:, :], hT[:, :], start=True, stop=True).then_inc(s_g, 1)
            def gates(j):
                pe.wait_ge(s_diag, j + 1)
                if j >= 2:
                    pe.wait_ge(s_x1, j - 1)
                pe.matmul(p_b[:, j % 2, :], ones, diag[:, 4 * j:4 * j + 4, :].rearrange("p b d -> p (b d)"),
                          start=True, stop=True).then_inc(s_b, 1)
            def tokens_T(j):
                pe.wait_ge(s_x1, j + 1)
                if j >= 2:
                    pe.wait_ge(s_x1T, j - 1)
                for i in range(4):
                    t = pe.transpose(p_t[:, j % 2, 128 * i:128 * i + 128], x1tok[:, 4 * j + i, :], ident)
                t.then_inc(s_t, 1)

            def logits(j):
                pe.wait_ge(s_x1T, j + 1)
                for i in range(4):
                    to = p_l[:, 4 * j + i, :] if j > 0 else p_s[:, E * i:E * i + E]
                    m = pe.matmul(to, x1T[:, 4 * j + i, :], wgT[:, :], start=True, stop=True)
                m.then_inc(s_l, 1)

            for j in range(5):
                gates(j)
            tokens_T(0)
            gates(5)
            tokens_T(1)
            logits(0)
            gates(6)
            gates(7)
            for j in range(2, J):
                tokens_T(j)
                logits(j - 1)
            logits(J - 1)
            pe.wait_ge(s_sw, 48)
            for g in range(NG):
                pe.wait_ge(s_M, g + 1)
                if g >= 1:
                    pe.wait_ge(s_cr, g)
                m = maskM[:, :, :].rearrange("p e b -> p (e b)")
                pe.matmul(p_c[:, 0, :, :].rearrange("p e b -> p (e b)"), ones_h[:, :], m, start=True, stop=True)
                pe.matmul(p_c[:, 1, :, :].rearrange("p e b -> p (e b)"), negtri_h[:, :], m,
                          start=True, stop=True).then_inc(s_c, 1)
                tokens = x1T[:, 4 * g:4 * g + 4, :].rearrange("p b n -> p (b n)")
                if g >= 1:
                    pe.wait_ge(s_zm, g)
                pe.matmul(p_b[:, 0, :], sw[:, 0, :], tokens, start=True, stop=True)
                pe.matmul(p_b[:, 1, :], sw[:, 1, :], tokens, start=True, stop=True).then_inc(s_zh, 1)
                pe.wait_ge(s_zm, g + 1)
                if g >= 1:
                    pe.wait_ge(s_zc, g)
                pe.matmul(p_t[:, 0, :], sw[:, 2, :], zh[:, :], start=True, stop=True).then_inc(s_zo, 1)

        @block.vector
        def _(dve):
            v = Chain(dve, s_v)
            dve.memset(warm[:, 0:1], 0.0).then_inc(s_warm, 1)
            dve.wait_ge(s_cst, 16)
            dve.tensor_copy(ones_h[:, :], ones)
            dve.tensor_copy(negtri_h[:, :], cst[:, 256:384])
            dve.memset(carry[:, :], 0.0)
            v.link(dve.memset(keep_run[:, :, :], 1.0))
            dve.memset(keep_run[:, :, 0:1], 0.0)
            dve.wait_ge(s_smallT, 1)
            dve.tensor_copy(condT[:, :], p_s[:, 128:160]).then_inc(s_smallc, 1)
            dve.tensor_copy(wgT[:, :], p_s[:, 160:192]).then_inc(s_smallc, 1)
            dve.tensor_copy(W1T[:, :], p_s[:, 192:320]).then_inc(s_smallc, 1)
            dve.tensor_copy(W2T[:, :], p_s[:, 320:448]).then_inc(s_smallc, 1)
            dve.wait_ge(s_small, 96)
            dve.wait_ge(s_sig, 1)
            dve.scalar_tensor_tensor(out=hT[:, :], in0=p_s[:, 0:32], scalar=b1[:, 0:1], in1=sig[:, :],
                                     op0=ALU.add, op1=ALU.mult).then_inc(s_hs, 1)
            dve.wait_ge(s_gs, 1)
            v.link(dve.tensor_scalar(g1T[:, :], gateT[:, :], 1.0, None, ALU.add))
            def spread(j):
                bs = slice(4 * j, 4 * j + 4)
                dve.tensor_tensor(diag[:, bs, :], ident[:, None, :].to_broadcast([128, 4, 128]),
                                  g1T[:, bs][:, :, None].to_broadcast([128, 4, 128]), ALU.mult).then_inc(s_diag, 1)

            spread(0)
            spread(1)
            for j in range(J):
                if j + 2 < J:
                    spread(j + 2)
                bs = slice(4 * j, 4 * j + 4)
                dve.wait_ge(s_b, j + 1)
                dve.wait_ge(s_x[j // 2], 16)
                dve.tensor_tensor(x1tok[:, bs, :], xtok[:, bs, :],
                                  p_b[:, j % 2, :].rearrange("p (b d) -> p b d", b=4), ALU.mult).then_inc(s_x1, 1)

            def wide(col, n):
                return col[:, :, None].to_broadcast([N, GB, n])

            def shared_expert(j):
                dve.wait_ge(s_zs, j + 1)
                if j >= 1:
                    dve.wait_ge(s_zo, j)
                dve.tensor_tensor(zh[:, :], zs[:, :], p_b[:, 1, :], ALU.mult).then_inc(s_zm, 1)

            for g in range(NG):
                bs = slice(g * GB, (g + 1) * GB)
                dve.wait_ge(s_l, 1 if g == 0 else 4 * (g // 4 + 1))
                logits = p_l[:, bs, :] if g > 0 else p_s[:, 0:GB * E].rearrange("p (b e) -> p b e", b=GB)
                v.link(dve.tensor_reduce(r1[:, :, 0], logits, X, ALU.max))
                dve.tensor_tensor(sc[:, :, :], logits, wide(r1[:, :, 0], E), ALU.subtract).then_inc(s_sub, 1)
                dve.wait_ge(s_exp, g + 1)
                v.link(dve.tensor_reduce(r1[:, :, 1], sc[:, :, :], X, ALU.add))
                v.link(dve.reciprocal(r1[:, :, 2], r1[:, :, 1]))
                v.link(dve.tensor_tensor(sc[:, :, :], sc[:, :, :], wide(r1[:, :, 2], E), ALU.mult))
                v.link(dve.tensor_reduce(gmax[:, :, :], sc[:, :, :].rearrange("p b (g i) -> p b g i", g=GROUPS),
                                         X, ALU.max))
                other = gmax[:, :, None, :].to_broadcast([N, GB, GROUPS, GROUPS])
                own = gmax[:, :, :, None].to_broadcast([N, GB, GROUPS, GROUPS])
                dve.tensor_tensor(cmp2[:, :, :, :], other, own, ALU.is_gt)
                v.link(dve.tensor_tensor(cmp1[:, :, :, :], other, own, ALU.is_equal))
                v.link(dve.tensor_tensor(cmp1[:, :, :, :], cmp1[:, :, :, :],
                                         before_g[:, None, :, :].to_broadcast([N, GB, GROUPS, GROUPS]), ALU.mult))
                v.link(dve.tensor_tensor(cmp1[:, :, :, :], cmp1[:, :, :, :], cmp2[:, :, :, :], ALU.add))
                v.link(dve.tensor_reduce(keepm[:, :, :], cmp1[:, :, :, :], X, ALU.add))
                v.link(dve.tensor_scalar(keepg[:, :, :], keepm[:, :, :], float(KEPT_GROUPS), None, ALU.is_lt))
                v.link(dve.tensor_scalar(keepm[:, :, :], keepg[:, :, :], -1.0, None, ALU.add))
                msv = ms[:, :, :].rearrange("p b (g i) -> p b g i", g=GROUPS)
                v.link(dve.tensor_tensor(msv, sc[:, :, :].rearrange("p b (g i) -> p b g i", g=GROUPS),
                                         keepg[:, :, :, None].to_broadcast([N, GB, GROUPS, PER_GROUP]), ALU.mult))
                v.link(dve.tensor_tensor(msv, msv,
                                         keepm[:, :, :, None].to_broadcast([N, GB, GROUPS, PER_GROUP]), ALU.add))
                for b in range(GB):
                    n = v.add(dve.max(v8[:, b, :], ms[:, b, :]))
                v.wait(n)
                for b in range(GB):
                    n = v.add(dve.max_index(i8[:, b, :], v8[:, b, :], ms[:, b, :]))
                v.wait(n)
                v.link(dve.tensor_copy(idxf[:, :, :], i8[:, :, 0:K]))
                if g >= 1:
                    dve.wait_ge(s_c, g)
                v.link(dve.tensor_tensor(onehot[:, :, :, :], idxf[:, :, :, None].to_broadcast([N, GB, K, E]),
                                         iota[:, None, None, :].to_broadcast([N, GB, K, E]), ALU.is_equal))
                with nc.allow_low_precision(reason="zeros and ones"):
                    dve.tensor_reduce(maskM[:, :, :].rearrange("p e b -> p b e"),
                                      onehot[:, :, :, :].rearrange("p b k e -> p b e k"), X, ALU.add).then_inc(s_M, 1)
                v.link(dve.tensor_reduce(r1[:, :, 0], v8[:, :, 0:K], X, ALU.add))
                v.link(dve.tensor_scalar(r1[:, :, 1], r1[:, :, 0], 1e-9, None, ALU.add))
                v.link(dve.reciprocal(r1[:, :, 2], r1[:, :, 1]))
                v.link(dve.tensor_tensor(wk[:, bs, :], v8[:, :, 0:K], wide(r1[:, :, 2], K), ALU.mult))
                dve.wait_ge(s_c, g + 1)
                v.link(dve.tensor_copy(tot[:, :, :], p_c[:, 0, :, :]))
                v.link(dve.tensor_tensor(tot[:, :, 0], tot[:, :, 0], carry[:, :], ALU.add))
                flat = "p e b -> p (e b)"
                v.link(dve.tensor_tensor_scan(run[:, :, :].rearrange(flat), keep_run[:, :, :].rearrange(flat),
                                              tot[:, :, :].rearrange(flat), 0.0, ALU.mult, ALU.add))
                dve.tensor_copy(carry[:, :], run[:, :, GB - 1])
                v.link(dve.tensor_tensor(pos[:, :, :], p_c[:, 1, :, :], run[:, :, :], ALU.add))
                dve.engine_nop().then_inc(s_cr, 1)
                v.link(dve.tensor_tensor(ohpos[:, :, :, :], onehot[:, :, :, :],
                                         pos[:, :, :].rearrange("p e b -> p b e")[:, :, None, :]
                                         .to_broadcast([N, GB, K, E]), ALU.mult))
                v.link(dve.tensor_reduce(posk[:, :, :], ohpos[:, :, :, :], X, ALU.add))
                v.link(dve.tensor_scalar(keepk[:, :, :], posk[:, :, :], float(CAP), None, ALU.is_lt))
                v.link(dve.scalar_tensor_tensor(destf[:, :, :], idxf[:, :, :], float(CAP), posk[:, :, :],
                                                ALU.mult, ALU.add))
                v.link(dve.tensor_tensor(wk[:, bs, :], wk[:, bs, :], keepk[:, :, :], ALU.mult))
                v.link(dve.scalar_tensor_tensor(destf[:, :, :], destf[:, :, :], dump, keepk[:, :, :],
                                                ALU.subtract, ALU.mult))
                dve.tensor_scalar(dest[:, bs, :], destf[:, :, :], dump, None, ALU.add).then_inc(s_dest, 1)
                shared_expert(g)


def turns(eng, count, body, last=1):
    body(0)
    with eng.Fori(1, count - last, 1) as i:
        body(i)
    for i in range(count - last, count):
        body(i)


def is_last(i, count):
    return isinstance(i, int) and i == count - 1


def wait(eng, sem, value):
    if not isinstance(value, int) or value > 0:
        eng.wait_ge(sem, value)


PARTS = CAP // 128
PA = 3
EU = 4


def expert_phase(nc, a, r, xbuf, obuf, idx_tm, w_tm):
    with ExitStack() as ctx:
        kit = Kit(nc, ctx, "ex")
        ident = r.ident
        zero = kit.sb("zero", [128, 128])
        xe = kit.sb("xe", [128, EU, PARTS, D])
        we = kit.sb("we", [128, EU, 3, 128])
        w_high, w_low = (kit.sb(n, [128, EU, 2, 128], F32R) for n in ("w_high", "w_low"))
        xeT_high, xeT_low = (kit.sb(n, [D, 2, CAP], F32R) for n in ("xeT_high", "xeT_low"))
        sa, hh = kit.sb("sa", [128, CAP]), kit.sb("hh", [128, CAP])
        oe = kit.sb("oe", [128, EU, PARTS, D])
        na = PA * 128
        shares = [(0, slice(0, na), range(0, PA)), (1, slice(na, CAP), range(PA, PARTS))]
        p_t = [kit.ps(f"p_t{h}", [128, 512]) for h in range(2)]
        p_1 = [kit.ps(f"p_1{h}", [128, 512]) for h in range(2)]
        p_3 = [kit.ps(f"p_3{h}", [128, 512]) for h in range(2)]
        p_o = [kit.ps(f"p_o{h}", [128, 512]) for h in range(2)]

        s_zero, s_zst = kit.sem("zero"), kit.sem("zst")
        s_ix, s_offset, s_bias, s_high = kit.sem("ix"), kit.sem("offset"), kit.sem("bias"), kit.sem("high")
        s_x = [kit.sem(f"x{u}") for u in range(EU)]
        s_w = [kit.sem(f"w{u}") for u in range(EU)]
        s_st = [kit.sem(f"st{u}") for u in range(EU)]
        s_t, s_xT, s_xl, s_1, s_3, s_silu, s_hh, s_o, s_oe = (
            kit.sem(n) for n in ("t", "xT", "xl", "h1", "h3", "silu", "hh", "o", "oe"))
        s_wh, s_wl = kit.sem("wh"), kit.sem("wl")
        T = E // EU
        xv = xbuf.rearrange("(e p j) d -> e p j d", p=128, j=PARTS)
        ov = obuf[0:SLOTS, :].rearrange("(e p j) d -> e p j d", p=128, j=PARTS)
        block = ctx.enter_context(nc.Block())

        @block.sync
        def _(sp):
            def load(e, u):
                sp.dma_start(xe[:, u, :, :], xv[bass.ds(e, 1)].rearrange("o p j d -> p (o j) d")).then_inc(s_x[u], 16)
                for i, name in enumerate(("L0_ffn_w1", "L0_ffn_w3", "L0_ffn_w2")):
                    sp.dma_start(we[:, u, i, :], a[name][bass.ds(e, 1)].rearrange("o p n -> p (o n)")).then_inc(s_w[u], 16)

            for u in range(EU):
                load(u, u)
            sp.wait_ge(s_zero, 1)
            sp.dma_start(obuf[SLOTS:SLOTS + 128, :], zero[:, :]).then_inc(s_zst, 16)
            for t in range(CT):
                for to, src in ((r.ix, idx_tm), (r.wc, w_tm)):
                    sp.dma_start(to[B * t:B * t + B, :, :],
                                 src.rearrange("(c t) b k -> t b c k", t=CT)[t]).then_inc(s_ix, 16)

            def turn(i):
                for u in range(EU):
                    e = i * EU + u
                    wait(sp, s_oe, (e + 1) * 2)
                    sp.dma_start(ov[bass.ds(e, 1)].rearrange("o p j d -> p (o j) d"), oe[:, u, :, :]).then_inc(s_st[u], 16)
                    if not is_last(i, T):
                        load(e + EU, u)

            turns(sp, T, turn)
            for u in range(EU):
                sp.wait_ge(s_st[u], 16 * T)
            sp.wait_ge(s_zst, 16)
            sp.wait_ge(s_ix, 32 * CT)

        @block.gpsimd
        def _(pool):
            def cut_weights(e, u, i):
                wait(pool, s_w[u], 48 * (i + 1))
                wait(pool, s_3, 2 * (e - EU) + 2)
                pool.tensor_tensor(w_high[:, u, :, :], we[:, u, 0:2, :], zero[:, None, :].to_broadcast([128, 2, 128]),
                                   ALU.add).then_inc(s_wh, 1)
                wait(pool, s_wh, e + 1)
                pool.tensor_tensor(w_low[:, u, :, :], we[:, u, 0:2, :], w_high[:, u, :, :], ALU.subtract).then_inc(s_wl, 1)

            def turn(i):
                for u in range(EU):
                    cut_weights(i * EU + u, u, i)

            pool.memset(zero[:, :], 0.0).then_inc(s_zero, 1)
            pool.wait_ge(s_zero, 1)
            for u in range(EU):
                cut_weights(u, u, 0)
            with pool.Fori(1, T, 1) as i:
                turn(i)

        @block.tensor
        def _(pe):
            def transposes(e, u, i):
                wait(pe, s_x[u], 16 * (i + 1))
                for h, _, tiles in shares:
                    wait(pe, s_xl, 2 * e - 1 + h)
                    for j in tiles:
                        t = pe.transpose(p_t[h][:, 128 * (j - tiles[0]):128 * (j - tiles[0]) + 128],
                                         xe[:, u, j, :], ident[:, :])
                    t.then_inc(s_t, 1)

            def turn(i):
                for u in range(EU):
                    e = i * EU + u
                    wait(pe, s_wl, e + 1)
                    for h, cols, tiles in shares:
                        def products(out, w):
                            pe.matmul(out, w_high[:, u, w, :], xeT_high[:, u % 2, cols], start=True, stop=False)
                            pe.matmul(out, w_low[:, u, w, :], xeT_high[:, u % 2, cols], start=False, stop=False)
                            wait(pe, s_xl, 2 * e + 1 + h)
                            return pe.matmul(out, w_high[:, u, w, :], xeT_low[:, u % 2, cols], start=False, stop=True)

                        n = len(tiles) * 128
                        wait(pe, s_xT, 2 * e + 1 + h)
                        wait(pe, s_silu, 2 * e - 1 + h)
                        products(p_1[h][:, 0:n], 0).then_inc(s_1, 1)
                        wait(pe, s_hh, 2 * e - 1 + h)
                        products(p_3[h][:, 0:n], 1).then_inc(s_3, 1)
                    if not (is_last(i, T) and u == EU - 1):
                        transposes(e + 1, (u + 1) % EU, i + (u + 1) // EU)
                    wait(pe, s_w[u], 48 * (i + 1))
                    for h, cols, tiles in shares:
                        wait(pe, s_hh, 2 * e + 1 + h)
                        wait(pe, s_oe, 2 * e - 1 + h)
                        for j in tiles:
                            q = 128 * (j - tiles[0])
                            m = pe.matmul(p_o[h][:, q:q + 128], hh[:, 128 * j:128 * j + 128], we[:, u, 2, :],
                                          start=True, stop=True)
                        m.then_inc(s_o, 1)

            for layer in range(DEPTH):
                for c, (lo, hi) in enumerate(FCHUNKS):
                    for part in range(2):
                        o, q = part * HID, 6 * layer + 3 * part + c
                        m = pe.matmul(p_o[0][0:hi - lo, q:q + 1], r.w1[:, layer, o + lo:o + hi], r.lb[:, layer:layer + 1],
                                      start=True, stop=True)
            m.then_inc(s_offset, 1)
            transposes(0, 0, 0)
            pe.wait_ge(s_bias, 1)
            turns(pe, T, turn)

        @block.scalar
        def _(act):
            def copy_xT(e, u):
                for h, cols, tiles in shares:
                    wait(act, s_t, 2 * e + 1 + h)
                    wait(act, s_3, 2 * e - 3 + h)
                    act.activation(xeT_high[:, u % 2, cols], p_t[h][:, 0:len(tiles) * 128], ACT.Copy).then_inc(s_xT, 1)

            def turn(i):
                for u in range(EU):
                    e = i * EU + u
                    for h, cols, tiles in shares:
                        wait(act, s_1, 2 * e + 1 + h)
                        wait(act, s_hh, 2 * e - 1 + h)
                        act.activation(sa[:, cols], p_1[h][:, 0:len(tiles) * 128], ACT.Silu).then_inc(s_silu, 1)
                    if not (is_last(i, T) and u == EU - 1):
                        copy_xT(e + 1, u + 1)

            copy_xT(0, 0)
            turns(act, T, turn)

        @block.vector
        def _(dve):
            def low_xT(e, u):
                for h, cols, tiles in shares:
                    wait(dve, s_xT, 2 * e + 1 + h)
                    wait(dve, s_3, 2 * e - 3 + h)
                    dve.tensor_tensor(xeT_low[:, u % 2, cols], p_t[h][:, 0:len(tiles) * 128], xeT_high[:, u % 2, cols],
                                      ALU.subtract).then_inc(s_xl, 1)

            def turn(i):
                for u in range(EU):
                    e = i * EU + u
                    for h, cols, tiles in shares:
                        wait(dve, s_silu, 2 * e + 1 + h)
                        wait(dve, s_3, 2 * e + 1 + h)
                        wait(dve, s_o, 2 * e - 1 + h)
                        dve.tensor_tensor(hh[:, cols], sa[:, cols], p_3[h][:, 0:len(tiles) * 128],
                                          ALU.mult).then_inc(s_hh, 1)
                    if not (is_last(i, T) and u == EU - 1):
                        low_xT(e + 1, u + 1)
                    for h, cols, tiles in shares:
                        wait(dve, s_o, 2 * e + 1 + h)
                        if h == 0:
                            wait(dve, s_st[u], 16 * i)
                        dve.tensor_copy(oe[:, u, tiles[0]:tiles[-1] + 1, :],
                                        p_o[h][:, 0:len(tiles) * 128].rearrange("p (j d) -> p j d", d=D)
                                        ).then_inc(s_oe, 1)

            dve.tensor_copy(r.wqkv_high[:, :, :], r.wqkv[:, :, :]).then_inc(s_high, 1)
            dve.wait_ge(s_high, 1)
            dve.tensor_tensor(r.wqkv_low[:, :, :], r.wqkv[:, :, :], r.wqkv_high[:, :, :], ALU.subtract)
            dve.wait_ge(s_offset, 1)
            for layer in range(DEPTH):
                for c, (lo, hi) in enumerate(FCHUNKS):
                    for q in (c, 3 + c):
                        b = dve.tensor_tensor(r.b1l[0:hi - lo, layer, q:q + 1], p_o[0][0:hi - lo, 6 * layer + q:6 * layer + q + 1],
                                              r.b1[0:hi - lo, layer, q:q + 1], ALU.add)
            b.then_inc(s_bias, 1)
            low_xT(0, 0)
            turns(dve, T, turn)


CU = 4


def recurrence_phase(nc, r, obuf, zT, xl):
    with ExitStack() as ctx:
        kit = Kit(nc, ctx, "rc")
        ident, cond, Wx, Wh, bias = r.ident, r.cond, r.Wx, r.Wh, r.bias
        h0T = kit.sb("h0T", [D, B])
        rows = kit.sb("rows", [128, CU, K, D])
        acc = kit.sb("acc", [128, 2, D])
        hr = kit.sb("hr", [D, CU, CT, B])
        p_0 = kit.ps("p_0", [128, 512])
        p_t = [kit.ps(f"p_t{i}", [128, 512]) for i in range(2)]
        p_w = [kit.ps(f"p_w{i}", [128, 512]) for i in range(2)]
        s_h0, s_h0c, s_w1g = kit.sem("h0"), kit.sem("h0c"), kit.sem("w1g")
        s_g = [kit.sem(f"g{u}") for u in range(CU)]
        s_acc, s_t, s_x2, s_mm, s_h, s_hc, s_v = (kit.sem(n) for n in ("acc", "t", "x2", "mm", "h", "hc", "v"))
        T = CHUNKS // CU
        block = ctx.enter_context(nc.Block())

        @block.gpsimd
        def _(pool):
            for c in range(CHUNKS):
                i, u = divmod(c, CU)
                wait(pool, s_acc, c - CU + 1)
                for k in range(K):
                    pool.indirect_dma_start(
                        rows[:, u, k, :], None, obuf,
                        bass.IndirectOffsetOnAxis(ap=r.ix[:, c, k:k + 1], axis=0)).then_inc(s_g[u], 16)

        @block.vector
        def _(dve):
            for layer in range(DEPTH):
                dve.tensor_tensor(r.tcos[:, layer, :, :], r.rot[:, 0, :, :], r.scales[:, layer, :, :], ALU.mult)
                for lo, hi in ((0, DH // 2), (DH // 2, 0)):
                    dve.tensor_tensor(r.tsin[:, layer, :, lo:lo + DH // 2], r.rot[:, 1, :, lo:lo + DH // 2],
                                      r.scales[:, layer, :, hi:hi + DH // 2], ALU.mult)
            w = Chain(dve, s_w1g)
            w.link(dve.tensor_tensor(r.w1g[:, :, :], r.w1[:, :, :],
                                     r.lg[:, :, None].to_broadcast([D, DEPTH, 2 * HID]), ALU.mult))
            w.link(dve.tensor_copy(r.w1g_high[:, :, :], r.w1g[:, :, :]))
            dve.tensor_tensor(r.w1g_low[:, :, :], r.w1g[:, :, :], r.w1g_high[:, :, :], ALU.subtract)
            dve.memset(xl[D // 2:D, :, 0:1], 0.0)
            dve.wait_ge(s_h0, 1)
            dve.tensor_copy(h0T[:, :], p_0[:, 0:B]).then_inc(s_h0c, 1)

            def keep_h(c, u):
                dve.wait_ge(s_h, (c + 1) * CT)
                for half, o in HALVES:
                    ins = dve.tensor_copy(xl[half, :, bass.ds(c * CT + o, CT)], hr[half, u, :, :].rearrange("p t b -> p b t"))
                ins.then_inc(s_hc, 1)

            def turn(i):
                v = Chain(dve, s_v, i * CU * (K - 1))
                for u in range(CU):
                    c = i * CU + u
                    dve.wait_ge(s_g[u], (i + 1) * 16 * K)
                    wait(dve, s_t, c - 1)
                    for k in range(K):
                        add_to = r.xc[:, bass.ds(c, 1), :].rearrange("p o d -> p (o d)") if k == 0 else acc[:, u % 2, :]
                        ins = dve.scalar_tensor_tensor(out=acc[:, u % 2, :], in0=rows[:, u, k, :],
                                                       scalar=r.wc[:, bass.ds(c, 1), k:k + 1], in1=add_to,
                                                       op0=ALU.mult, op1=ALU.add)
                        if k < K - 1:
                            v.link(ins)
                    ins.then_inc(s_acc, 1)
                    dve.wait_ge(s_t, c + 1)
                    zc = zT[:, bass.ds(c * CT, CT), :]
                    dve.tensor_tensor(zc, p_t[u % 2][:, 0:128].rearrange("p (t b) -> p t b", t=CT), zc,
                                      ALU.add).then_inc(s_x2, 1)
                    if u > 0:
                        keep_h(c - 1, u - 1)
                    elif not (isinstance(i, int) and i == 0):
                        keep_h(c - 1, CU - 1)

            turns(dve, T, turn)
            keep_h(CHUNKS - 1, CU - 1)

        @block.tensor
        def _(pe):
            pe.transpose(p_0[:, 0:B], cond[:, :], ident[0:B, 0:B]).then_inc(s_h0, 1)
            pe.wait_ge(s_h0c, 1)

            def chunk_T(c, u):
                pe.wait_ge(s_acc, c + 1)
                wait(pe, s_x2, c - 1)
                pe.transpose(p_t[u % 2][:, 0:128], acc[:, u % 2, :], ident[:, :]).then_inc(s_t, 1)

            def input_part(c, u):
                pe.wait_ge(s_x2, c + 1)
                wait(pe, s_h, (c - 1) * CT)
                pe.matmul(p_w[u % 2][:, 0:128], Wx[:, :], zT[:, bass.ds(c * CT, CT), :].rearrange("p t b -> p (t b)"),
                          start=True, stop=True, skip_group_check=True)

            chunk_T(0, 0)
            input_part(0, 0)

            def turn(i):
                for u in range(CU):
                    c = i * CU + u
                    last = isinstance(c, int) and c == CHUNKS - 1
                    for t in range(CT):
                        if t > 0:
                            prev = hr[:, u, t - 1, :]
                        elif u > 0 or not (isinstance(i, int) and i == 0):
                            prev = hr[:, (u - 1) % CU, CT - 1, :]
                        else:
                            prev = h0T[:, :]
                        wait(pe, s_h, c * CT + t)
                        pe.matmul(p_w[u % 2][:, B * t:B * t + B], Wh[:, :], prev, start=False, stop=True,
                                  skip_group_check=True).then_inc(s_mm, 1)
                        if t == CT - 2 and not last:
                            chunk_T(c + 1, (u + 1) % CU)
                    if not last:
                        input_part(c + 1, (u + 1) % CU)

            turns(pe, T, turn)

        @block.scalar
        def _(act):
            def turn(i):
                for u in range(CU):
                    c = i * CU + u
                    wait(act, s_hc, c - CU + 1)
                    for t in range(CT):
                        act.wait_ge(s_mm, c * CT + t + 1)
                        act.activation(hr[:, u, t, :], p_w[u % 2][:, B * t:B * t + B], ACT.Tanh,
                                       bias=bias[:, 0:1]).then_inc(s_h, 1)

            turns(act, T, turn)


def exists(b):
    return not isinstance(b, int) or 0 <= b < B


AU = 4
LO, HI = 0, 1


def after_group(i, u):
    return u == 1 and not (isinstance(i, int) and i == 0)


def attention_phase(nc, r, layer, xl):
    with ExitStack() as ctx:
        kit = Kit(nc, ctx, f"at{layer}")
        ident, mask, wo = r.ident, r.mask, r.wo[:, layer, :, :]
        w_high, w_low = r.wqkv_high[:, layer, :], r.wqkv_low[:, layer, :]
        tcos, tsin = r.tcos[:, layer, :, :], r.tsin[:, layer, :, :]
        minus_half = kit.sb("minus_half", [N, 16])
        h_high, h_low = kit.sb("h_high", [D, 2, N], F32R), kit.sb("h_low", [D, 2, N], F32R)
        raw = kit.sb("raw", [N, 2, 2 * INNER])
        sq = kit.sb("sq", [N, 2 * INNER])
        ss, rn = kit.sb("ss", [N, 2, 16]), kit.sb("rn", [N, 2, 16])
        t1, t2 = kit.sb("t1", [N, 2, 2 * INNER]), kit.sb("t2", [N, 2, 2 * INNER])
        qn = kit.sb("qn", [N, 2, 2 * INNER])
        vaug = kit.sb("vaug", [N, AU, HEADS, DH + 1])
        qT = kit.sb("qT", [128, 4, N])
        kT = kit.sb("kT", [128, 4, 2, N])
        mx, gate = kit.sb("mx", [N, 2, 4]), kit.sb("gate", [N, 2])
        sm, pr, prT = ([kit.sb(f"{n}{r}", [N, 4, N]) for r in range(2)] for n in ("sm", "pr", "prT"))
        rinv = kit.sb("rinv", [N, 2, 4])
        on = kit.sb("on", [N, HEADS, DH])
        oT = kit.sb("oT", [128, 4, AU, N])
        p_qk = kit.ps("p_qk", [N, 2 * INNER])
        p_v = kit.ps("p_v", [128, 512])
        p_t = [kit.ps(f"p_t{r}", [128, 512]) for r in range(2)]
        p_s = [kit.ps(f"p_s{r}", [128, 512]) for r in range(2)]
        p_o = kit.ps("p_o", [128, 512])

        s_zero, s_one = kit.sem("zero"), kit.sem("one")
        (s_hh, s_h, s_qk, s_v, s_raw, s_vc, s_sq, s_sum, s_ss, s_t1, s_t2, s_rn, s_add, s_qn, s_Tq, s_Tk, s_Tqc, s_Tkc, s_oT,
         s_oTc, s_wo, s_xl) = (kit.sem(n) for n in (
             "hh", "h", "qk", "v", "raw", "vc", "sq", "sum", "ss", "t1", "t2", "rn", "add", "qn", "Tq", "Tk", "Tqc", "Tkc", "oT",
             "oTc", "wo", "xl"))
        s_S, s_mx, s_sub, s_P, s_PT, s_PTc, s_O, s_rinv, s_on = (
            [kit.sem(f"{n}{r}") for r in range(2)] for n in ("S", "mx", "sub", "P", "PT", "PTc", "O", "rinv", "on"))
        TURNS = B // AU
        block = ctx.enter_context(nc.Block())

        @block.gpsimd
        def _(pool):
            def low_part(b, u):
                wait(pool, s_v, b - 1)
                wait(pool, s_hh, b + 1)
                pool.tensor_tensor(h_low[:, u % 2, :], xl[:, bass.ds(b, 1), 0:N].rearrange("p o n -> p (o n)"),
                                   h_high[:, u % 2, :], ALU.subtract).then_inc(s_h, 1)

            def normal(b, u):
                u = u % 2
                wait(pool, s_ss, b + 1)
                wait(pool, s_qn, b - 1)
                pool.tensor_tensor(rn[:, u, :], ss[:, u, :], minus_half[:, :], ALU.pow).then_inc(s_rn, 1)
                if isinstance(b, int) and b == 0:
                    low_part(b + 2, u)
                    return
                if exists(b + 2):
                    low_part(b + 2, u)
                wait(pool, s_t1, b + 1)
                wait(pool, s_t2, b + 1)
                wait(pool, s_Tk, b - 1)
                pool.tensor_tensor(qn[:, u, :], t1[:, u, :], t2[:, u, :], ALU.add).then_inc(s_add, 1)
                wait(pool, s_rn, b + 1)
                wait(pool, s_add, b + 1)
                qv = qn[:, u, :].rearrange("p (g d) -> p g d", g=16)
                pool.tensor_tensor(qv, qv, rn[:, u, :, None].to_broadcast([N, 16, DH]), ALU.mult).then_inc(s_qn, 1)

            low_part(0, 0)
            low_part(1, 1)
            pool.memset(minus_half[:, :], -0.5).then_inc(s_one, 1)
            pool.memset(vaug[:, :, :, DH:DH + 1], 1.0).then_inc(s_one, 1)
            pool.memset(kT[:, :, :, :], 0.0).then_inc(s_zero, 1)
            pool.wait_ge(s_one, 1)
            normal(0, 0)
            normal(1, 1)

            def turn(i):
                for u in range(AU):
                    b = i * AU + u
                    if exists(b + 2):
                        normal(b + 2, u)

            turns(pool, TURNS, turn)

        @block.tensor
        def _(pe):
            def products(out, u, w):
                cols = slice(w * INNER, (w + 1) * INNER)
                high, low = h_high[:, u % 2, :], h_low[:, u % 2, :]
                pe.matmul(out, high, w_high[:, cols], start=True, stop=False)
                pe.matmul(out, high, w_low[:, cols], start=False, stop=False)
                return pe.matmul(out, low, w_high[:, cols], start=False, stop=True)

            def project_qk(b, u):
                wait(pe, s_h, b + 1)
                wait(pe, s_raw, b)
                products(p_qk[:, 0:INNER], u, 0)
                products(p_qk[:, INNER:2 * INNER], u, 1).then_inc(s_qk, 1)

            def project_v(b, u, group):
                wait(pe, s_vc, b)
                wait(pe, s_oTc, b - 4)
                wait(pe, s_xl, group)
                products(p_v[:, :], u, 2).then_inc(s_v, 1)

            def transpose_qk(b, u):
                wait(pe, s_qn, b + 1)
                for w, sem in ((0, s_Tq), (1, s_Tk)):
                    wait(pe, s_PTc[w], b - w)
                    for c in range(4):
                        q = w * INNER + 128 * c
                        t = pe.transpose(p_t[w][:, 128 * c:128 * c + 128], qn[:, u % 2, q:q + 128], ident[:, :])
                    t.then_inc(sem, 1)

            def scores(b, r):
                wait(pe, s_Tqc, b + 1)
                wait(pe, s_Tkc, 2 * b + 2)
                wait(pe, s_mx[r], b)
                for c in range(2):
                    m = pe.matmul(p_s[r][:, 256 * c:256 * c + 256], qT[:, 2 * r + c, :],
                                  kT[:, 2 * r + c, :, :].rearrange("p j n -> p (j n)"), start=True, stop=True)
                m.then_inc(s_S[r], 1)

            def transpose_p(b, r):
                wait(pe, s_P[r], b + 1)
                if r == HI:
                    wait(pe, s_Tkc, 2 * b + (4 if exists(b + 1) else 2))
                for j in range(4):
                    t = pe.transpose(p_t[r][:, 128 * j:128 * j + 128], pr[r][:, j, :], ident[:, :])
                t.then_inc(s_PT[r], 1)

            def output(b, u, r):
                wait(pe, s_PTc[r], b + 1)
                wait(pe, s_vc, b + 1)
                wait(pe, s_on[1 - r], b + r)
                for j in range(4):
                    m = pe.matmul(p_o[:, (DH + 1) * j:(DH + 1) * (j + 1)], prT[r][:, j, :], vaug[:, u, 4 * r + j, :],
                                  start=True, stop=True)
                m.then_inc(s_O[r], 1)

            def transpose_o(b, group):
                wait(pe, s_xl, group)
                wait(pe, s_on[HI], b + 1)
                wait(pe, s_on[LO], b + 1)
                wait(pe, s_vc, b + 5 if exists(b + 4) else B)
                if not exists(b + 4):
                    wait(pe, s_oTc, b)
                for c in range(4):
                    t = pe.transpose(p_v[:, 128 * c:128 * c + 128], on[:, 2 * c:2 * c + 2, :].rearrange("p r d -> p (r d)"),
                                     ident[:, :])
                t.then_inc(s_oT, 1)

            def out_project(g):
                wait(pe, s_oTc, AU * g + AU)
                wait(pe, s_vc, AU * g + 8 if exists(AU * g + 8) else B)
                for c in range(4):
                    m = pe.matmul(p_v[:, :], wo[:, c, :], oT[:, c, :, :].rearrange("p b n -> p (b n)"),
                                  start=(c == 0), stop=(c == 3))
                m.then_inc(s_wo, 1)

            for b in range(3):
                project_qk(b, b)
                project_v(b, b, 0)
            transpose_qk(0, 0)

            def turn(i):
                for u in range(AU):
                    b = i * AU + u
                    scores(b, LO)
                    if after_group(i, u - 1):
                        transpose_o(b - 2, i)
                    if exists(b - 1):
                        transpose_p(b - 1, HI)
                    if exists(b + 3):
                        project_qk(b + 3, u + 3)
                        if not after_group(i, u):
                            project_v(b + 3, u + 3, 0)
                    if exists(b - 1):
                        output(b - 1, (u - 1) % AU, HI)
                    transpose_p(b, LO)
                    scores(b, HI)
                    if after_group(i, u):
                        out_project(i - 1)
                    if exists(b + 1):
                        transpose_qk(b + 1, u + 1)
                    if after_group(i, u):
                        output(b, u, LO)
                        if exists(b + 3):
                            project_v(b + 3, u + 3, i)
                    elif exists(b - 1):
                        transpose_o(b - 1, 0)
                    if not after_group(i, u):
                        output(b, u, LO)

            turns(pe, TURNS, turn)
            transpose_p(B - 1, HI)
            output(B - 1, AU - 1, HI)
            transpose_o(B - 1, 0)
            out_project(TURNS - 1)

        @block.scalar
        def _(act):
            def copy_qk(b, u):
                wait(act, s_qk, b + 1)
                wait(act, s_t1, b - 1)
                wait(act, s_t2, b - 1)
                wait(act, s_sq, b - 1)
                act.activation(raw[:, u % 2, :], p_qk[:, :], ACT.Copy).then_inc(s_raw, 1)

            def copy_v(b, u):
                wait(act, s_v, b + 1)
                wait(act, s_O[HI], b - 3)
                wait(act, s_O[LO], b - 3)
                act.activation(vaug[:, u % AU, :, 0:DH], p_v[:, :].rearrange("p (h d) -> p h d", h=HEADS), ACT.Copy).then_inc(s_vc, 1)

            def square(b, u):
                wait(act, s_raw, b + 1)
                wait(act, s_sum, b)
                act.activation(sq[:, :], raw[:, u % 2, :], ACT.Square).then_inc(s_sq, 1)

            def copy_qkT(b):
                wait(act, s_Tq, b + 1)
                wait(act, s_S[HI], b)
                act.activation(qT[:, :, :].rearrange("p c n -> p (c n)"), p_t[0][:, :], ACT.Copy).then_inc(s_Tqc, 1)
                wait(act, s_Tk, b + 1)
                for j in range(2):
                    half = slice(64 * j, 64 * j + 64)
                    act.activation(kT[half, :, j, :], p_t[1][half, :].rearrange("p (c n) -> p c n", c=4),
                                   ACT.Copy).then_inc(s_Tkc, 1)

            def exp(b, r):
                wait(act, s_sub[r], b + 1)
                wait(act, s_PT[r], b)
                act.activation(pr[r][:, :, :], sm[r][:, :, :], ACT.Exp, scale=8.0).then_inc(s_P[r], 1)

            def copy_pT(b, r):
                wait(act, s_PT[r], b + 1)
                wait(act, s_O[r], b)
                act.activation(prT[r][:, :, :].rearrange("p c n -> p (c n)"), p_t[r][:, :], ACT.Copy).then_inc(s_PTc[r], 1)

            def copy_oT(b, u, group):
                wait(act, s_oT, b + 1)
                wait(act, s_wo, group)
                act.activation(oT[:, :, u, :], p_v[:, :].rearrange("p (c n) -> p c n", c=4), ACT.Copy).then_inc(s_oTc, 1)

            act.wait_ge(s_one, 2)
            act.wait_ge(s_zero, 1)
            for b in range(3):
                copy_qk(b, b)
                copy_v(b, b)
                square(b, b)
            copy_qkT(0)

            def turn(i):
                for u in range(AU):
                    b = i * AU + u
                    if after_group(i, u - 1):
                        copy_oT(b - 2, 0, i)
                    if exists(b - 1):
                        copy_pT(b - 1, HI)
                    exp(b, LO)
                    if exists(b + 3):
                        copy_qk(b + 3, u + 3)
                        if not after_group(i, u):
                            copy_v(b + 3, u + 3)
                    copy_pT(b, LO)
                    if exists(b + 3):
                        square(b + 3, u + 3)
                    if after_group(i, u):
                        exp(b, HI)
                    if exists(b + 1):
                        copy_qkT(b + 1)
                    if after_group(i, u) and exists(b + 3):
                        copy_v(b + 3, u + 3)
                    if not after_group(i, u) and exists(b - 1):
                        copy_oT(b - 1, (u - 1) % AU, 0)
                    if not after_group(i, u):
                        exp(b, HI)

            turns(act, TURNS, turn)
            copy_pT(B - 1, HI)
            copy_oT(B - 1, AU - 1, TURNS - 1)

        @block.vector
        def _(dve):
            view = "p (w h d) -> p w h d"

            def norms(b, u):
                wait(dve, s_sq, b + 1)
                wait(dve, s_rn, b - 1)
                dve.tensor_reduce(ss[:, u % 2, :], sq[:, :].rearrange("p (g d) -> p g d", g=16), X, ALU.add).then_inc(s_sum, 1)

            def floor(b, u):
                wait(dve, s_sum, b + 1)
                dve.tensor_scalar(ss[:, u % 2, :], ss[:, u % 2, :], 1e-24, None, ALU.max).then_inc(s_ss, 1)

            def rotate_cos(b, u):
                wait(dve, s_raw, b + 1)
                wait(dve, s_add, b - 1)
                dve.tensor_tensor(t1[:, u % 2, :].rearrange(view, w=2, h=HEADS), raw[:, u % 2, :].rearrange(view, w=2, h=HEADS),
                                  tcos[:, :, None, :].to_broadcast([N, 2, HEADS, DH]), ALU.mult).then_inc(s_t1, 1)

            def rotate_sin(b, u):
                src = raw[:, u % 2, :].rearrange(view, w=2, h=HEADS)
                to = t2[:, u % 2, :].rearrange(view, w=2, h=HEADS)
                for lo, hi in ((0, DH // 2), (DH // 2, 0)):
                    ins = dve.tensor_tensor(to[:, :, :, lo:lo + DH // 2], src[:, :, :, hi:hi + DH // 2],
                                            tsin[:, :, None, lo:lo + DH // 2].to_broadcast([N, 2, HEADS, DH // 2]), ALU.mult)
                ins.then_inc(s_t2, 1)

            def shifted(b, u):
                wait(dve, s_v, b - 1)
                xb = xl[:, bass.ds(b, 1), 0:N].rearrange("p o n -> p (o n)")
                dve.tensor_copy(h_high[:, u % 2, :], xb).then_inc(s_hh, 1)

            def masked(b, r):
                wait(dve, s_S[r], b + 1)
                wait(dve, s_P[r], b)
                wait(dve, s_sub[r], b)
                dve.memset(gate[:, r:r + 1], 0.0)
                for j in range(4):
                    m = dve.tensor_tensor_reduce(out=sm[r][:, j, :], in0=p_s[r][:, 128 * j:128 * j + 128], in1=mask[:, :],
                                                 scale=1.0, scalar=3 * MASKED, op0=ALU.add, op1=ALU.max,
                                                 accum_out=mx[:, r, j:j + 1])
                m.then_inc(s_mx[r], 1)

            def below_max(b, r):
                wait(dve, s_mx[r], b + 1)
                dve.tensor_tensor(sm[r][:, :, :], sm[r][:, :, :], mx[:, r, :, None].to_broadcast([N, 4, N]),
                                  ALU.subtract).then_inc(s_sub[r], 1)

            ov = p_o[:, 0:4 * (DH + 1)].rearrange("p (c d) -> p c d", c=4)

            def invert(b, r):
                wait(dve, s_O[r], b + 1)
                wait(dve, s_on[r], b)
                dve.reciprocal(rinv[:, r, :], ov[:, :, DH]).then_inc(s_rinv[r], 1)

            def divide(b, r):
                wait(dve, s_rinv[r], b + 1)
                wait(dve, s_oT, b)
                dve.tensor_tensor(on[:, 4 * r:4 * r + 4, :], ov[:, :, 0:DH], rinv[:, r, :, None].to_broadcast([N, 4, DH]),
                                  ALU.mult).then_inc(s_on[r], 1)

            def add_group(g):
                wait(dve, s_wo, g + 1)
                wait(dve, s_h, AU * g + AU)
                for half, o in HALVES:
                    xb = xl[half, bass.ds(AU * g, AU), o:o + N]
                    ins = dve.tensor_tensor(xb, p_v[half, :].rearrange("p (b n) -> p b n", b=AU), xb, ALU.add)
                ins.then_inc(s_xl, 1)

            for b in range(2):
                shifted(b, b)
            shifted(2, 0)
            norms(0, 0)
            floor(0, 0)
            rotate_cos(0, 0)
            rotate_sin(0, 0)
            dve.wait_ge(s_t1, 1)
            dve.wait_ge(s_t2, 1)
            dve.tensor_tensor(qn[:, 0, :], t1[:, 0, :], t2[:, 0, :], ALU.add).then_inc(s_add, 1)
            shifted(3, 1)
            norms(1, 1)
            floor(1, 1)
            dve.wait_ge(s_rn, 1)
            dve.wait_ge(s_add, 1)
            qv = qn[:, 0, :].rearrange("p (g d) -> p g d", g=16)
            dve.tensor_tensor(qv, qv, rn[:, 0, :, None].to_broadcast([N, 16, DH]), ALU.mult).then_inc(s_qn, 1)
            rotate_cos(1, 1)
            rotate_sin(1, 1)

            def turn(i):
                for u in range(AU):
                    b = i * AU + u
                    masked(b, LO)
                    if exists(b + 4):
                        shifted(b + 4, u)
                    below_max(b, LO)
                    if after_group(i, u - 1):
                        invert(b - 1, LO)
                        divide(b - 1, LO)
                    if exists(b + 2):
                        norms(b + 2, u)
                    if exists(b + 2):
                        floor(b + 2, u)
                        rotate_cos(b + 2, u)
                    if exists(b - 1):
                        invert(b - 1, HI)
                    if exists(b + 2):
                        rotate_sin(b + 2, u)
                    if exists(b - 1):
                        divide(b - 1, HI)
                    masked(b, HI)
                    below_max(b, HI)
                    if after_group(i, u):
                        add_group(i - 1)
                    else:
                        invert(b, LO)
                        divide(b, LO)

            turns(dve, TURNS, turn)
            invert(B - 1, HI)
            divide(B - 1, HI)
            add_group(TURNS - 1)


def ffn_phase(nc, r, layer, xl, x2T, out):
    final = layer == DEPTH - 1
    with ExitStack() as ctx:
        kit = Kit(nc, ctx, f"ff{layer}")
        ident, ones, cm = r.ident, r.ones, r.cm
        w_high, w_low = r.w1g_high[:, layer, :], r.w1g_low[:, layer, :]
        w2, b1l, b2 = r.w2[:, layer, :, :], r.b1l[:, layer, :], r.b2[:, layer:layer + 1]
        minus_half = kit.sb("minus_half", [128, 4])
        sq, rstd = kit.sb("sq", [D, 512]), kit.sb("rstd", [D, 512])
        vs, rs = kit.sb("vs", [N, 4]), kit.sb("rs", [N, 4])
        diag = kit.sb("diag", [N, 4, N])
        hn = kit.sb("hn", [D, 512])
        hn_high, hn_low = kit.sb("hn_high", [D, 2, 512], F32R), kit.sb("hn_low", [D, 2, 512], F32R)
        gg, hm = kit.sb("gg", [128, 3, 512]), kit.sb("hm", [128, 3, 512])
        res, ot = kit.sb("res", [D, 2, 512]), kit.sb("ot", [N, 2, 4, D])
        p_c, p_v = kit.ps("p_c", [128, 512]), kit.ps("p_v", [128, 512])
        p_a = [kit.ps(f"p_a{i}", [128, 512]) for i in range(2)]
        p_g = [kit.ps(f"p_g{i}", [128, 512]) for i in range(2)]
        p_d, p_r = kit.ps("p_d", [128, 512]), kit.ps("p_r", [128, 512])
        (s_mh, s_hh, s_hl, s_cen, s_sq, s_var, s_vs, s_rs, s_diag, s_bc, s_rstd, s_hn, s_w1, s_gelu, s_hm, s_d, s_x,
         s_res, s_r, s_ot) = (kit.sem(n) for n in (
             "mh", "hh", "hl", "cen", "sq", "var", "vs", "rs", "diag", "bc", "rstd", "hn", "w1", "gelu", "hm", "d", "x",
             "res", "r", "ot"))
        s_out = [kit.sem(f"out{u}") for u in range(2)]
        TURNS = J // 2
        block = ctx.enter_context(nc.Block())

        def here(j):
            return not isinstance(j, int) or j < J

        if final:
            @block.sync
            def _(sp):
                ov = out.rearrange("(j b) n d -> j n b d", b=4)

                def turn(i):
                    for u in range(2):
                        j = 2 * i + u
                        sp.wait_ge(s_ot, j + 1)
                        sp.dma_start(ov[bass.ds(j, 1)].rearrange("o n b d -> n (o b) d"), ot[:, u, :, :]).then_inc(s_out[u], 16)

                turns(sp, TURNS, turn)
                for u in range(2):
                    sp.wait_ge(s_out[u], 16 * TURNS)

        @block.gpsimd
        def _(pool):
            pool.memset(minus_half[:, :], -0.5).then_inc(s_mh, 1)
            pool.wait_ge(s_mh, 1)

            def turn(i):
                for u in range(2):
                    j = 2 * i + u
                    pool.wait_ge(s_vs, j + 1)
                    wait(pool, s_diag, j)
                    pool.tensor_tensor(rs[:, :], vs[:, :], minus_half[:, :], ALU.pow).then_inc(s_rs, 1)

            turns(pool, TURNS, turn)

        @block.tensor
        def _(pe):
            def center(j):
                wait(pe, s_hn, j)
                pe.matmul(p_c[:, :], cm[:, 0:128], xl[:, bass.ds(4 * j, 4), 0:N],
                          start=True, stop=True).then_inc(s_cen, 1)

            def variance(j):
                wait(pe, s_sq, j + 1)
                wait(pe, s_rstd, j)
                for q in range(4):
                    m = pe.matmul(p_v[:, q:q + 1], sq[:, 128 * q:128 * q + 128], cm[:, 128:129], start=True, stop=True)
                m.then_inc(s_var, 1)

            def broadcast(j):
                wait(pe, s_diag, j + 1)
                pe.matmul(p_v[:, :], ones, diag[:, :, :].rearrange("p b n -> p (b n)"), start=True, stop=True).then_inc(s_bc, 1)

            def hidden(j, u, c):
                n, s = 3 * j + c, (3 * u + c) % 2
                lo, hi = FCHUNKS[c]
                wait(pe, s_hm, n - 1)
                wait(pe, s_gelu, n - 1)
                outs = ((p_g[s][0:hi - lo, :], slice(HID + lo, HID + hi)), (p_a[s][0:hi - lo, :], slice(lo, hi)))
                for out_rows, cols in outs:
                    pe.matmul(out_rows, w_low[:, cols], hn_high[:, u, :], start=True, stop=False)
                    pe.matmul(out_rows, w_high[:, cols], hn_high[:, u, :], start=False, stop=False)
                wait(pe, s_hl, j + 1)
                for out_rows, cols in outs:
                    m = pe.matmul(out_rows, w_high[:, cols], hn_low[:, u, :], start=False, stop=True)
                m.then_inc(s_w1, 1)

            center(0)
            variance(0)
            broadcast(0)
            pe.wait_ge(s_hh, 1)
            hidden(0, 0, 0)
            center(1)

            def turn(i):
                for u in range(2):
                    j = 2 * i + u
                    hidden(j, u, 1)
                    if here(j + 1):
                        variance(j + 1)
                    hidden(j, u, 2)
                    wait(pe, s_x, j)
                    for c, (lo, hi) in enumerate(FCHUNKS):
                        wait(pe, s_hm, 3 * j + c + 1)
                        m = pe.matmul(p_d[:, :], w2[0:hi - lo, c, :], hm[0:hi - lo, c, :], start=(c == 0), stop=(c == 2))
                        if c == 0 and here(j + 1):
                            broadcast(j + 1)
                    m.then_inc(s_d, 1)
                    if here(j + 1):
                        wait(pe, s_hh, j + 2)
                        hidden(j + 1, (u + 1) % 2, 0)
                    if here(j + 2):
                        center(j + 2)
                    if final:
                        wait(pe, s_res, j + 1)
                        wait(pe, s_ot, j)
                        for b in range(4):
                            t = pe.transpose(p_r[:, 128 * b:128 * b + 128], res[:, u, 128 * b:128 * b + 128], ident)
                        t.then_inc(s_r, 1)

            turns(pe, TURNS, turn)

        @block.scalar
        def _(act):
            def squares(j):
                wait(act, s_cen, j + 1)
                wait(act, s_var, j)
                act.activation(sq[:, :], p_c[:, :], ACT.Square).then_inc(s_sq, 1)

            def copy_rstd(j):
                wait(act, s_bc, j + 1)
                wait(act, s_hn, j)
                act.activation(rstd[:, :], p_v[:, :], ACT.Copy).then_inc(s_rstd, 1)

            def gelu(j, u, c):
                n, s = 3 * j + c, (3 * u + c) % 2
                w = FCHUNKS[c][1] - FCHUNKS[c][0]
                wait(act, s_w1, n + 1)
                wait(act, s_hm, n - 2)
                act.activation(gg[0:w, c, :], p_g[s][0:w, :], ACT.Gelu, bias=b1l[0:w, 3 + c:4 + c]).then_inc(s_gelu, 1)

            squares(0)
            copy_rstd(0)
            gelu(0, 0, 0)
            squares(1)

            def turn(i):
                for u in range(2):
                    j = 2 * i + u
                    gelu(j, u, 1)
                    gelu(j, u, 2)
                    if here(j + 1):
                        copy_rstd(j + 1)
                        gelu(j + 1, (u + 1) % 2, 0)
                    if here(j + 2):
                        squares(j + 2)
                    if final:
                        wait(act, s_r, j + 1)
                        wait(act, s_out[u], 16 * i)
                        act.activation(ot[:, u, :, :].rearrange("p b d -> p (b d)"), p_r[:, :], ACT.Copy).then_inc(s_ot, 1)

            turns(act, TURNS, turn)

        @block.vector
        def _(dve):
            def deviation(j):
                wait(dve, s_var, j + 1)
                wait(dve, s_rs, j)
                dve.tensor_scalar(vs[:, :], p_v[:, 0:4], 1e-5, None, ALU.add).then_inc(s_vs, 1)

            def spread(j):
                wait(dve, s_rs, j + 1)
                wait(dve, s_bc, j)
                dve.tensor_tensor(diag[:, :, :], ident[:, None, :].to_broadcast([N, 4, N]),
                                  rs[:, :, None].to_broadcast([N, 4, N]), ALU.mult).then_inc(s_diag, 1)

            def normal(j, u):
                wait(dve, s_rstd, j + 1)
                wait(dve, s_w1, 3 * (j - 1))
                dve.tensor_tensor(hn_high[:, u, :], p_c[:, :], rstd[:, :], ALU.mult).then_inc(s_hh, 1)
                wait(dve, s_hl, j)
                dve.tensor_tensor(hn[:, :], p_c[:, :], rstd[:, :], ALU.mult).then_inc(s_hn, 1)
                wait(dve, s_hh, j + 1)
                wait(dve, s_hn, j + 1)
                dve.tensor_tensor(hn_low[:, u, :], hn[:, :], hn_high[:, u, :], ALU.subtract).then_inc(s_hl, 1)

            def gate(j, u, c):
                n, s = 3 * j + c, (3 * u + c) % 2
                w = FCHUNKS[c][1] - FCHUNKS[c][0]
                wait(dve, s_gelu, n + 1)
                wait(dve, s_d, j)
                dve.scalar_tensor_tensor(out=hm[0:w, c, :], in0=p_a[s][0:w, :], scalar=b1l[0:w, c:c + 1],
                                         in1=gg[0:w, c, :], op0=ALU.add, op1=ALU.mult).then_inc(s_hm, 1)

            deviation(0)
            spread(0)
            normal(0, 0)
            gate(0, 0, 0)

            def turn(i):
                for u in range(2):
                    j = 2 * i + u
                    if here(j + 1):
                        deviation(j + 1)
                    gate(j, u, 1)
                    if here(j + 1):
                        spread(j + 1)
                    gate(j, u, 2)
                    if here(j + 1):
                        normal(j + 1, (u + 1) % 2)
                    wait(dve, s_d, j + 1)
                    dv = p_d[:, :].rearrange("p (b n) -> p b n", b=4)
                    rv = res[:, u, :].rearrange("p (b n) -> p b n", b=4)
                    if final:
                        wait(dve, s_r, j - 1)
                    for half, o in HALVES:
                        xv = xl[half, bass.ds(4 * j, 4), o:o + N]
                        ins = dve.scalar_tensor_tensor(out=rv[half] if final else xv, in0=dv[half], scalar=b2[half, 0:1],
                                                       in1=xv, op0=ALU.add, op1=ALU.add)
                    ins.then_inc(s_x, 1)
                    if final:
                        dve.wait_ge(s_x, j + 1)
                        dve.tensor_tensor(rv, rv, x2T[:, :, bass.ds(4 * j, 4)].rearrange("p n b -> p b n"),
                                          ALU.add).then_inc(s_res, 1)
                    if here(j + 1):
                        gate(j + 1, (u + 1) % 2, 0)

            turns(dve, TURNS, turn)


def program(nc, a, out):
    xbuf = nc.dram_tensor("xbuf", (SLOTS, D), F32, kind="Internal").ap()
    obuf = nc.dram_tensor("obuf", (SLOTS + 128, D), F32, kind="Internal").ap()
    idx_tm = nc.dram_tensor("idx_tm", (N, B, K), I32, kind="Internal").ap()
    w_tm = nc.dram_tensor("w_tm", (N, B, K), F32, kind="Internal").ap()
    with ExitStack() as ctx:
        r = Resident(nc, ctx)
        x2T = ctx.enter_context(nc.sbuf_tensor("x2T", [D, N, B], F32))
        dispatch_phase(nc, a, r, xbuf, idx_tm, w_tm, x2T)
        r.parts(nc, ctx)
        expert_phase(nc, a, r, xbuf, obuf, idx_tm, w_tm)
        xl = ctx.enter_context(nc.sbuf_tensor("xl", [D, B, N + 1], F32))
        recurrence_phase(nc, r, obuf, x2T, xl)
        for layer in range(DEPTH):
            attention_phase(nc, r, layer, xl)
            ffn_phase(nc, r, layer, xl, x2T, out)


def kernel(**inputs):
    import concourse.bacc as bacc
    from concourse.bass_utils import run_bass_kernel_spmd

    nc = bacc.Bacc("TRN2", target_bir_lowering=False, num_devices=1)
    arrays = {k: np.ascontiguousarray(v) for k, v in inputs.items()}
    arrays.update(constants())
    args = {k: nc.dram_tensor(f"in_{k}", v.shape, mybir.dt.from_np(v.dtype), kind="ExternalInput").ap()
            for k, v in arrays.items()}
    out = nc.dram_tensor("out", (B, N, D), F32, kind="ExternalOutput").ap()
    program(nc, args, out)
    r = run_bass_kernel_spmd(nc, [{f"in_{k}": v for k, v in arrays.items()}], core_ids=[0])
    return r.results[0]["out"]
```
